# Optimizing a Trainium2 kernel written in Bass

```python
import numpy as np
import jax
import jax.numpy as jnp

def _softmax(x, axis=-1):
    return jax.nn.softmax(x, axis=axis)

def _gelu(x):
    return jax.nn.gelu(x, approximate=True)

def _silu(x):
    return jax.nn.silu(x)

def _sigmoid(x):
    return jax.nn.sigmoid(x)

def _layernorm(x, axis=-1, eps=1e-05):
    m = jnp.mean(x, axis=axis, keepdims=True)
    v = jnp.var(x, axis=axis, keepdims=True)
    return (x - m) / jnp.sqrt(v + eps)

def _scatter_add(tgt, idx, src, axis=0):
    return tgt.at[idx].add(src)

def _segment_sum(src, seg, n):
    return jax.ops.segment_sum(src, seg, n)
kernel_name = 'mk_gnn_resnorm_d4_gnn_r32_4b79bb'

def setup_inputs(seed: int=0):
    np.random.seed(seed)
    _w = jnp.asarray

    def _rec_inputs():
        import jax
        import jax.numpy as jnp
        _gk = jax.random.key(seed)
        x = -0.0003713 + 1 * jax.random.normal(jax.random.fold_in(_gk, 1), (50000, 256), jnp.float32)
        src = jax.random.randint(jax.random.fold_in(_gk, 2), (25000,), 0, 50000, jnp.int32)
        dst = jax.random.randint(jax.random.fold_in(_gk, 3), (25000,), 0, 50000, jnp.int32)
        _o = jnp.argsort(dst, stable=True)
        src = src[_o]
        dst = dst[_o]
        edge_weight = jax.random.uniform(jax.random.fold_in(_gk, 13), (25000,), jnp.float32, 0.0, 1)
        return (x, src, dst, edge_weight)
    x, src, dst, edge_weight = _rec_inputs()

    def _L0_gnn_setup():
        import jax, jax.numpy as jnp
        import numpy as np
        N, IN, H, C = (50000, 256, 8, 32)
        E = 25000
        key = jax.random.key(seed)
        ks = jax.random.split(key, 10)
        s = 1.0 / np.sqrt(IN)
        inp = {'x': jax.random.normal(ks[0], (N, IN), dtype=jnp.float32), 'edge_index': jax.random.randint(ks[1], (2, E), 0, N, dtype=jnp.int32), 'Wq': jax.random.uniform(ks[2], (IN, H * C), jnp.float32, -s, s), 'bq': jnp.zeros((H * C,), jnp.float32), 'Wk': jax.random.uniform(ks[3], (IN, H * C), jnp.float32, -s, s), 'bk': jnp.zeros((H * C,), jnp.float32), 'Wv': jax.random.uniform(ks[4], (IN, H * C), jnp.float32, -s, s), 'bv': jnp.zeros((H * C,), jnp.float32), 'Ws': jax.random.uniform(ks[5], (IN, H * C), jnp.float32, -s, s), 'bs': jnp.zeros((H * C,), jnp.float32)}
        return inp
    _L0_gnn_all = _L0_gnn_setup()
    _L0_gnn_in = {k: v for k, v in _L0_gnn_all.items() if k in ('Wq', 'bq', 'Wk', 'bk', 'Wv', 'bv', 'Ws', 'bs')}
    del _L0_gnn_all

    def _L1_gnn_setup():
        import jax, jax.numpy as jnp
        import numpy as np
        N_NODES = 3125
        F_DIM = 256
        NNZ = 50000

        def _prelu(x, a):
            return jnp.where(x >= 0, x, a * x)

        def _hconv(x, W, b, src, dst, n):
            xt = x @ W
            ones = jnp.ones(src.shape, xt.dtype)
            D = jax.ops.segment_sum(ones, src, num_segments=n)
            B = jax.ops.segment_sum(ones, dst, num_segments=n)
            Dinv = jnp.where(D > 0, 1.0 / D, 0.0)
            Binv = jnp.where(B > 0, 1.0 / B, 0.0)
            m = jax.ops.segment_sum(xt[src], dst, num_segments=n) * Binv[:, None]
            out = jax.ops.segment_sum(m[dst], src, num_segments=n) * Dinv[:, None]
            return out + b
        key = jax.random.key(seed)
        k0, k1, k2, k3 = jax.random.split(key, 4)
        x = jax.random.normal(k0, (N_NODES, F_DIM), dtype=jnp.float32)
        edge_index = jax.random.randint(k1, (2, NNZ), 0, N_NODES, dtype=jnp.int32)
        scale = (2.0 / F_DIM) ** 0.5
        W1 = jax.random.normal(k2, (F_DIM, F_DIM), dtype=jnp.float32) * scale
        W2 = jax.random.normal(k3, (F_DIM, F_DIM), dtype=jnp.float32) * scale
        b1 = jnp.zeros((F_DIM,), jnp.float32)
        b2 = jnp.zeros((F_DIM,), jnp.float32)
        a = jnp.full((1,), 0.25, jnp.float32)
        return {'x': x, 'edge_index': edge_index, 'W1': W1, 'b1': b1, 'W2': W2, 'b2': b2, 'a': a}
    _L1_gnn_all = _L1_gnn_setup()
    _L1_gnn_in = {k: v for k, v in _L1_gnn_all.items() if k in ('W1', 'b1', 'W2', 'b2', 'a')}
    del _L1_gnn_all

    def _L2_gnn_setup():
        import jax, jax.numpy as jnp
        import numpy as np
        N, E, IN_CH, H, C = (50000, 25000, 256, 4, 64)
        key = jax.random.key(seed)
        k1, k2, k3, k4 = jax.random.split(key, 4)
        x = jax.random.normal(k1, (N, IN_CH), dtype=jnp.float32)
        edge_index = jax.random.randint(k2, (2, E), 0, N, dtype=jnp.int64)
        W = jax.random.normal(k3, (H * C, IN_CH), dtype=jnp.float32) * 0.05
        att = jax.random.normal(k4, (H, 2 * C), dtype=jnp.float32) * 0.05
        return {'x': x, 'edge_index': edge_index, 'W': W, 'att': att}
    _L2_gnn_all = _L2_gnn_setup()
    _L2_gnn_in = {k: v for k, v in _L2_gnn_all.items() if k in ('W', 'att')}
    del _L2_gnn_all

    def _L3_gnn_setup():
        import jax, jax.numpy as jnp
        import numpy as np
        N, E, C = (50000, 25000, 256)
        EPS = 1e-05
        key = jax.random.key(seed)
        ks = jax.random.split(key, 6)
        s = 1.0 / np.sqrt(C)
        return {'x': jax.random.normal(ks[0], (N, C), jnp.float32), 'edge_weight': jax.random.uniform(ks[1], (E,), jnp.float32), 'W_rel': jax.random.normal(ks[2], (C, C), jnp.float32) * s, 'b_rel': jnp.zeros((C,), jnp.float32), 'W_root': jax.random.normal(ks[3], (C, C), jnp.float32) * s, 'gamma': jnp.ones((C,), jnp.float32), 'beta': jnp.zeros((C,), jnp.float32), 'edge_index': jax.random.randint(ks[4], (2, E), 0, N, jnp.int32), 'batch': jnp.zeros((N,), jnp.int32)}
    _L3_gnn_all = _L3_gnn_setup()
    _L3_gnn_in = {k: v for k, v in _L3_gnn_all.items() if k in ('W_rel', 'b_rel', 'W_root', 'gamma', 'beta')}
    del _L3_gnn_all
    return {'x': x, 'src': src, 'dst': dst, 'edge_weight': edge_weight, 'L0_gnn_Wq': _L0_gnn_in['Wq'], 'L0_gnn_bq': _L0_gnn_in['bq'], 'L0_gnn_Wk': _L0_gnn_in['Wk'], 'L0_gnn_bk': _L0_gnn_in['bk'], 'L0_gnn_Wv': _L0_gnn_in['Wv'], 'L0_gnn_bv': _L0_gnn_in['bv'], 'L0_gnn_Ws': _L0_gnn_in['Ws'], 'L0_gnn_bs': _L0_gnn_in['bs'], 'L1_gnn_W1': _L1_gnn_in['W1'], 'L1_gnn_b1': _L1_gnn_in['b1'], 'L1_gnn_W2': _L1_gnn_in['W2'], 'L1_gnn_b2': _L1_gnn_in['b2'], 'L1_gnn_a': _L1_gnn_in['a'], 'L2_gnn_W': _L2_gnn_in['W'], 'L2_gnn_att': _L2_gnn_in['att'], 'L3_gnn_W_rel': _L3_gnn_in['W_rel'], 'L3_gnn_b_rel': _L3_gnn_in['b_rel'], 'L3_gnn_W_root': _L3_gnn_in['W_root'], 'L3_gnn_gamma': _L3_gnn_in['gamma'], 'L3_gnn_beta': _L3_gnn_in['beta']}

def reference(x, src, dst, edge_weight, L0_gnn_Wq, L0_gnn_bq, L0_gnn_Wk, L0_gnn_bk, L0_gnn_Wv, L0_gnn_bv, L0_gnn_Ws, L0_gnn_bs, L1_gnn_W1, L1_gnn_b1, L1_gnn_W2, L1_gnn_b2, L1_gnn_a, L2_gnn_W, L2_gnn_att, L3_gnn_W_rel, L3_gnn_b_rel, L3_gnn_W_root, L3_gnn_gamma, L3_gnn_beta):
    import jax
    import jax.numpy as jnp

    def _L0_gnn_ref(x, edge_index, Wq, bq, Wk, bk, Wv, bv, Ws, bs):
        import jax, jax.numpy as jnp
        import numpy as np
        N, IN, H, C = (50000, 256, 8, 32)
        E = 25000
        n = x.shape[0]
        q = (x @ Wq + bq).reshape(n, H, C)
        k = (x @ Wk + bk).reshape(n, H, C)
        v = (x @ Wv + bv).reshape(n, H, C)
        src, dst = (edge_index[0], edge_index[1])
        alpha = jnp.einsum('ehc,ehc->eh', q[dst], k[src]) / jnp.sqrt(jnp.float32(C))
        amax = jax.ops.segment_max(alpha, dst, num_segments=n)
        ex = jnp.exp(alpha - amax[dst])
        denom = jax.ops.segment_sum(ex, dst, num_segments=n)
        attn = ex / denom[dst]
        msg = (v[src] * attn[:, :, None]).reshape(-1, H * C)
        out = jax.ops.segment_sum(msg, dst, num_segments=n)
        return out + x @ Ws + bs

    def _L1_gnn_ref(x, edge_index, W1, b1, W2, b2, a):
        import jax, jax.numpy as jnp
        import numpy as np
        N_NODES = 3125
        F_DIM = 256
        NNZ = 50000

        def _prelu(x, a):
            return jnp.where(x >= 0, x, a * x)

        def _hconv(x, W, b, src, dst, n):
            xt = x @ W
            ones = jnp.ones(src.shape, xt.dtype)
            D = jax.ops.segment_sum(ones, src, num_segments=n)
            B = jax.ops.segment_sum(ones, dst, num_segments=n)
            Dinv = jnp.where(D > 0, 1.0 / D, 0.0)
            Binv = jnp.where(B > 0, 1.0 / B, 0.0)
            m = jax.ops.segment_sum(xt[src], dst, num_segments=n) * Binv[:, None]
            out = jax.ops.segment_sum(m[dst], src, num_segments=n) * Dinv[:, None]
            return out + b
        src, dst = (edge_index[0], edge_index[1])
        n = x.shape[0]
        h = _prelu(_hconv(x, W1, b1, src, dst, n), a)
        h = _hconv(h, W2, b2, src, dst, n) + x
        return _prelu(h, a)

    def _L2_gnn_ref(x, edge_index, W, att):
        import jax, jax.numpy as jnp
        import numpy as np
        N, E, IN_CH, H, C = (50000, 25000, 256, 4, 64)
        n = x.shape[0]
        src, dst = (edge_index[0], edge_index[1])
        Wh = (x @ W.T).reshape(n, H, C)
        e_src = jnp.einsum('ehc,hc->eh', Wh[src], att[:, :C])
        e_dst = jnp.einsum('ehc,hc->eh', Wh[dst], att[:, C:])
        e = jax.nn.leaky_relu(e_src + e_dst, negative_slope=0.2)
        e_max = jax.ops.segment_max(e, dst, num_segments=n)
        e_exp = jnp.exp(e - e_max[dst])
        denom = jax.ops.segment_sum(e_exp, dst, num_segments=n)
        alpha = e_exp / (denom[dst] + 1e-16)
        agg = jax.ops.segment_sum(alpha[:, :, None] * Wh[src], dst, num_segments=n)
        return jax.nn.elu(agg.reshape(n, H * C))

    def _L3_gnn_ref(x, edge_weight, W_rel, b_rel, W_root, gamma, beta, edge_index, batch):
        import jax, jax.numpy as jnp
        import numpy as np
        N, E, C = (50000, 25000, 256)
        EPS = 1e-05
        src, dst = (edge_index[0], edge_index[1])
        msg = x[src] * edge_weight[:, None]
        agg = jax.ops.segment_sum(msg, dst, num_segments=x.shape[0])
        out = agg @ W_rel.T + b_rel + x @ W_root.T
        mean = out.mean(axis=0)
        var = out.var(axis=0)
        out = (out - mean) * jax.lax.rsqrt(var + EPS) * gamma + beta
        out = jax.nn.relu(out)
        out = jax.nn.relu(out + x)
        return out
    edge_index = jnp.stack([src, dst])
    batch0 = jnp.zeros((50000,), jnp.int32)
    x = _layernorm(x + _L0_gnn_ref(x, edge_index, L0_gnn_Wq, L0_gnn_bq, L0_gnn_Wk, L0_gnn_bk, L0_gnn_Wv, L0_gnn_bv, L0_gnn_Ws, L0_gnn_bs), axis=-1)
    x = _layernorm(x + _L1_gnn_ref(x, edge_index, L1_gnn_W1, L1_gnn_b1, L1_gnn_W2, L1_gnn_b2, L1_gnn_a), axis=-1)
    x = _layernorm(x + _L2_gnn_ref(x, edge_index, L2_gnn_W, L2_gnn_att), axis=-1)
    x = _layernorm(x + _L3_gnn_ref(x, edge_weight, L3_gnn_W_rel, L3_gnn_b_rel, L3_gnn_W_root, L3_gnn_gamma, L3_gnn_beta, edge_index, batch0), axis=-1)
    return x

_drawn_inputs = setup_inputs


def setup_inputs(seed=0):
    import zlib

    import numpy as np

    out = dict(_drawn_inputs(seed))
    spreads = {'L0_gnn_bq': (0.0, 2.0),
     'L0_gnn_bk': (0.0, 2.0),
     'L0_gnn_bv': (0.0, 0.1),
     'L0_gnn_bs': (0.0, 0.1),
     'L1_gnn_b1': (0.0, 0.1),
     'L1_gnn_b2': (0.0, 0.1),
     'L3_gnn_b_rel': (0.0, 2.0),
     'L3_gnn_gamma': (1.0, 0.2),
     'L3_gnn_beta': (0.0, 0.1)}
    factors = {'L2_gnn_att': 3.426, 'L0_gnn_Wq': 2.809}
    for name, (base, spread) in spreads.items():
        noise = np.random.default_rng([zlib.crc32(name.encode()), seed]).standard_normal(out[name].shape)
        drawn = base * np.exp(spread * noise) if base else spread * noise
        out[name] = jnp.asarray(drawn.astype(out[name].dtype))
    for name, factor in factors.items():
        out[name] = (out[name] * factor).astype(out[name].dtype)
    return out
```

```python
from contextlib import ExitStack, contextmanager

import concourse.bass as bass
from concourse import mybir

ALU = mybir.AluOpType
ACT = mybir.ActivationFunctionType
F32 = mybir.dt.float32
BF16 = mybir.dt.bfloat16
FP16 = mybir.dt.float16
I32 = mybir.dt.int32

P = 128
N = 50000
E = 25000
C = 256
H = C // P
CH = 512
TPC = CH // P
NCH = -(-E // CH)
EP = NCH * CH
NT = EP // P
KR = NT // 2
HI = -(-(N + 1) // P)
G = 6
NG = N // (P * G)
TAIL = N - NG * P * G
SKIP = float(1 << 20)
BIG = 1e30
EPS = 1e-5
REC = 4
META = 5 * TPC


class Tally:

    def __init__(self, nc, name, per=1, lead=0):
        self.sem = nc.alloc_semaphore(name)
        self.per = per
        self.lead = lead

    def open(self, engine):
        engine.sem_inc(self.sem, self.lead * self.per)

    def at(self, rnd, step=None):
        return (rnd + self.lead) * self.per + (self.per if step is None else step)

    def free(self, rnd):
        return rnd * self.per + self.per


@contextmanager
def stage(nc):
    before = nc.snapshot_sems()
    yield
    nc.clear_and_free_semaphores(nc.allocated_since(before))
    nc.all_engine_barrier()


def rounds(engine, count, unroll, body, peel=0):
    for turn in range(peel):
        for u in range(unroll):
            body(turn * unroll + u, u, turn)
    if count // unroll > peel:
        with engine.Fori(peel, count // unroll) as i:
            for u in range(unroll):
                body(i * unroll + u, u, i)
    for u in range(count % unroll):
        body(count // unroll * unroll + u, u, count // unroll)


def later(turn, than=0):
    return not isinstance(turn, int) or turn > than


def constants(nc, top, k):
    k.ident = top.enter_context(nc.sbuf_tensor("ident", [P, P], F32))
    k.ident_bf = top.enter_context(nc.sbuf_tensor("ident_bf", [P, P], BF16))
    k.eps = top.enter_context(nc.sbuf_tensor("eps", [P, 1], F32))
    zeroed = nc.alloc_semaphore("ident_zeroed")
    made = nc.alloc_semaphore("ident_made")
    with nc.Block() as block:
        @block.gpsimd
        def _(pool):
            pool.memset(k.eps[:], EPS)
            pool.memset(k.ident[:], 0.0).then_inc(zeroed, 1)
            pool.wait_ge(zeroed, 1)
            pool.affine_select(out=k.ident[:], in_=k.ident[:], compare_op=ALU.not_equal, fill=1.0, base=0,
                               pattern=[[-1, P]], channel_multiplier=1).then_inc(made, 1)
            pool.wait_ge(made, 1)
            pool.tensor_copy(k.ident_bf[:], k.ident[:])


def key_columns(nc, top, ctx_sort, k, src, dst, edge_weight):
    k.edge = {f: ctx_sort.enter_context(nc.sbuf_tensor(f"edge_{f}", [P, NT, 3], F32)) for f in ("src", "dst")}
    k.cols = {f: ctx_sort.enter_context(nc.sbuf_tensor(f"col_{f}", [P, NT], F32))
              for f in ("src_hi", "src_lo", "dst_hi", "dst_lo")}
    TURN = (("src", (k.edge["src"][:, :, 0], k.edge["dst"][:, :, 1])),
            ("dst", (k.edge["dst"][:, :, 0], k.edge["src"][:, :, 1])),
            ("w", (k.edge["src"][:, :, 2], k.edge["dst"][:, :, 2])),
            *((f, (k.cols[f][:],)) for f in k.cols))
    k.key_rows = {f: nc.dram_tensor(f"keys_{f}", (EP,), F32, kind="Internal").ap() for f in ("src", "dst")}
    full = E // (2 * P)
    rest = E - full * 2 * P
    with ExitStack() as ctx:
        raw = {f: ctx.enter_context(nc.sbuf_tensor(f"raw_{f}", [KR, 2 * P], I32)) for f in ("src", "dst")}
        part = {f: ctx.enter_context(nc.sbuf_tensor(f"part_{f}", [KR, 2 * P], I32))
                for f in ("src_hi", "src_lo", "dst_hi", "dst_lo")}
        rows = {f: ctx.enter_context(nc.sbuf_tensor(f"row_{f}", [KR, 2 * P], F32)) for f, _ in TURN}
        ps = ctx.enter_context(nc.psum_tensor("keys_T", [P, 2, 4, P], F32))
        s_padded = nc.alloc_semaphore("keys_padded")
        s_loaded = nc.alloc_semaphore("keys_loaded")
        s_parts = nc.alloc_semaphore("keys_parts")
        s_float = nc.alloc_semaphore("keys_float")
        s_turned = nc.alloc_semaphore("keys_turned")
        s_kept = nc.alloc_semaphore("keys_kept")
        s_stored = nc.alloc_semaphore("keys_stored")
        with nc.Block() as block:
            @block.sync
            def _(sp):
                sp.wait_ge(s_padded, 3)
                for tile, ap in ((raw["src"], src), (raw["dst"], dst), (rows["w"], edge_weight)):
                    sp.dma_start(tile[0:full, :], ap[0:full * 2 * P].rearrange("(r c) -> r c", c=2 * P)
                                 ).then_inc(s_loaded, 16)
                    sp.dma_start(tile[full:full + 1, 0:rest], ap[full * 2 * P:E].rearrange("(r c) -> r c", r=1)
                                 ).then_inc(s_loaded, 16)
                sp.wait_ge(s_float, 6)
                for f in ("src", "dst"):
                    sp.dma_start(k.key_rows[f].rearrange("(r c) -> r c", c=2 * P), rows[f][:]).then_inc(s_stored, 16)
                sp.wait_ge(s_stored, 32)

            @block.vector
            def _(dve):
                dve.memset(raw["src"][:], N).then_inc(s_padded, 1)
                dve.memset(raw["dst"][:], N).then_inc(s_padded, 1)
                dve.memset(rows["w"][:], 0.0).then_inc(s_padded, 1)
                dve.wait_ge(s_loaded, 6 * 16)
                for f in ("src", "dst"):
                    dve.tensor_scalar(part[f + "_hi"][:], raw[f][:], 7, None, ALU.arith_shift_right).then_inc(s_parts, 1)
                    dve.tensor_scalar(part[f + "_lo"][:], raw[f][:], P - 1, None, ALU.bitwise_and).then_inc(s_parts, 1)
                dve.wait_ge(s_parts, 4)
                for f in ("src", "dst"):
                    dve.tensor_copy(rows[f][:], raw[f][:]).then_inc(s_float, 1)
                    dve.tensor_copy(rows[f + "_hi"][:], part[f + "_hi"][:]).then_inc(s_float, 1)
                    dve.tensor_copy(rows[f + "_lo"][:], part[f + "_lo"][:]).then_inc(s_float, 1)
                for n, (f, outs) in enumerate(TURN):
                    dve.wait_ge(s_turned, n + 1)
                    for c in range(2):
                        for out in outs:
                            ins = dve.tensor_copy(out[:, c:NT:2], ps[:, n % 2, c, 0:KR])
                    ins.then_inc(s_kept, 1)

            @block.tensor
            def _(pe):
                pe.wait_ge(s_float, 6)
                for n, (f, _) in enumerate(TURN):
                    if n >= 2:
                        pe.wait_ge(s_kept, n - 1)
                    for c in range(2):
                        ins = pe.transpose(ps[:, n % 2, c, 0:KR], rows[f][:, c * P:(c + 1) * P], k.ident[0:KR, 0:KR])
                    ins.then_inc(s_turned, 1)


def sort_edges(nc, top, k):
    KEYS = ("dst", "src")
    k.records = {f: nc.dram_tensor(f"records_{f}", (EP + 1, REC), F32, kind="Internal").ap() for f in KEYS}
    k.node_end = {f: nc.dram_tensor(f"node_end_{f}", (HI * P,), I32, kind="Internal").ap() for f in KEYS}
    with ExitStack() as ctx:
        def sb(name, shape, dt):
            return ctx.enter_context(nc.sbuf_tensor(name, shape, dt))

        iota_hi32, iota_lo32 = sb("iota_hi32", [P, HI], I32), sb("iota_lo32", [P, P], I32)
        iota_hi, iota_lo = sb("iota_hi", [P, HI], FP16), sb("iota_lo", [P, P], FP16)
        zero_bf = sb("zero_bf", [P, HI], BF16)
        ones = sb("ones", [P, P], F32)
        upto = sb("upto", [P, P], F32)
        below = sb("below", [P, P], F32)
        below_bf = sb("below_bf", [P, P], BF16)
        first = sb("first", [1, REC], F32)
        cnt = {f: sb(f"cnt_{f}", [P, HI], F32) for f in KEYS}
        incl = {f: sb(f"incl_{f}", [P, HI], F32) for f in KEYS}
        start = {f: sb(f"start_{f}", [P, HI], F32) for f in KEYS}
        end = {f: sb(f"end_{f}", [P, HI], F32) for f in KEYS}
        end_hi = {f: sb(f"end_hi_{f}", [P, HI], BF16) for f in KEYS}
        end_lo = {f: sb(f"end_lo_{f}", [P, HI], BF16) for f in KEYS}
        none = {f: sb(f"none_{f}", [P, HI], F32) for f in KEYS}
        node = {f: sb(f"node_{f}", [P, HI], F32) for f in KEYS}
        node_i = {f: sb(f"node_i_{f}", [P, 4, P], I32) for f in KEYS}
        tot = {f: sb(f"tot_{f}", [1, HI], F32) for f in KEYS}
        run = {f: sb(f"run_{f}", [1, HI], F32) for f in KEYS}
        offs = {f: sb(f"offs_{f}", [1, HI], F32) for f in KEYS}
        ones_row = sb("ones_row", [1, HI], F32)
        s_mk = [nc.alloc_semaphore(f"sort_const{n}") for n in range(3)]

        with nc.Block() as block:
            @block.gpsimd
            def _(pool):
                pool.iota(iota_hi32[:], pattern=[[1, HI]], base=0, channel_multiplier=0).then_inc(s_mk[0], 1)
                pool.iota(iota_lo32[:], pattern=[[1, P]], base=0, channel_multiplier=0).then_inc(s_mk[0], 1)
                pool.memset(ones[:], 1.0).then_inc(s_mk[0], 1)
                pool.wait_ge(s_mk[0], 3)
                pool.affine_select(out=upto[:], in_=ones[:], compare_op=ALU.is_ge, fill=0.0, base=0,
                                   pattern=[[1, P]], channel_multiplier=-1).then_inc(s_mk[1], 1)
                pool.affine_select(out=below[:], in_=ones[:], compare_op=ALU.is_gt, fill=0.0, base=0,
                                   pattern=[[-1, P]], channel_multiplier=1).then_inc(s_mk[1], 1)

            @block.vector
            def _(dve):
                dve.memset(zero_bf[:], 0.0)
                dve.memset(ones_row[:], 1.0)
                dve.memset(first[:], -1.0).then_inc(s_mk[2], 1)
                dve.wait_ge(s_mk[1], 2)
                dve.tensor_copy(iota_hi[:], iota_hi32[:])
                dve.tensor_copy(iota_lo[:], iota_lo32[:])
                dve.tensor_copy(below_bf[:], below[:])

        one_hi = [{f: sb(f"one_hi{u}_{f}", [P, HI], BF16) for f in KEYS} for u in range(2)]
        one_lo = [{f: sb(f"one_lo{u}_{f}", [P, P], BF16) for f in KEYS} for u in range(2)]

        with ExitStack() as st:
            hist = {f: st.enter_context(nc.psum_tensor(f"hist_{f}", [P, 512], F32)) for f in KEYS}
            made = Tally(nc, "count_made", 2)
            used = Tally(nc, "count_used", 2, lead=2)
            done = nc.alloc_semaphore("count_done")
            with nc.Block() as block:
                @block.vector
                def _(dve):
                    def tile(t, u, turn):
                        dve.wait_ge(used.sem, used.free(t))
                        for f in KEYS:
                            dve.tensor_scalar(one_hi[u][f][:], iota_hi[:], k.cols[f + "_hi"][:, bass.ds(t, 1)], None,
                                              ALU.is_equal)
                            dve.tensor_scalar(one_lo[u][f][:], iota_lo[:], k.cols[f + "_lo"][:, bass.ds(t, 1)], None,
                                              ALU.is_equal).then_inc(made.sem, 1)
                    rounds(dve, NT, 2, tile)
                    dve.wait_ge(done, 2)
                    for f in KEYS:
                        dve.tensor_copy(cnt[f][:], hist[f][:, 0:HI])

                @block.tensor
                def _(pe):
                    used.open(pe)
                    for f in KEYS:
                        pe.matmul(hist[f][:, 0:HI], zero_bf[:, 0:P], zero_bf[:], start=True, stop=False)

                    def tile(t, u, turn):
                        for n, f in enumerate(KEYS):
                            pe.wait_ge(made.sem, made.at(t, n + 1))
                            pe.matmul(hist[f][:, 0:HI], one_lo[u][f][:], one_hi[u][f][:], start=False, stop=False
                                      ).then_inc(used.sem, 1)
                    rounds(pe, NT, 2, tile)
                    for f in KEYS:
                        pe.matmul(hist[f][:, 0:HI], zero_bf[:, 0:P], zero_bf[:], start=False, stop=True
                                  ).then_inc(done, 1)

        with ExitStack() as st:
            tot_ps = {f: st.enter_context(nc.psum_tensor(f"tot_ps_{f}", [1, 512], F32)) for f in KEYS}
            incl_ps = {f: st.enter_context(nc.psum_tensor(f"incl_ps_{f}", [P, 512], F32)) for f in KEYS}
            turn_ps = {f: st.enter_context(nc.psum_tensor(f"turn_ps_{f}", [P, 4, P], F32)) for f in KEYS}
            summed = nc.alloc_semaphore("pre_summed")
            tot_out = nc.alloc_semaphore("pre_tot")
            ran = nc.alloc_semaphore("pre_ran")
            offs_ok = nc.alloc_semaphore("pre_offs")
            incl_ok = nc.alloc_semaphore("pre_incl")
            copied = nc.alloc_semaphore("pre_copied")
            ended = nc.alloc_semaphore("pre_ended")
            rounded = nc.alloc_semaphore("pre_rounded")
            node_ok = nc.alloc_semaphore("pre_node")
            turned = nc.alloc_semaphore("pre_turned")
            node_int = nc.alloc_semaphore("pre_int")
            stored = nc.alloc_semaphore("pre_stored")
            with nc.Block() as block:
                @block.tensor
                def _(pe):
                    for f in KEYS:
                        pe.matmul(tot_ps[f][:, 0:HI], ones[:, 0:1], cnt[f][:], start=True, stop=True).then_inc(summed, 1)
                    for n, f in enumerate(KEYS):
                        pe.wait_ge(offs_ok, n + 1)
                        pe.matmul(incl_ps[f][:, 0:HI], upto[:], cnt[f][:], start=True, stop=False)
                        pe.matmul(incl_ps[f][:, 0:HI], ones[0:1, :], offs[f][:], start=False, stop=True).then_inc(incl_ok, 1)
                    for n, f in enumerate(KEYS):
                        pe.wait_ge(node_ok, 2 * n + 2)
                        for c in range(4):
                            w = min(P, HI - c * P)
                            ins = pe.transpose(turn_ps[f][0:w, c, :], node[f][:, c * P:c * P + w], k.ident[:])
                        ins.then_inc(turned, 1)

                @block.vector
                def _(dve):
                    for n, f in enumerate(KEYS):
                        dve.wait_ge(summed, n + 1)
                        dve.tensor_copy(tot[f][:], tot_ps[f][:, 0:HI]).then_inc(tot_out, 1)
                        dve.wait_ge(tot_out, n + 1)
                        dve.tensor_tensor_scan(run[f][:], ones_row[:], tot[f][:], 0.0, ALU.mult, ALU.add).then_inc(ran, 1)
                        dve.wait_ge(ran, n + 1)
                        dve.tensor_tensor(offs[f][:], run[f][:], tot[f][:], ALU.subtract).then_inc(offs_ok, 1)
                    for n, f in enumerate(KEYS):
                        dve.wait_ge(incl_ok, n + 1)
                        dve.tensor_copy(incl[f][:], incl_ps[f][:, 0:HI]).then_inc(copied, 1)
                        dve.wait_ge(copied, n + 1)
                        dve.tensor_tensor(start[f][:], incl[f][:], cnt[f][:], ALU.subtract)
                        dve.tensor_scalar(end[f][:], incl[f][:], -1.0, None, ALU.add).then_inc(ended, 1)
                        dve.tensor_scalar(none[f][:], cnt[f][:], 0.0, SKIP, ALU.is_equal, ALU.mult).then_inc(node_ok, 1)
                        dve.wait_ge(ended, n + 1)
                        dve.tensor_copy(end_hi[f][:], end[f][:]).then_inc(rounded, 1)
                        dve.wait_ge(node_ok, 2 * n + 1)
                        dve.tensor_tensor(node[f][:], end[f][:], none[f][:], ALU.add).then_inc(node_ok, 1)
                        dve.wait_ge(rounded, n + 1)
                        dve.tensor_tensor(end_lo[f][:], end[f][:], end_hi[f][:], ALU.subtract)
                    for n, f in enumerate(KEYS):
                        dve.wait_ge(turned, n + 1)
                        dve.tensor_copy(node_i[f][:, 0:3, :], turn_ps[f][:, 0:3, :])
                        w = HI - 3 * P
                        dve.tensor_copy(node_i[f][0:w, 3, :], turn_ps[f][0:w, 3, :]).then_inc(node_int, 1)

                @block.sync
                def _(sp):
                    for n, f in enumerate(KEYS):
                        sp.dma_start(k.records[f][0:1, :], first[:]).then_inc(stored, 16)
                    for n, f in enumerate(KEYS):
                        sp.wait_ge(node_int, n + 1)
                        for c in range(4):
                            w = min(P, HI - c * P)
                            sp.dma_start(k.node_end[f][c * P * P:(c * P + w) * P].rearrange("(h l) -> h l", l=P),
                                         node_i[f][0:w, c, :]).then_inc(stored, 16)
                    sp.wait_ge(stored, 16 * 10)

        with ExitStack() as st:
            def sb2(name, shape, dt):
                return st.enter_context(nc.sbuf_tensor(name, shape, dt))

            OTHER = {"dst": "src", "src": "dst"}
            AHEAD = 4
            key_row = [{f: sb2(f"key_row{u}_{f}", [P, P], F32) for f in KEYS} for u in range(AHEAD)]
            lo_T = [{f: sb2(f"lo_T{u}_{f}", [P, P], F32) for f in KEYS} for u in range(2)]
            lo_Tb = [{f: sb2(f"lo_Tb{u}_{f}", [P, P], BF16) for f in KEYS} for u in range(2)]
            table = [{f: sb2(f"table{u}_{f}", [P, HI], F32) for f in KEYS} for u in range(2)]
            same = [{f: sb2(f"same{u}_{f}", [P, P], BF16) for f in KEYS} for u in range(2)]
            junk = {f: [sb2(f"junk{n}_{f}", [P, HI], F32) for n in range(3)] for f in KEYS}
            got = [{f: sb2(f"got{u}_{f}", [P, 4], F32) for f in KEYS} for u in range(2)]
            rank = [{f: sb2(f"rank{u}_{f}", [P, 1], I32) for f in KEYS} for u in range(2)]
            rec = [{f: sb2(f"rec{u}_{f}", [P, REC], F32) for f in KEYS} for u in range(2)]
            count_ps = {f: st.enter_context(nc.psum_tensor(f"count_ps_{f}", [P, 512], F32)) for f in KEYS}
            turn_bf = {f: st.enter_context(nc.psum_tensor(f"turn_bf_{f}", [P, 1024], BF16)) for f in KEYS}
            at_ps = {f: st.enter_context(nc.psum_tensor(f"at_ps_{f}", [P, 512], F32)) for f in KEYS}
            end_ps = {f: st.enter_context(nc.psum_tensor(f"end_ps_{f}", [P, 512], F32)) for f in KEYS}
            row_in = [Tally(nc, f"rank_row_in{u}", 32) for u in range(AHEAD)]
            made = Tally(nc, "rank_made", 2)
            turned = Tally(nc, "rank_turned", 2)
            copied = Tally(nc, "rank_copied", 2)
            looked = Tally(nc, "rank_looked", 2)
            counted = Tally(nc, "rank_counted", 2, lead=2)
            same_ok = Tally(nc, "rank_same", 2)
            picked = Tally(nc, "rank_picked", 2, lead=1)
            row_used = Tally(nc, "rank_row_used", 2, lead=AHEAD)
            ranked = Tally(nc, "rank_ranked", 2)
            packed = Tally(nc, "rank_packed", 2)
            sent = [Tally(nc, f"rank_sent{u}", 32) for u in range(2)]
            opened = nc.alloc_semaphore("rank_opened")
            beat = nc.alloc_semaphore("rank_beat")
            with nc.Block() as block:
                @block.sync
                def _(sp):
                    def tile(t, u, turn):
                        sp.wait_ge(row_used.sem, row_used.free(t))
                        for f in KEYS:
                            sp.dma_start(key_row[u][f][:],
                                         k.key_rows[f][bass.ds(t * P, P)].partition_broadcast(P)
                                         ).then_inc(row_in[u].sem, 16)
                    rounds(sp, NT, AHEAD, tile)

                @block.vector
                def _(dve):
                    row_used.open(dve)
                    picked.open(dve)

                    def make(t, u):
                        dve.wait_ge(counted.sem, counted.free(t))
                        for f in KEYS:
                            dve.tensor_scalar(one_hi[u][f][:], iota_hi[:], k.cols[f + "_hi"][:, bass.ds(t, 1)], None,
                                              ALU.is_equal)
                            dve.tensor_scalar(one_lo[u][f][:], iota_lo[:], k.cols[f + "_lo"][:, bass.ds(t, 1)], None,
                                              ALU.is_equal).then_inc(made.sem, 1)

                    def pick(t, slot, turn):
                        u, rec_turn = slot % 2, turn * 2 + slot // 2
                        dve.wait_ge(row_in[slot].sem, row_in[slot].at(turn))
                        for f in KEYS:
                            dve.tensor_scalar(same[u][f][:], key_row[slot][f][:], k.edge[f][:, bass.ds(t, 1), 0], None,
                                              ALU.is_equal).then_inc(same_ok.sem, 1)
                        dve.wait_ge(picked.sem, picked.free(t))
                        for n, f in enumerate(KEYS):
                            dve.wait_ge(same_ok.sem, same_ok.at(t, n + 1))
                            dve.tensor_tensor_reduce(junk[f][0][:, 0:P], same[u][f][:], below_bf[:], 1.0, 0.0, ALU.mult,
                                                     ALU.add, got[u][f][:, 2:3]).then_inc(row_used.sem, 1)
                        for n, f in enumerate(KEYS):
                            dve.wait_ge(looked.sem, looked.at(t, n + 1))
                            dve.tensor_tensor_reduce(junk[f][1][:], at_ps[f][:, 0:HI], one_hi[u][f][:], 1.0, 0.0,
                                                     ALU.mult, ALU.add, got[u][f][:, 0:1])
                            dve.wait_ge(packed.sem, packed.at(t))
                            dve.tensor_tensor_reduce(junk[f][2][:], end_ps[f][:, 0:HI], one_hi[u][f][:], 1.0, 0.0,
                                                     ALU.mult, ALU.add, rec[u][OTHER[f]][:, 3:4]).then_inc(picked.sem, 1)
                        dve.wait_ge(picked.sem, picked.at(t))
                        for f in KEYS:
                            dve.scalar_tensor_tensor(rank[u][f][:], got[u][f][:, 0:1], 1.0, got[u][f][:, 2:3],
                                                     ALU.add, ALU.add).then_inc(ranked.sem, 1)

                    dve.wait_ge(opened, 1)
                    make(0, 0)

                    def tile(t, slot, turn):
                        make(t + 1, (slot + 1) % 2)
                        pick(t, slot, turn)
                    rounds(dve, NT - 1, AHEAD, tile)
                    pick(NT - 1, (NT - 1) % AHEAD, (NT - 1) // AHEAD)

                @block.scalar
                def _(act):
                    def records(t, u, turn):
                        if later(turn):
                            act.wait_ge(sent[u].sem, sent[u].at(turn - 1))
                        act.wait_ge(opened, 1)
                        for f in KEYS:
                            act.copy(rec[u][f][:, 0:3], k.edge[f][:, bass.ds(t, 1), :].rearrange("p a w -> p (a w)")
                                     ).then_inc(packed.sem, 1)

                    def tile(t, u, turn):
                        act.wait_ge(counted.sem, counted.at(t - 1))
                        for n, f in enumerate(KEYS):
                            act.copy(table[u][f][:], count_ps[f][:, 0:HI])
                            act.wait_ge(turned.sem, turned.at(t, n + 1))
                            act.copy(lo_T[u][f][:], turn_bf[f][:, 0:P])
                            act.copy(lo_Tb[u][f][:], turn_bf[f][:, 0:P]).then_inc(copied.sem, 1)
                    act.wait_ge(opened, 1)

                    def both(t, u, turn):
                        records(t, u, turn)
                        tile(t + 1, (u + 1) % 2, None)
                    tile(0, 0, 0)
                    rounds(act, NT - 1, 2, both, peel=1)
                    records(NT - 1, (NT - 1) % 2, (NT - 1) // 2)

                @block.tensor
                def _(pe):
                    for f in KEYS:
                        pe.matmul(count_ps[f][:, 0:HI], k.ident[:], start[f][:], start=True, stop=True
                                  ).then_inc(counted.sem, 2)
                    pe.wait_ge(counted.sem, 4)
                    pe.sem_inc(opened, 1)

                    def tile(t, u, turn):
                        for n, f in enumerate(KEYS):
                            pe.wait_ge(made.sem, made.at(t, n + 1))
                            pe.transpose(turn_bf[f][:, 0:P], one_lo[u][f][:], k.ident_bf[:]).then_inc(turned.sem, 1)
                        pe.wait_ge(picked.sem, picked.free(t))
                        for n, f in enumerate(KEYS):
                            pe.wait_ge(copied.sem, copied.at(t, n + 1))
                            pe.matmul(at_ps[f][:, 0:HI], lo_T[u][f][:], table[u][f][:], start=True, stop=True)
                            pe.matmul(end_ps[f][:, 0:HI], lo_Tb[u][f][:], end_hi[f][:], start=True, stop=False)
                            pe.matmul(end_ps[f][:, 0:HI], lo_Tb[u][f][:], end_lo[f][:], start=False, stop=True
                                      ).then_inc(looked.sem, 1)
                            pe.matmul(count_ps[f][:, 0:HI], one_lo[u][f][:], one_hi[u][f][:], start=False, stop=True,
                                      skip_group_check=True).then_inc(counted.sem, 1)
                    rounds(pe, NT, 2, tile)

                @block.gpsimd
                def _(pool):
                    last = pool.to_reg(EP)

                    def tile(t, u, turn):
                        for n, f in enumerate(KEYS):
                            pool.wait_ge(ranked.sem, ranked.at(t, n + 1))
                            pool.sem_inc(beat, 1)
                            pool.indirect_dma_start(
                                out=k.records[f], out_offset=bass.IndirectOffsetOnAxis(ap=rank[u][f][:, 0:1], axis=0),
                                in_=rec[u][f][:], in_offset=None, bounds_check=last, oob_is_err=False
                            ).then_inc(sent[u].sem, 16)
                    rounds(pool, NT, 2, tile)
                    for u in range(2):
                        pool.wait_ge(sent[u].sem, sent[u].at(NT // 2 - 1))


def position_columns(nc, top, k):
    k.keep = {f: nc.dram_tensor(f"keep_{f}", (EP,), BF16, kind="Internal").ap() for f in ("dst", "src")}
    size = {f: nc.dram_tensor(f"size_{f}", (EP,), F32, kind="Internal").ap() for f in ("dst", "src")}
    k.reset = nc.dram_tensor("reset", (EP,), F32, kind="Internal").ap()
    k.meta = {f: nc.dram_tensor(f"meta_{f}", (P, NCH, META), I32, kind="Internal").ap() for f in ("dst", "src")}
    k.META_AT = {"key": 0, "other": TPC, "other_end": 2 * TPC, "inv": 3 * TPC, "weight": 4 * TPC}
    HALF = EP // 2
    with ExitStack() as ctx:
        meta = {f: ctx.enter_context(nc.sbuf_tensor(f"meta_sb_{f}", [P, NCH, META], I32)) for f in k.keep}

        def field(f, what):
            at = k.META_AT[what]
            return meta[f][:, :, at:at + TPC]

        FIELDS = [(f, w, field(f, n)) for f in k.keep for w, n in ((0, "key"), (1, "other"), (3, "other_end"), (2, "weight"))]
        reset = ctx.enter_context(nc.sbuf_tensor("reset_rows", [KR, 2 * P], F32))
        here = {f: ctx.enter_context(nc.sbuf_tensor(f"here_{f}", [KR, 2 * P, REC], F32)) for f in k.keep}
        prev = {f: ctx.enter_context(nc.sbuf_tensor(f"prev_{f}", [KR, 2 * P, REC], F32)) for f in k.keep}
        keep = {f: ctx.enter_context(nc.sbuf_tensor(f"keep_rows_{f}", [KR, 2 * P], BF16)) for f in k.keep}
        fld = [ctx.enter_context(nc.sbuf_tensor(f"field{n}", [KR, 2 * P], F32)) for n in range(len(FIELDS))]
        line = ctx.enter_context(nc.sbuf_tensor("keep_line", [1, HALF], BF16))
        ones = ctx.enter_context(nc.sbuf_tensor("ones_line", [1, HALF], BF16))
        sizes = ctx.enter_context(nc.sbuf_tensor("size_line", [1, HALF], F32))
        size_rows = {f: ctx.enter_context(nc.sbuf_tensor(f"size_rows_{f}", [KR, 2 * P], F32)) for f in k.keep}
        inv_rows = {f: ctx.enter_context(nc.sbuf_tensor(f"inv_rows_{f}", [KR, 2 * P], F32)) for f in k.keep}
        ps = ctx.enter_context(nc.psum_tensor("fields_T", [P, 2, 4, P], F32))
        carry = ctx.enter_context(nc.sbuf_tensor("size_carry", [1, 1], F32))
        TURN = [(fld[n], out) for n, (_, _, out) in enumerate(FIELDS)] + [(inv_rows[f], field(f, "inv")) for f in k.keep]
        s_reset = nc.alloc_semaphore("pos_reset")
        s_meta = nc.alloc_semaphore("pos_meta")
        s_carry = nc.alloc_semaphore("pos_carry")
        s_in = nc.alloc_semaphore("pos_in")
        s_keep = nc.alloc_semaphore("pos_keep")
        s_keep_out = nc.alloc_semaphore("pos_keep_out")
        s_line = nc.alloc_semaphore("pos_line")
        s_sized = nc.alloc_semaphore("pos_sized")
        s_size_out = nc.alloc_semaphore("pos_size_out")
        s_size_in = nc.alloc_semaphore("pos_size_in")
        s_field = nc.alloc_semaphore("pos_field")
        s_turned = nc.alloc_semaphore("pos_turned")
        s_kept = nc.alloc_semaphore("pos_kept")
        s_node = nc.alloc_semaphore("pos_node")
        with nc.Block() as block:
            @block.sync
            def _(sp):
                for f in k.keep:
                    flat = k.records[f].rearrange("r c -> (r c)")
                    sp.dma_start(here[f][:], flat[REC:REC + EP * REC].rearrange("(r c w) -> r c w", c=2 * P, w=REC)
                                 ).then_inc(s_in, 16)
                    sp.dma_start(prev[f][:], flat[0:EP * REC].rearrange("(r c w) -> r c w", c=2 * P, w=REC)
                                 ).then_inc(s_in, 16)
                for n, f in enumerate(k.keep):
                    sp.wait_ge(s_keep, n + 1)
                    sp.dma_start(k.keep[f].rearrange("(r c) -> r c", c=2 * P), keep[f][:]).then_inc(s_keep_out, 16)
                sp.wait_ge(s_keep_out, 32)
                step = 0
                for f in k.keep:
                    for h in range(2):
                        if step:
                            sp.wait_ge(s_sized, step)
                            sp.wait_ge(s_size_out, 16 * step)
                        sp.dma_start(line[:], k.keep[f][h * HALF:(h + 1) * HALF].rearrange("(r c) -> r c", r=1)
                                     ).then_inc(s_line, 16)
                        sp.wait_ge(s_sized, step + 1)
                        sp.dma_start(size[f][h * HALF:(h + 1) * HALF].rearrange("(r c) -> r c", r=1), sizes[:]
                                     ).then_inc(s_size_out, 16)
                        step += 1
                sp.wait_ge(s_size_out, 16 * 4)
                for f in k.keep:
                    sp.dma_start(size_rows[f][:], size[f].rearrange("(r c) -> r c", c=2 * P)).then_inc(s_size_in, 16)
                sp.wait_ge(s_reset, 1)
                sp.dma_start(k.reset.rearrange("(r c) -> r c", c=2 * P), reset[:]).then_inc(s_meta, 16)
                sp.wait_ge(s_kept, len(TURN))
                for f in k.keep:
                    sp.dma_start(k.meta[f], meta[f][:]).then_inc(s_meta, 16)
                sp.wait_ge(s_meta, 48)

            @block.vector
            def _(dve):
                dve.memset(ones[:], 1.0)
                dve.wait_ge(s_in, 64)
                for f in k.keep:
                    dve.tensor_tensor(keep[f][:], here[f][:, :, 0], prev[f][:, :, 0], ALU.is_equal).then_inc(s_keep, 1)
                dve.wait_ge(s_keep, 1)
                dve.tensor_scalar(reset[:], keep["dst"][:], -1.0, BIG, ALU.add, ALU.mult).then_inc(s_reset, 1)
                for n, (f, w, _) in enumerate(FIELDS):
                    if w in (0, 1):
                        dve.tensor_scalar(fld[n][:], here[f][:, :, w], float(N - 1), None, ALU.min).then_inc(s_field, 1)
                    else:
                        dve.tensor_copy(fld[n][:], here[f][:, :, w]).then_inc(s_field, 1)
                step = 0
                for f in k.keep:
                    for h in range(2):
                        dve.wait_ge(s_line, 16 * (step + 1))
                        if h == 1:
                            dve.tensor_copy(carry[:], sizes[:, HALF - 1:HALF]).then_inc(s_carry, 1)
                            dve.wait_ge(s_carry, step // 2 + 1)
                        if step:
                            dve.wait_ge(s_size_out, 16 * step)
                        dve.tensor_tensor_scan(sizes[:], line[:], ones[:], carry[:] if h else 0.0,
                                               ALU.mult, ALU.add).then_inc(s_sized, 1)
                        step += 1
                dve.wait_ge(s_size_in, 32)
                for f in k.keep:
                    dve.reciprocal(inv_rows[f][:], size_rows[f][:]).then_inc(s_field, 1)
                for n, (_, out) in enumerate(TURN):
                    dve.wait_ge(s_turned, n + 1)
                    is_float = n >= len(FIELDS) or FIELDS[n][1] == 2
                    for c in range(2):
                        to = (out.bitcast(F32) if is_float else out).rearrange("p a (b c) -> p a b c", c=2)[:, :, :, c]
                        ins = dve.tensor_copy(to, ps[:, n % 2, c, 0:KR].rearrange("p (a b) -> p a b", b=TPC // 2))
                    ins.then_inc(s_kept, 1)

            @block.tensor
            def _(pe):
                for n, (rows, _) in enumerate(TURN):
                    pe.wait_ge(s_field, n + 1)
                    if n >= 2:
                        pe.wait_ge(s_kept, n - 1)
                    for c in range(2):
                        ins = pe.transpose(ps[:, n % 2, c, 0:KR], rows[:, c * P:(c + 1) * P], k.ident[0:KR, 0:KR])
                    ins.then_inc(s_turned, 1)


def load_weights(nc, top, k, w):
    def sb(name, shape, dt=F32, ctx=top):
        return ctx.enter_context(nc.sbuf_tensor(name, shape, dt))

    PLAIN = ("Wq", "Wk", "Wv", "Ws", "W1", "W2", "W")
    TURNED = ("W", "W_rel", "W_root")
    COLS, ROWS = ("bq", "bk", "bv"), ("bs", "b1", "b2", "b_rel")
    k.w = {f: sb(f"w_{f}", [P, H, C]) for f in PLAIN}
    k.wT = {f: sb(f"wT_{f}", [P, H, C]) for f in TURNED}
    k.col = {f: sb(f"bias_{f}", [P, H]) for f in COLS}
    k.row = {f: sb(f"row_{f}", [P, C]) for f in ROWS}
    k.row["zero"] = sb("row_zero", [P, C])
    k.slope = sb("slope", [P, 1])
    HEADS2 = w["att"].shape[0]
    CPH = C // HEADS2
    k.w_att = sb("w_att", [P, H, 2, HEADS2])
    s_zero = nc.alloc_semaphore("w_zero")
    s_in = nc.alloc_semaphore("w_in")
    s_turned = nc.alloc_semaphore("w_turned")
    s_kept = nc.alloc_semaphore("w_kept")
    with ExitStack() as ctx:
        raw = {f: sb(f"raw_{f}", [P, H, C], ctx=ctx) for f in TURNED if f not in PLAIN}
        att = sb("att_blocks", [P, H, 2, HEADS2], ctx=ctx)
        ps = ctx.enter_context(nc.psum_tensor("w_ps", [P, 4, H, C], F32))
        with nc.Block() as block:
            @block.sync
            def _(sp):
                n = 0
                for f, t in [(f, k.w[f]) for f in PLAIN] + list(raw.items()):
                    sp.dma_start(t[:], w[f].rearrange("(h p) c -> p h c", p=P)).then_inc(s_in, 16)
                    n += 16
                for f in ROWS:
                    sp.dma_start(k.row[f][:], w[f].partition_broadcast(P)).then_inc(s_in, 16)
                    n += 16
                sp.dma_start(k.slope[:], w["a"].partition_broadcast(P)).then_inc(s_in, 16)
                with nc.allow_non_contiguous_dma(reason="columns of a few words"):
                    for f in COLS:
                        sp.dma_start(k.col[f][:], w[f].rearrange("(h p) -> p h", p=P)).then_inc(s_in, 16)
                        n += 16
                    sp.wait_ge(s_zero, 1)
                    for h in range(HEADS2):
                        lo = h * CPH % P
                        for s in range(2):
                            sp.dma_start(att[lo:lo + CPH, h * CPH // P, s, h:h + 1],
                                         w["att"][h, s * CPH:(s + 1) * CPH].rearrange("(c o) -> c o", o=1)
                                         ).then_inc(s_in, 16)
                            n += 16
                sp.wait_ge(s_in, n + 16)

            ALL_IN = 16 * (len(PLAIN) + len(raw) + len(ROWS) + 1 + len(COLS) + 2 * HEADS2)

            @block.tensor
            def _(pe):
                pe.wait_ge(s_in, ALL_IN)
                for n, f in enumerate(TURNED):
                    t = k.w.get(f, raw.get(f))
                    for a in range(H):
                        for b in range(H):
                            ins = pe.transpose(ps[:, n, a, b * P:(b + 1) * P], t[:, b, a * P:(a + 1) * P], k.ident[:])
                    ins.then_inc(s_turned, 1)
                for a in range(H):
                    for b in range(H):
                        ins = pe.matmul(ps[:, 3, a, 0:2 * HEADS2], k.w["W"][:, b, a * P:(a + 1) * P],
                                        att[:, b, :, :].rearrange("p s h -> p (s h)"), start=(b == 0), stop=(b == H - 1))
                ins.then_inc(s_turned, 1)

            @block.vector
            def _(dve):
                dve.memset(k.row["zero"][:], 0.0)
                dve.memset(att[:], 0.0).then_inc(s_zero, 1)
                dve.wait_ge(s_in, ALL_IN)
                for h in range(H):
                    dve.tensor_tensor(k.w["Ws"][:, h, h * P:(h + 1) * P], k.w["Ws"][:, h, h * P:(h + 1) * P], k.ident[:],
                                      ALU.add)
                for n, f in enumerate(TURNED):
                    dve.wait_ge(s_turned, n + 1)
                    dve.tensor_copy(k.wT[f][:], ps[:, n, :, :])
                dve.wait_ge(s_turned, len(TURNED) + 1)
                dve.tensor_copy(k.w_att[:].rearrange("p h s n -> p h (s n)"), ps[:, 3, :, 0:2 * HEADS2])


def sum_pass(nc, top, k, name, order, table, what, out, matrix=None, weighted=False, scaled=False, bias=None,
             prelu=False):
    SL = 4
    WB = 2
    IDX, INV, WGT = k.META_AT[what], k.META_AT["inv"], k.META_AT["weight"]
    with ExitStack() as ctx:
        def sb(n, shape, dt=F32):
            return [ctx.enter_context(nc.sbuf_tensor(f"{name}_{n}{u}", shape, dt)) for u in range(SL)]

        meta, keep, rows = sb("meta", [P, META], I32), sb("keep", [P, CH], BF16), sb("rows", [P, TPC, C])
        acc, res, neg = sb("acc", [P, H, CH]), sb("res", [P, TPC, C]), sb("neg", [P, TPC, C])[0]
        turn_ps = [ctx.enter_context(nc.psum_tensor(f"{name}_turn{u}", [P, H, CH], F32)) for u in range(WB)]
        row_ps = [ctx.enter_context(nc.psum_tensor(f"{name}_row{u}", [P, TPC, C], F32)) for u in range(WB)]
        loaded = [Tally(nc, f"{name}_loaded{u}", 32) for u in range(SL)]
        gathered = [Tally(nc, f"{name}_gathered{u}", 16 * TPC) for u in range(SL)]
        weighed = Tally(nc, f"{name}_weighed")
        turned = Tally(nc, f"{name}_turned", H, lead=SL)
        summed = Tally(nc, f"{name}_summed", H, lead=SL)
        mapped = Tally(nc, f"{name}_mapped", 2, lead=SL)
        affine = Tally(nc, f"{name}_affine")
        bent = Tally(nc, f"{name}_bent")
        kept = Tally(nc, f"{name}_kept", 1, lead=SL)
        stored = [Tally(nc, f"{name}_stored{u}", 16) for u in range(SL)]
        zeroed = nc.alloc_semaphore(f"{name}_zeroed")
        beat = nc.alloc_semaphore(f"{name}_beat")
        with nc.Block() as block:
            @block.sync
            def _(sp):
                def chunk(c, u, turn):
                    sp.wait_ge(kept.sem, kept.at(c - SL))
                    sp.dma_start(meta[u][:], k.meta[order][:, bass.ds(c, 1), :].rearrange("p a w -> p (a w)")
                                 ).then_inc(loaded[u].sem, 16)
                    sp.dma_start(keep[u][:], k.keep[order][bass.ds(c * CH, CH)].partition_broadcast(P)
                                 ).then_inc(loaded[u].sem, 16)
                rounds(sp, NCH, SL, chunk)

            @block.gpsimd
            def _(pool):
                last = pool.to_reg(table.shape[0] - 1)

                def chunk(c, u, turn):
                    pool.wait_ge(loaded[u].sem, loaded[u].at(turn))
                    pool.wait_ge(turned.sem, turned.at(c - SL))
                    pool.sem_inc(beat, 1)
                    for t in range(TPC):
                        pool.indirect_dma_start(
                            out=rows[u][:, t, :], out_offset=None, in_=table,
                            in_offset=bass.IndirectOffsetOnAxis(ap=meta[u][:, IDX + t:IDX + t + 1], axis=0),
                            bounds_check=last, oob_is_err=False).then_inc(gathered[u].sem, 16)
                rounds(pool, NCH, SL, chunk)

            @block.tensor
            def _(pe):
                turned.open(pe)
                mapped.open(pe)

                def turn_chunk(c, u, turn):
                    if weighted:
                        pe.wait_ge(weighed.sem, weighed.at(c))
                    else:
                        pe.wait_ge(gathered[u].sem, gathered[u].at(turn))
                    pe.wait_ge(summed.sem, summed.at(c - WB))
                    for h in range(H):
                        for t in range(TPC):
                            ins = pe.transpose(turn_ps[u % WB][:, h, t * P:(t + 1) * P],
                                               rows[u][:, t, h * P:(h + 1) * P], k.ident[:])
                        ins.then_inc(turned.sem, 1)

                def map_chunk(c, u):
                    pe.wait_ge(kept.sem, kept.at(c - WB))
                    pe.wait_ge(summed.sem, summed.at(c))
                    for t in range(TPC):
                        at = slice(t * P, (t + 1) * P)
                        for h in range(H):
                            if matrix is None:
                                ins = pe.transpose(row_ps[u % WB][:, t, h * P:(h + 1) * P], acc[u][:, h, at], k.ident[:])
                            else:
                                ins = pe.matmul(row_ps[u % WB][:, t, :], acc[u][:, h, at], matrix[:, h, :],
                                                start=(h == 0), stop=(h == H - 1))
                        if t % 2:
                            ins.then_inc(mapped.sem, 1)

                def turn_next(c, u, turn):
                    turn_chunk(c + 1, (u + 1) % SL, turn + (u + 1) // SL)
                turn_chunk(0, 0, 0)

                def step(c, u, turn):
                    turn_next(c, u, turn)
                    map_chunk(c, u)
                rounds(pe, NCH - 1, SL, step)
                map_chunk(NCH - 1, (NCH - 1) % SL)

            @block.vector
            def _(dve):
                dve.memset(acc[SL - 1][:], 0.0).then_inc(zeroed, 1)
                summed.open(dve)
                dve.wait_ge(zeroed, 1)
                if bias is not None:
                    kept.open(dve)

                def sum_chunk(c, u, turn):
                    dve.wait_ge(loaded[u].sem, loaded[u].at(turn))
                    dve.wait_ge(mapped.sem, mapped.at(c - SL))
                    dve.wait_ge(summed.sem, summed.at(c - 1))
                    for h in range(H):
                        dve.wait_ge(turned.sem, turned.at(c, h + 1))
                        dve.tensor_tensor_scan(acc[u][:, h, :], keep[u][:], turn_ps[u % WB][:, h, :],
                                               acc[(u - 1) % SL][:, h, CH - 1:CH], ALU.mult, ALU.add
                                               ).then_inc(summed.sem, 1)

                def keep_chunk(c, u, turn):
                    if later(turn):
                        dve.wait_ge(stored[u].sem, stored[u].at(turn - 1))
                    for t in range(TPC):
                        if t % 2 == 0:
                            dve.wait_ge(mapped.sem, mapped.at(c, t // 2 + 1))
                        factor = meta[u][:, INV + t:INV + t + 1].bitcast(F32) if scaled else 1.0
                        ins = dve.scalar_tensor_tensor(res[u][:, t, :], row_ps[u % WB][:, t, :], factor, bias[:],
                                                       ALU.mult, ALU.add)
                    if not prelu:
                        ins.then_inc(kept.sem, 1)
                        return
                    ins.then_inc(affine.sem, 1)
                    dve.wait_ge(affine.sem, affine.at(c))
                    dve.wait_ge(kept.sem, kept.at(c - 1))
                    dve.tensor_scalar(neg[:], res[u][:], 0.0, k.slope[:, 0:1], ALU.min, ALU.mult).then_inc(bent.sem, 1)
                    dve.wait_ge(bent.sem, bent.at(c))
                    dve.scalar_tensor_tensor(res[u][:], res[u][:], 0.0, neg[:], ALU.max, ALU.add).then_inc(kept.sem, 1)

                def step(c, u, turn):
                    sum_chunk(c + 1, (u + 1) % SL, turn + (u + 1) // SL)
                    if bias is not None:
                        keep_chunk(c, u, turn)
                sum_chunk(0, 0, 0)
                rounds(dve, NCH - 1, SL, step, peel=1)
                if bias is not None:
                    keep_chunk(NCH - 1, (NCH - 1) % SL, (NCH - 1) // SL)

            @block.scalar
            def _(act):
                if bias is None:
                    kept.open(act)

                def weigh(c, u, turn):
                    act.wait_ge(gathered[u].sem, gathered[u].at(turn))
                    for t in range(TPC):
                        ins = act.activation(rows[u][:, t, :], rows[u][:, t, :], ACT.Copy,
                                             scale=meta[u][:, WGT + t:WGT + t + 1].bitcast(F32))
                    ins.then_inc(weighed.sem, 1)

                def keep_chunk(c, u, turn):
                    if bias is None:
                        if later(turn):
                            act.wait_ge(stored[u].sem, stored[u].at(turn - 1))
                        for t in range(TPC):
                            if t % 2 == 0:
                                act.wait_ge(mapped.sem, mapped.at(c, t // 2 + 1))
                            ins = act.activation(res[u][:, t, :], row_ps[u % WB][:, t, :], ACT.Copy,
                                                 scale=meta[u][:, INV + t:INV + t + 1].bitcast(F32) if scaled else 1.0)
                        ins.then_inc(kept.sem, 1)
                    act.wait_ge(kept.sem, kept.at(c))
                    act.dma_start(out[bass.ds(c * CH, CH), :].rearrange("(t p) f -> p t f", p=P), res[u][:]
                                  ).then_inc(stored[u].sem, 16)

                def step(c, u, turn):
                    if weighted:
                        weigh(c + 1, (u + 1) % SL, turn + (u + 1) // SL)
                    keep_chunk(c, u, turn)
                if weighted:
                    weigh(0, 0, 0)
                rounds(act, NCH - 1, SL, step, peel=1)
                keep_chunk(NCH - 1, (NCH - 1) % SL, (NCH - 1) // SL)
                for u in range(SL):
                    act.wait_ge(stored[u].sem, stored[u].at((NCH - 1 - u) // SL))


def attention_pass(nc, top, k, name, heads, src_table, src_what, dst_table, out, dot, scale, bias=None):
    SL = 2
    CPH = C // heads
    IDX_S, IDX_D = k.META_AT[src_what], k.META_AT["key"]
    ALPHA = 0.2
    NJ = 3
    with ExitStack() as ctx:
        def sb1(n, shape, dt=F32):
            return ctx.enter_context(nc.sbuf_tensor(f"{name}_{n}", shape, dt))

        def sb(n, shape, dt=F32):
            return [sb1(f"{n}{u}", shape, dt) for u in range(SL)]

        def ps(n, shape):
            return ctx.enter_context(nc.psum_tensor(f"{name}_{n}", shape, F32))

        meta, reset = sb("meta", [P, META], I32), sb("reset", [heads, CH])
        src_rows, dst_rows = sb("src_rows", [P, TPC, C]), sb("dst_rows", [P, TPC, C])
        src_T, dst_T = sb("src_T", [P, H, CH]), sb("dst_T", [P, H, CH])
        query, prod = sb1("query", [P, H, CH]), sb1("prod", [P, H, CH])
        value = sb("value", [P, H, CH])
        top_m = sb("max", [heads, CH + 1])
        shifted = sb1("shifted", [heads, CH])
        score = sb1("score", [heads, 2, CH])
        diff, expo = sb("diff", [heads, 2, CH]), sb("expo", [heads, 2, CH])
        den = sb("den", [heads, CH])
        part, acc = sb1("part", [P, H, CH]), sb("acc", [P, H, CH])
        inv = sb("inv", [P, TPC, heads])
        res = sb("res", [P, TPC, C])
        low, up = sb1("low", [P, TPC, C]), sb1("up", [P, TPC, C])
        sel, sel_T, ones = sb1("sel", [P, H, heads]), sb1("sel_T", [heads, C]), sb1("ones", [P, C])
        turn_ps = ps("turn", [P, H, CH])
        proj_ps = [ps(f"proj{n}", [P, CH]) for n in range(NJ)]
        score_ps = ps("score_ps", [P, CH])
        back_ps = [ps(f"back{n}", [P, CH]) for n in range(2)]
        T = lambda n, per=1, lead=0: Tally(nc, f"{name}_{n}", per, lead)
        loaded = [T(f"loaded{u}", 32) for u in range(SL)]
        got_src = [T(f"got_src{u}", 16 * TPC) for u in range(SL)]
        got_dst = [T(f"got_dst{u}", 16 * TPC) for u in range(SL)]
        turned = T("turned", 2, lead=SL)
        in_T = T("in_T", 2, lead=SL)
        projected = T("projected", 6 if dot else 2)
        proj_out = T("proj_out", 2 * H if dot else H, lead=SL)
        multiplied = T("multiplied", H, lead=SL)
        scored = T("scored", 1, lead=SL)
        maxed = T("maxed", 2, lead=SL)
        shift_ok = T("shift_ok")
        diffed = T("diffed", 2, lead=SL)
        leaky = T("leaky", 2, lead=SL)
        exped = T("exped", 1, lead=SL)
        summed = T("summed", 1, lead=SL)
        spread = T("spread", H, lead=SL)
        parted = T("parted", H, lead=SL)
        ran = T("ran", H, lead=SL)
        den_T = T("den_T", 1, lead=SL)
        inverted = T("inverted", 2, lead=SL)
        back = T("back", 2, lead=SL)
        divided = T("divided", 2, lead=SL)
        kept = T("kept", 1, lead=SL)
        lowered, elu_e = T("lowered", 1, lead=SL), T("elu_e", 1, lead=SL)
        stored = [T(f"stored{u}", 16) for u in range(SL)]
        setup = [nc.alloc_semaphore(f"{name}_setup{n}") for n in range(4)]
        beat = nc.alloc_semaphore(f"{name}_beat")
        pe_beat = nc.alloc_semaphore(f"{name}_pe_beat")
        with nc.Block() as block:
            @block.gpsimd
            def _(pool):
                pool.wait_ge(setup[0], 1)
                selv = sel[:].rearrange("p a b -> p (a b)")
                pool.affine_select(out=sel[:], in_=ones[:, 0:H * heads].rearrange("p (a b) -> p a b", a=H),
                                   compare_op=ALU.is_ge, fill=0.0, base=0, pattern=[[P, H], [-CPH, heads]],
                                   channel_multiplier=1).then_inc(setup[1], 1)
                pool.affine_select(out=sel_T[:], in_=ones[0:heads, :], compare_op=ALU.is_ge, fill=0.0, base=0,
                                   pattern=[[1, C]], channel_multiplier=-CPH).then_inc(setup[1], 1)
                pool.wait_ge(setup[1], 2)
                pool.affine_select(out=sel[:], in_=sel[:], compare_op=ALU.is_ge, fill=0.0, base=CPH - 1,
                                   pattern=[[-P, H], [CPH, heads]], channel_multiplier=-1).then_inc(setup[2], 1)
                pool.affine_select(out=sel_T[:], in_=sel_T[:], compare_op=ALU.is_ge, fill=0.0, base=CPH - 1,
                                   pattern=[[-1, C]], channel_multiplier=CPH).then_inc(setup[2], 1)
                last_s = pool.to_reg(src_table.shape[0] - 1)
                last_d = pool.to_reg(dst_table.shape[0] - 1)

                def chunk(c, u, turn):
                    pool.wait_ge(loaded[u].sem, loaded[u].at(turn))
                    pool.wait_ge(turned.sem, turned.at(c - SL))
                    pool.sem_inc(beat, 1)
                    for rows, table, idx, last, got in ((src_rows, src_table, IDX_S, last_s, got_src),
                                                        (dst_rows, dst_table, IDX_D, last_d, got_dst)):
                        for t in range(TPC):
                            pool.indirect_dma_start(
                                out=rows[u][:, t, :], out_offset=None, in_=table,
                                in_offset=bass.IndirectOffsetOnAxis(ap=meta[u][:, idx + t:idx + t + 1], axis=0),
                                bounds_check=last, oob_is_err=False).then_inc(got[u].sem, 16)
                rounds(pool, NCH, SL, chunk)

            @block.sync
            def _(sp):
                def chunk(c, u, turn):
                    sp.wait_ge(turned.sem, turned.at(c - SL))
                    sp.wait_ge(maxed.sem, maxed.at(c - SL))
                    sp.dma_start(meta[u][:], k.meta["dst"][:, bass.ds(c, 1), :].rearrange("p a w -> p (a w)")
                                 ).then_inc(loaded[u].sem, 16)
                    sp.dma_start(reset[u][:], k.reset[bass.ds(c * CH, CH)].partition_broadcast(heads)
                                 ).then_inc(loaded[u].sem, 16)
                rounds(sp, NCH, SL, chunk)

            @block.tensor
            def _(pe):
                for t in (turned, scored, spread, den_T, back):
                    t.open(pe)
                pe.wait_ge(setup[2], 2)

                def project(c, n, weight, half, rhs):
                    for h in range(H):
                        ins = pe.matmul(proj_ps[n % NJ][:], weight[:, h, half * P:(half + 1) * P], rhs[:, h, :],
                                        start=(h == 0), stop=(h == H - 1))
                    ins.then_inc(projected.sem, 1)

                def front(c, u, turn):
                    for n, (rows, got) in enumerate(((src_rows, got_src), (dst_rows, got_dst))):
                        pe.wait_ge(got[u].sem, got[u].at(turn))
                        pe.wait_ge(in_T.sem, in_T.at(c - 1 + n, 2 if n == 0 else 1))
                        for h in range(H):
                            for t in range(TPC):
                                ins = pe.transpose(turn_ps[:, h, t * P:(t + 1) * P], rows[u][:, t, h * P:(h + 1) * P],
                                                   k.ident[:])
                        ins.then_inc(turned.sem, 1)
                    pe.wait_ge(in_T.sem, in_T.at(c))
                    if dot:
                        pe.wait_ge(proj_out.sem, proj_out.at(c - 1))
                        pe.wait_ge(inverted.sem, inverted.at(c - 2))
                        project(c, 0, k.w["Wq"], 0, dst_T[u])
                        project(c, 1, k.w["Wk"], 0, src_T[u])
                        project(c, 2, k.w["Wq"], 1, dst_T[u])
                        pe.wait_ge(proj_out.sem, proj_out.at(c, 1))
                        project(c, 3, k.w["Wk"], 1, src_T[u])
                        pe.wait_ge(multiplied.sem, multiplied.at(c, 1))
                        project(c, 4, k.w["Wv"], 0, src_T[u])
                        pe.wait_ge(proj_out.sem, proj_out.at(c, 2))
                        project(c, 5, k.w["Wv"], 1, src_T[u])
                        pe.wait_ge(maxed.sem, maxed.at(c - 1, 1))
                        pe.wait_ge(diffed.sem, diffed.at(c - 1))
                        pe.wait_ge(multiplied.sem, multiplied.at(c))
                        for h in range(H):
                            ins = pe.matmul(score_ps[0:heads, :], sel[:, h, :], prod[:, h, :], start=(h == 0), stop=(h == H - 1))
                        ins.then_inc(scored.sem, 1)
                    else:
                        pe.wait_ge(leaky.sem, leaky.at(c - 1))
                        for n, rhs in enumerate((src_T[u], dst_T[u])):
                            for h in range(H):
                                ins = pe.matmul(score_ps[0:heads, :], k.w_att[:, h, n, :], rhs[:, h, :],
                                                start=(n == 0 and h == 0), stop=(n == 1 and h == H - 1))
                        ins.then_inc(scored.sem, 1)
                        pe.wait_ge(proj_out.sem, proj_out.at(c - 1))
                        project(c, 0, k.wT["W"], 0, src_T[u])
                        project(c, 1, k.wT["W"], 1, src_T[u])

                den_ps = proj_ps[0] if dot else proj_ps[2]

                def rear(c, u, after):
                    pe.wait_ge(exped.sem, exped.at(c))
                    for h in range(H):
                        at = slice(h * P, (h + 1) * P)
                        if h == 0:
                            pe.wait_ge(divided.sem, divided.at(c - 1))
                        else:
                            pe.wait_ge(parted.sem, parted.at(c, h))
                            pe.wait_ge(ran.sem, ran.at(c, h))
                        pe.matmul(back_ps[0][:], sel_T[:, at], expo[u][:, 1, :], start=True, stop=True)
                        pe.matmul(back_ps[1][:], sel_T[:, at], expo[u][:, 0, :], start=True, stop=True
                                  ).then_inc(spread.sem, 1)
                    pe.wait_ge(summed.sem, summed.at(c))
                    if dot:
                        pe.wait_ge(multiplied.sem, multiplied.at(after))
                    pe.wait_ge(inverted.sem, inverted.at(c - 1))
                    pe.sem_inc(pe_beat, 1)
                    for t in range(TPC):
                        ins = pe.transpose(den_ps[:, t * heads:(t + 1) * heads], den[u][:, t * P:(t + 1) * P],
                                           k.ident[0:heads, 0:heads])
                    ins.then_inc(den_T.sem, 1)
                    pe.wait_ge(ran.sem, ran.at(c))
                    for t in range(TPC):
                        for h in range(H):
                            ins = pe.transpose(back_ps[t // 2][:, (t % 2) * C + h * P:(t % 2) * C + (h + 1) * P],
                                               acc[u][:, h, t * P:(t + 1) * P], k.ident[:])
                        if t % 2:
                            ins.then_inc(back.sem, 1)

                front(0, 0, 0)

                def step(c, u, turn):
                    front(c + 1, (u + 1) % SL, turn + (u + 1) // SL)
                    rear(c, u, c + 1)
                rounds(pe, NCH - 1, SL, step)
                rear(NCH - 1, (NCH - 1) % SL, NCH - 1)

            @block.scalar
            def _(act):
                for t in (in_T, proj_out, exped, elu_e):
                    t.open(act)

                def front(c, u):
                    for n, to in enumerate((src_T, dst_T)):
                        act.wait_ge(turned.sem, turned.at(c, n + 1))
                        if n == 0:
                            act.wait_ge(scored.sem, scored.at(c - SL))
                            if dot:
                                act.wait_ge(projected.sem, projected.at(c - 1))
                            else:
                                act.wait_ge(projected.sem, projected.at(c - 1))
                        act.copy(to[u][:], turn_ps[:]).then_inc(in_T.sem, 1)
                    if dot:
                        act.wait_ge(multiplied.sem, multiplied.at(c - 1))
                        for h in range(H):
                            act.wait_ge(projected.sem, projected.at(c, 2 * h + 1))
                            act.activation(query[:, h, :], proj_ps[2 * h % NJ][:], ACT.Identity, bias=k.col["bq"][:, h:h + 1]
                                           ).then_inc(proj_out.sem, 1)
                        act.wait_ge(parted.sem, parted.at(c - SL))
                        for h in range(H):
                            act.wait_ge(projected.sem, projected.at(c, 5 + h))
                            act.activation(value[u][:, h, :], proj_ps[(4 + h) % NJ][:], ACT.Identity,
                                           bias=k.col["bv"][:, h:h + 1]).then_inc(proj_out.sem, 1)
                    else:
                        act.wait_ge(parted.sem, parted.at(c - SL))
                        for h in range(H):
                            act.wait_ge(projected.sem, projected.at(c, 1 + h))
                            act.copy(value[u][:, h, :], proj_ps[h][:]).then_inc(proj_out.sem, 1)
                    act.wait_ge(diffed.sem, diffed.at(c))
                    act.wait_ge(summed.sem, summed.at(c - SL))
                    act.wait_ge(spread.sem, spread.at(c - SL))
                    act.activation(expo[u][:], diff[u][:], ACT.Exp, scale=scale).then_inc(exped.sem, 1)

                def rear(c, u, turn):
                    if not dot:
                        act.wait_ge(lowered.sem, lowered.at(c))
                        act.activation(low[:], low[:], ACT.Exp)
                        act.activation(up[:], res[u][:], ACT.Relu).then_inc(elu_e.sem, 1)
                    act.wait_ge(kept.sem, kept.at(c))
                    act.dma_start(out[bass.ds(c * CH, CH), :].rearrange("(t p) f -> p t f", p=P), res[u][:]
                                  ).then_inc(stored[u].sem, 16)

                front(0, 0)

                def step(c, u, turn):
                    front(c + 1, (u + 1) % SL)
                    rear(c, u, turn)
                rounds(act, NCH - 1, SL, step)
                rear(NCH - 1, (NCH - 1) % SL, (NCH - 1) // SL)
                for u in range(SL):
                    act.wait_ge(stored[u].sem, stored[u].at((NCH - 1 - u) // SL))

            @block.vector
            def _(dve):
                dve.memset(ones[:], 1.0).then_inc(setup[0], 1)
                for t in (multiplied, maxed, diffed, leaky, summed, parted, ran, inverted, divided, kept, lowered):
                    t.open(dve)
                dve.memset(top_m[SL - 1][:], -BIG)
                dve.memset(den[SL - 1][:], 0.0)
                dve.memset(acc[SL - 1][:], 0.0).then_inc(setup[3], 1)
                dve.wait_ge(setup[3], 1)

                def front(c, u, turn):
                    before = (u - 1) % SL
                    if dot:
                        dve.wait_ge(scored.sem, scored.at(c - 1))
                        for h in range(H):
                            dve.wait_ge(proj_out.sem, proj_out.at(c, h + 1))
                            dve.wait_ge(projected.sem, projected.at(c, 2 * h + 2))
                            dve.scalar_tensor_tensor(prod[:, h, :], proj_ps[(2 * h + 1) % NJ][:], k.col["bk"][:, h:h + 1],
                                                     query[:, h, :], ALU.add, ALU.mult).then_inc(multiplied.sem, 1)
                    dve.wait_ge(scored.sem, scored.at(c))
                    dve.wait_ge(diffed.sem, diffed.at(c - 1))
                    if dot:
                        scores = score_ps[0:heads, :]
                    else:
                        dve.tensor_scalar(score[:, 0, :], score_ps[0:heads, :], ALPHA, None, ALU.mult).then_inc(leaky.sem, 1)
                        dve.wait_ge(leaky.sem, leaky.at(c, 1))
                        dve.tensor_tensor(score[:, 1, :], score[:, 0, :], score_ps[0:heads, :], ALU.max).then_inc(leaky.sem, 1)
                        dve.wait_ge(leaky.sem, leaky.at(c))
                        scores = score[:, 1, :]
                    dve.wait_ge(loaded[u].sem, loaded[u].at(turn))
                    dve.wait_ge(maxed.sem, maxed.at(c - 1))
                    dve.tensor_copy(top_m[u][:, 0:1], top_m[before][:, CH:CH + 1])
                    dve.tensor_tensor_scan(top_m[u][:, 1:CH + 1], reset[u][:], scores, top_m[before][:, CH:CH + 1],
                                           ALU.add, ALU.max).then_inc(maxed.sem, 1)
                    dve.wait_ge(maxed.sem, maxed.at(c, 1))
                    dve.tensor_tensor(shifted[:], top_m[u][:, 0:CH], reset[u][:], ALU.add).then_inc(maxed.sem, 1)
                    dve.wait_ge(exped.sem, exped.at(c - SL))
                    dve.tensor_tensor(diff[u][:, 1, :], scores, top_m[u][:, 1:CH + 1], ALU.subtract).then_inc(diffed.sem, 1)
                    dve.wait_ge(maxed.sem, maxed.at(c))
                    dve.tensor_tensor(diff[u][:, 0, :], shifted[:], top_m[u][:, 1:CH + 1], ALU.subtract
                                      ).then_inc(diffed.sem, 1)

                def rear(c, u, turn):
                    before = (u - 1) % SL
                    dve.wait_ge(exped.sem, exped.at(c))
                    dve.wait_ge(den_T.sem, den_T.at(c - SL))
                    dve.wait_ge(summed.sem, summed.at(c - 1))
                    dve.tensor_tensor_scan(den[u][:], expo[u][:, 0, :], expo[u][:, 1, :], den[before][:, CH - 1:CH],
                                           ALU.mult, ALU.add).then_inc(summed.sem, 1)
                    dve.wait_ge(proj_out.sem, proj_out.at(c))
                    dve.wait_ge(back.sem, back.at(c - SL))
                    dve.wait_ge(ran.sem, ran.at(c - 1))
                    for h in range(H):
                        dve.wait_ge(spread.sem, spread.at(c, h + 1))
                        dve.tensor_tensor(part[:, h, :], back_ps[0][:], value[u][:, h, :], ALU.mult).then_inc(parted.sem, 1)
                        dve.wait_ge(parted.sem, parted.at(c, h + 1))
                        dve.tensor_tensor_scan(acc[u][:, h, :], back_ps[1][:], part[:, h, :], acc[before][:, h, CH - 1:CH],
                                               ALU.mult, ALU.add).then_inc(ran.sem, 1)
                    dve.wait_ge(den_T.sem, den_T.at(c))
                    den_ps = (proj_ps[0] if dot else proj_ps[2])[:, 0:TPC * heads].rearrange("p (t n) -> p t n", n=heads)
                    dve.wait_ge(divided.sem, divided.at(c - SL))
                    dve.tensor_scalar(inv[u][:], den_ps, 0.0 if dot else 1e-16, None, ALU.add).then_inc(inverted.sem, 1)
                    dve.wait_ge(inverted.sem, inverted.at(c, 1))
                    dve.reciprocal(inv[u][:], inv[u][:]).then_inc(inverted.sem, 1)
                    dve.wait_ge(inverted.sem, inverted.at(c))
                    if later(turn):
                        dve.wait_ge(stored[u].sem, stored[u].at(turn - 1))
                    for n in range(2):
                        dve.wait_ge(back.sem, back.at(c, n + 1))
                        for t in range(2):
                            ins = dve.tensor_tensor(
                                res[u][:, 2 * n + t, :].rearrange("p (n c) -> p n c", n=heads),
                                back_ps[n][:, t * C:(t + 1) * C].rearrange("p (n c) -> p n c", n=heads),
                                inv[u][:, 2 * n + t, :].unsqueeze(2).to_broadcast([P, heads, CPH]), ALU.mult)
                        ins.then_inc(divided.sem, 1)
                    dve.wait_ge(divided.sem, divided.at(c))
                    if dot:
                        dve.tensor_tensor(res[u][:], res[u][:], bias[:].unsqueeze(1).to_broadcast([P, TPC, C]), ALU.add
                                          ).then_inc(kept.sem, 1)
                    else:
                        dve.wait_ge(kept.sem, kept.at(c - 1))
                        dve.tensor_scalar(low[:], res[u][:], 0.0, None, ALU.min).then_inc(lowered.sem, 1)
                        dve.wait_ge(elu_e.sem, elu_e.at(c))
                        dve.scalar_tensor_tensor(res[u][:], low[:], -1.0, up[:], ALU.add, ALU.add).then_inc(kept.sem, 1)

                front(0, 0, 0)

                def step(c, u, turn):
                    front(c + 1, (u + 1) % SL, turn + (u + 1) // SL)
                    rear(c, u, turn)
                rounds(dve, NCH - 1, SL, step, peel=1)
                rear(NCH - 1, (NCH - 1) % SL, (NCH - 1) // SL)


def groups(engine, unroll, body, peel=0):
    rounds(engine, NG, unroll, lambda g, u, turn: body(g, u, turn, P, G), peel)
    body(NG, NG % unroll, NG // unroll, TAIL, 1)


def node_rows(table, g, parts, tiles):
    return table[bass.ds(g * (P * G), parts * tiles), :].rearrange("(p j) f -> p j f", j=tiles)


def node_pass(nc, top, k, name, kind, table, ends, sums, default, out, matrix=None, stat_rows=None):
    SL = 3
    use_mm = matrix is not None
    norm = kind != "root"
    PAIRS = G // 2
    with ExitStack() as ctx:
        def sb1(n, shape, dt=F32):
            return ctx.enter_context(nc.sbuf_tensor(f"{name}_{n}", shape, dt))

        def sb(n, shape, dt=F32):
            return [sb1(f"{n}{u}", shape, dt) for u in range(SL)]

        x, g_in, idx = sb("x", [P, G, C]), sb("g", [P, G, C]), sb("idx", [P, G], I32)
        res = sb("res", [P, G, C])
        x_T = sb1("x_T", [P, PAIRS, 2, C])
        pos, neg = sb1("pos", [P, G, C]), sb1("neg", [P, G, C])
        stats, mean_var = sb1("stats", [P, G, 6]), sb1("mean_var", [P, G, 2])
        std, rstd, shift = sb1("std", [P, G]), sb1("rstd", [P, G]), sb1("shift", [P, G])
        part, one_col, zero_col = sb1("part", [P, 2, C]), sb1("one_col", [P, 1]), sb1("zero_col", [P, 1])
        neg_slope = sb1("neg_slope", [P, 1])
        turn_ps = [ctx.enter_context(nc.psum_tensor(f"{name}_turn{n}", [P, 2, C], F32)) for n in range(PAIRS)]
        y_ps = [ctx.enter_context(nc.psum_tensor(f"{name}_y{n}", [P, 2, C], F32)) for n in range(PAIRS)]
        stat_ps = ctx.enter_context(nc.psum_tensor(f"{name}_stat", [P, 2 * C], F32))
        T = lambda n, per=1, lead=0: Tally(nc, f"{name}_{n}", per, lead)
        loaded = [T(f"loaded{u}", 32) for u in range(SL)]
        gathered = [T(f"gathered{u}", 16 * G) for u in range(SL)]
        filled = T("filled", 1)
        turned = T("turned", PAIRS, lead=SL)
        in_T = T("in_T", PAIRS, lead=SL)
        mapped = T("mapped", PAIRS, lead=SL)
        added = T("added", PAIRS, lead=SL)
        split = T("split", 1)
        joined = T("joined", 1, lead=SL)
        ready = T("ready", 1, lead=SL)
        stat_ok = T("stat_ok", 1)
        aggregated = T("aggregated", 1)
        rooted = T("rooted", 1)
        inverted = T("inverted", 2)
        kept = T("kept", 1, lead=SL)
        squared = T("squared", 1)
        reduced = T("reduced", 2, lead=SL)
        totalled = T("totalled", 1, lead=SL)
        total = T("total", 1)
        stored = [T(f"stored{u}", 16) for u in range(SL)]
        s_set = nc.alloc_semaphore(f"{name}_set")
        s_stat = nc.alloc_semaphore(f"{name}_stat_out")
        beat = nc.alloc_semaphore(f"{name}_beat")
        dve_beat = nc.alloc_semaphore(f"{name}_dve_beat")
        npairs = lambda tiles: -(-tiles // 2)
        all_added = lambda tiles: npairs(tiles) if use_mm else PAIRS
        fill_on_act = kind == "hyper"

        def pair_tiles(n, tiles):
            return range(2 * n, min(2 * n + 2, tiles))

        def fill(engine, g, u, turn, parts, tiles):
            engine.wait_ge(ready.sem, ready.at(g - SL))
            src = default[0:parts, :].unsqueeze(1).to_broadcast([parts, tiles, C])
            if fill_on_act:
                engine.copy(g_in[u][0:parts, 0:tiles, :], src).then_inc(filled.sem, 1)
            else:
                engine.tensor_copy(g_in[u][0:parts, 0:tiles, :], src).then_inc(filled.sem, 1)

        AHEAD = SL - 1

        def fill_ahead(engine):
            for g in range(AHEAD):
                fill(engine, g, g % SL, g // SL, P, G)

        def nxt(engine, g, u, turn, parts, tiles):
            if tiles == G:
                fill(engine, g + AHEAD, (u + AHEAD) % SL, None, P, G)

        with nc.Block() as block:
            @block.sync
            def _(sp):
                def group(g, u, turn, parts, tiles):
                    sp.wait_ge(ready.sem, ready.at(g - SL))
                    sp.dma_start(x[u][0:parts, 0:tiles, :], node_rows(table, g, parts, tiles)).then_inc(loaded[u].sem, 16)
                    sp.dma_start(idx[u][0:parts, 0:tiles],
                                 ends[bass.ds(g * (P * G), parts * tiles)].rearrange("(p j) -> p j", j=tiles)
                                 ).then_inc(loaded[u].sem, 16)
                groups(sp, SL, group)

            @block.gpsimd
            def _(pool):
                last = pool.to_reg(EP - 1)

                def group(g, u, turn, parts, tiles):
                    pool.wait_ge(loaded[u].sem, loaded[u].at(turn))
                    pool.wait_ge(filled.sem, filled.at(g))
                    pool.sem_inc(beat, 1)
                    for j in range(tiles):
                        pool.indirect_dma_start(
                            out=g_in[u][0:parts, j, :], out_offset=None, in_=sums,
                            in_offset=bass.IndirectOffsetOnAxis(ap=idx[u][0:parts, j:j + 1], axis=0),
                            bounds_check=last, oob_is_err=False).then_inc(gathered[u].sem, 16)
                groups(pool, SL, group)

            @block.tensor
            def _(pe):
                turned.open(pe)
                mapped.open(pe)
                totalled.open(pe)
                pe.wait_ge(s_set, 1)
                if not norm:
                    pe.matmul(stat_ps[0:1, :], zero_col[:], part[:].rearrange("p s f -> p (s f)"), start=True, stop=False)

                def turn_group(g, u, turn, parts, tiles):
                    pe.wait_ge(loaded[u].sem, loaded[u].at(turn))
                    for n in range(npairs(tiles)):
                        pe.wait_ge(in_T.sem, in_T.at(g - 1, n + 1))
                        for j in pair_tiles(n, tiles):
                            for h in range(H):
                                ins = pe.transpose(turn_ps[n][:, j % 2, h * P:h * P + parts],
                                                   x[u][0:parts, j, h * P:(h + 1) * P], k.ident[0:parts, 0:parts])
                        ins.then_inc(turned.sem, 1)

                def map_group(g, u, turn, parts, tiles):
                    for n in range(npairs(tiles)):
                        pe.wait_ge(added.sem, added.at(g - 1, n + 1))
                        pe.wait_ge(in_T.sem, in_T.at(g, n + 1))
                        for j in pair_tiles(n, tiles):
                            for h in range(H):
                                ins = pe.matmul(y_ps[n][0:parts, j % 2, :], x_T[:, n, j % 2, h * P:h * P + parts],
                                                matrix[:, h, :], start=(h == 0), stop=(h == H - 1))
                        ins.then_inc(mapped.sem, 1)

                def total_group(g, u, turn, parts, tiles):
                    pe.wait_ge(reduced.sem, reduced.at(g))
                    pe.matmul(stat_ps[0:1, :], one_col[0:parts, :], part[0:parts].rearrange("p s f -> p (s f)"),
                              start=False, stop=False).then_inc(totalled.sem, 1)

                def group(g, u, turn, parts, tiles):
                    turn_group(g, u, turn, parts, tiles)
                    map_group(g, u, turn, parts, tiles)
                    if not norm:
                        total_group(g, u, turn, parts, tiles)
                if use_mm:
                    groups(pe, SL, group)
                if not norm:
                    pe.matmul(stat_ps[0:1, :], zero_col[:], part[:].rearrange("p s f -> p (s f)"), start=False, stop=True
                              ).then_inc(total.sem, 1)

            @block.scalar
            def _(act):
                in_T.open(act)
                if norm:
                    kept.open(act)

                def front(g, u, turn, parts, tiles):
                    if use_mm:
                        for n in range(npairs(tiles)):
                            act.wait_ge(mapped.sem, mapped.at(g - 1, n + 1))
                            act.wait_ge(turned.sem, turned.at(g, n + 1))
                            w = len(pair_tiles(n, tiles))
                            if parts == P:
                                act.copy(x_T[:, n, 0:w, :], turn_ps[n][:, 0:w, :]).then_inc(in_T.sem, 1)
                            else:
                                for h in range(H):
                                    ins = act.copy(x_T[:, n, 0, h * P:h * P + parts], turn_ps[n][:, 0, h * P:h * P + parts])
                                ins.then_inc(in_T.sem, 1)
                    if kind == "hyper":
                        act.wait_ge(added.sem, added.at(g, all_added(tiles)))
                        act.wait_ge(joined.sem, joined.at(g - 1))
                        at = (slice(0, parts), slice(0, tiles))
                        act.activation(pos[at], res[u][at], ACT.Relu)
                        act.activation(neg[at], res[u][at], ACT.Relu, scale=-1.0).then_inc(split.sem, 1)
                    if kind == "root":
                        act.wait_ge(added.sem, added.at(g, all_added(tiles)))
                        act.wait_ge(reduced.sem, reduced.at(g - 1))
                        at = (slice(0, parts), slice(0, tiles))
                        act.activation(pos[at], res[u][at], ACT.Square).then_inc(squared.sem, 1)

                def rear(g, u, turn, parts, tiles):
                    if norm:
                        act.wait_ge(aggregated.sem, aggregated.at(g))
                        act.activation(std[0:parts, 0:tiles], mean_var[0:parts, 0:tiles, 1], ACT.Sqrt,
                                       bias=k.eps[0:parts, :]).then_inc(rooted.sem, 1)
                        act.wait_ge(inverted.sem, inverted.at(g))
                        for j in range(tiles):
                            ins = act.activation(res[u][0:parts, j, :], res[u][0:parts, j, :], ACT.Identity,
                                                 bias=shift[0:parts, j:j + 1], scale=rstd[0:parts, j:j + 1])
                        ins.then_inc(kept.sem, 1)
                        act.wait_ge(kept.sem, kept.at(g))
                    else:
                        act.wait_ge(added.sem, added.at(g, all_added(tiles)))
                    act.dma_start(node_rows(out, g, parts, tiles), res[u][0:parts, 0:tiles, :]).then_inc(stored[u].sem, 16)

                def group(g, u, turn, parts, tiles):
                    if fill_on_act:
                        nxt(act, g, u, turn, parts, tiles)
                    front(g, u, turn, parts, tiles)
                    rear(g, u, turn, parts, tiles)
                if fill_on_act:
                    fill_ahead(act)
                groups(act, SL, group, peel=1)
                for u in range(SL):
                    act.wait_ge(stored[u].sem, stored[u].at((NG - u) // SL))

            @block.vector
            def _(dve):
                ready.open(dve)
                added.open(dve)
                reduced.open(dve)
                joined.open(dve)
                dve.memset(part[:], 0.0)
                dve.memset(zero_col[:], 0.0)
                dve.tensor_scalar(neg_slope[:], k.slope[:], -1.0, None, ALU.mult)
                dve.memset(one_col[:], 1.0).then_inc(s_set, 1)
                dve.wait_ge(s_set, 1)

                def group(g, u, turn, parts, tiles):
                    at = (slice(0, parts), slice(0, tiles))
                    if not fill_on_act:
                        nxt(dve, g, u, turn, parts, tiles)
                    dve.wait_ge(gathered[u].sem, tail_gathered(u) if tiles == 1 else gathered[u].at(turn))
                    if later(turn):
                        dve.wait_ge(stored[u].sem, stored[u].at(turn - 1))
                    if use_mm:
                        for n in range(npairs(tiles)):
                            w = len(pair_tiles(n, tiles))
                            dve.wait_ge(mapped.sem, mapped.at(g, n + 1))
                            ins = dve.tensor_tensor(res[u][0:parts, 2 * n:2 * n + w, :], y_ps[n][0:parts, 0:w, :],
                                                    g_in[u][0:parts, 2 * n:2 * n + w, :], ALU.add).then_inc(added.sem, 1)
                    else:
                        dve.wait_ge(loaded[u].sem, loaded[u].at(turn))
                        dve.tensor_tensor(res[u][at], g_in[u][at], x[u][at], ALU.add).then_inc(added.sem, PAIRS)
                    dve.wait_ge(added.sem, added.at(g, all_added(tiles)))
                    if kind == "hyper":
                        dve.wait_ge(split.sem, split.at(g))
                        dve.scalar_tensor_tensor(res[u][at], neg[at], neg_slope[0:parts, 0:1], pos[at], ALU.mult, ALU.add
                                                 ).then_inc(joined.sem, 1)
                        dve.wait_ge(joined.sem, joined.at(g))
                        dve.tensor_tensor(res[u][at], res[u][at], x[u][at], ALU.add).then_inc(ready.sem, 1)
                    if norm:
                        if kind == "hyper":
                            dve.wait_ge(ready.sem, ready.at(g))
                        for j in range(tiles):
                            ins = dve.bn_stats(stats[0:parts, j, :], res[u][0:parts, j, :])
                        if kind == "hyper":
                            ins.then_inc(stat_ok.sem, 1)
                        else:
                            ins.then_inc(ready.sem, 1)
                        if kind == "hyper":
                            dve.wait_ge(stat_ok.sem, stat_ok.at(g))
                        else:
                            dve.wait_ge(ready.sem, ready.at(g))
                        dve.sem_inc(dve_beat, 1)
                        for j in range(tiles):
                            ins = dve.bn_aggr(mean_var[0:parts, j, :], stats[0:parts, j, :])
                        ins.then_inc(aggregated.sem, 1)
                        dve.wait_ge(rooted.sem, rooted.at(g))
                        dve.wait_ge(kept.sem, kept.at(g - 1))
                        dve.reciprocal(rstd[0:parts, 0:tiles], std[0:parts, 0:tiles]).then_inc(inverted.sem, 1)
                        dve.wait_ge(inverted.sem, inverted.at(g, 1))
                        dve.scalar_tensor_tensor(shift[0:parts, 0:tiles], mean_var[0:parts, 0:tiles, 0], -1.0,
                                                 rstd[0:parts, 0:tiles], ALU.mult, ALU.mult).then_inc(inverted.sem, 1)
                    else:
                        dve.wait_ge(totalled.sem, totalled.at(g - 1))
                        dve.tensor_reduce(part[0:parts, 0, :], res[u][at].rearrange("p j f -> p f j"), mybir.AxisListType.X,
                                          ALU.add).then_inc(ready.sem, 1)
                        dve.wait_ge(squared.sem, squared.at(g))
                        dve.tensor_reduce(part[0:parts, 1, :], pos[at].rearrange("p j f -> p f j"), mybir.AxisListType.X,
                                          ALU.add).then_inc(reduced.sem, 2)

                def tail_gathered(u):
                    return gathered[u].at(NG // SL, 16)
                if not fill_on_act:
                    fill_ahead(dve)
                groups(dve, SL, group, peel=1)
                if not norm:
                    dve.wait_ge(total.sem, 1)
                    dve.tensor_copy(stat_rows[:], stat_ps[0:1, :].rearrange("p (s f) -> p s f", s=2))


def final_pass(nc, top, k, table, rooted_rows, stat_rows, gamma, beta, out):
    SL = 3
    name = "final"
    with ExitStack() as ctx:
        def sb1(n, shape, dt=F32):
            return ctx.enter_context(nc.sbuf_tensor(f"{name}_{n}", shape, dt))

        def sb(n, shape, dt=F32):
            return [sb1(f"{n}{u}", shape, dt) for u in range(SL)]

        x, y, res = sb("x", [P, G, C]), sb("y", [P, G, C]), sb("res", [P, G, C])
        stats, mean_var = sb1("stats", [P, G, 6]), sb1("mean_var", [P, G, 2])
        std, rstd, shift = sb1("std", [P, G]), sb1("rstd", [P, G]), sb1("shift", [P, G])
        gb = sb1("gamma_beta", [1, 2, C])
        mom = sb1("moments", [1, 2, C])
        sq, bn_var, bn_std, bn_inv, fac, mf = (sb1(n, [1, C]) for n in ("mean_sq", "bn_var", "bn_std", "bn_inv", "fac", "mf"))
        coef = sb1("coef", [1, 2, C])
        coefs = sb1("coefs", [P, 2, C])
        ones_row = sb1("ones_row", [1, P])
        ps = ctx.enter_context(nc.psum_tensor(f"{name}_ps", [P, 2, C], F32))
        T = lambda n, per=1, lead=0: Tally(nc, f"{name}_{n}", per, lead)
        s_in, s_prep, s_root, s_ps = (nc.alloc_semaphore(f"{name}_{n}") for n in ("in", "prep", "root", "ps"))
        s_co = nc.alloc_semaphore(f"{name}_co")
        dve_beat = nc.alloc_semaphore(f"{name}_dve_beat")
        loaded = [T(f"loaded{u}", 32) for u in range(SL)]
        scaled, shifted = T("scaled"), T("shifted")
        once, twice = T("once", lead=0), T("twice", lead=SL)
        stat_ok, aggregated, rooted = T("stat_ok"), T("aggregated"), T("rooted")
        inverted, kept = T("inverted", 2), T("kept", 1, lead=SL)
        stored = [T(f"stored{u}", 16) for u in range(SL)]
        with nc.Block() as block:
            @block.sync
            def _(sp):
                sp.dma_start(gb[:, 0, :], gamma.rearrange("(o f) -> o f", o=1)).then_inc(s_in, 16)
                sp.dma_start(gb[:, 1, :], beta.rearrange("(o f) -> o f", o=1)).then_inc(s_in, 16)

                def group(g, u, turn, parts, tiles):
                    sp.wait_ge(twice.sem, twice.at(g - SL))
                    for t, to in ((table, x), (rooted_rows, y)):
                        sp.dma_start(to[u][0:parts, 0:tiles, :], node_rows(t, g, parts, tiles)).then_inc(loaded[u].sem, 16)
                groups(sp, SL, group)

            @block.tensor
            def _(pe):
                pe.wait_ge(s_prep, 8)
                pe.matmul(ps[:].rearrange("p s f -> p (s f)"), ones_row[:], coef[:].rearrange("p s f -> p (s f)"),
                          start=True, stop=True).then_inc(s_ps, 1)

            @block.gpsimd
            def _(pool):
                pool.wait_ge(s_co, 1)

                def group(g, u, turn, parts, tiles):
                    at = (slice(0, parts), slice(0, tiles))
                    pool.wait_ge(loaded[u].sem, loaded[u].at(turn))
                    pool.tensor_tensor(y[u][at], y[u][at], coefs[0:parts, 0, :].unsqueeze(1).to_broadcast([parts, tiles, C]),
                                       ALU.mult).then_inc(scaled.sem, 1)
                    pool.wait_ge(scaled.sem, scaled.at(g))
                    pool.tensor_tensor(y[u][at], y[u][at], coefs[0:parts, 1, :].unsqueeze(1).to_broadcast([parts, tiles, C]),
                                       ALU.add).then_inc(shifted.sem, 1)
                groups(pool, SL, group)

            @block.vector
            def _(dve):
                twice.open(dve)
                dve.memset(ones_row[:], 1.0)
                dve.tensor_scalar(mom[:], stat_rows[:], 1.0 / N, None, ALU.mult).then_inc(s_prep, 1)
                dve.wait_ge(s_prep, 1)
                dve.tensor_tensor(sq[:], mom[:, 0, :], mom[:, 0, :], ALU.mult).then_inc(s_prep, 1)
                dve.wait_ge(s_prep, 2)
                dve.tensor_tensor(bn_var[:], mom[:, 1, :], sq[:], ALU.subtract).then_inc(s_prep, 1)
                dve.wait_ge(s_root, 1)
                dve.reciprocal(bn_inv[:], bn_std[:]).then_inc(s_prep, 1)
                dve.wait_ge(s_prep, 4)
                dve.wait_ge(s_in, 32)
                dve.tensor_tensor(coef[:, 0, :], bn_inv[:], gb[:, 0, :], ALU.mult).then_inc(s_prep, 1)
                dve.wait_ge(s_prep, 5)
                dve.tensor_tensor(mf[:], mom[:, 0, :], coef[:, 0, :], ALU.mult).then_inc(s_prep, 1)
                dve.wait_ge(s_prep, 6)
                dve.tensor_tensor(coef[:, 1, :], gb[:, 1, :], mf[:], ALU.subtract).then_inc(s_prep, 2)
                dve.wait_ge(s_ps, 1)
                dve.tensor_copy(coefs[:], ps[:]).then_inc(s_co, 1)

                def group(g, u, turn, parts, tiles):
                    at = (slice(0, parts), slice(0, tiles))
                    dve.wait_ge(shifted.sem, shifted.at(g))
                    if later(turn):
                        dve.wait_ge(stored[u].sem, stored[u].at(turn - 1))
                    dve.scalar_tensor_tensor(res[u][at], y[u][at], 0.0, x[u][at], ALU.max, ALU.add).then_inc(once.sem, 1)
                    dve.wait_ge(once.sem, once.at(g))
                    dve.scalar_tensor_tensor(res[u][at], res[u][at], 0.0, x[u][at], ALU.max, ALU.add).then_inc(twice.sem, 1)
                    dve.wait_ge(twice.sem, twice.at(g))
                    for j in range(tiles):
                        ins = dve.bn_stats(stats[0:parts, j, :], res[u][0:parts, j, :])
                    ins.then_inc(stat_ok.sem, 1)
                    dve.wait_ge(stat_ok.sem, stat_ok.at(g))
                    dve.sem_inc(dve_beat, 1)
                    for j in range(tiles):
                        ins = dve.bn_aggr(mean_var[0:parts, j, :], stats[0:parts, j, :])
                    ins.then_inc(aggregated.sem, 1)
                    dve.wait_ge(rooted.sem, rooted.at(g))
                    dve.wait_ge(kept.sem, kept.at(g - 1))
                    dve.reciprocal(rstd[0:parts, 0:tiles], std[0:parts, 0:tiles]).then_inc(inverted.sem, 1)
                    dve.wait_ge(inverted.sem, inverted.at(g, 1))
                    dve.scalar_tensor_tensor(shift[0:parts, 0:tiles], mean_var[0:parts, 0:tiles, 0], -1.0,
                                             rstd[0:parts, 0:tiles], ALU.mult, ALU.mult).then_inc(inverted.sem, 1)
                groups(dve, SL, group, peel=1)

            @block.scalar
            def _(act):
                kept.open(act)
                act.wait_ge(s_prep, 3)
                act.activation(bn_std[:], bn_var[:], ACT.Sqrt, bias=k.eps[0:1, :]).then_inc(s_root, 1)

                def group(g, u, turn, parts, tiles):
                    act.wait_ge(aggregated.sem, aggregated.at(g))
                    act.activation(std[0:parts, 0:tiles], mean_var[0:parts, 0:tiles, 1], ACT.Sqrt,
                                   bias=k.eps[0:parts, :]).then_inc(rooted.sem, 1)
                    act.wait_ge(inverted.sem, inverted.at(g))
                    for j in range(tiles):
                        ins = act.activation(res[u][0:parts, j, :], res[u][0:parts, j, :], ACT.Identity,
                                             bias=shift[0:parts, j:j + 1], scale=rstd[0:parts, j:j + 1])
                    ins.then_inc(kept.sem, 1)
                    act.wait_ge(kept.sem, kept.at(g))
                    act.dma_start(node_rows(out, g, parts, tiles), res[u][0:parts, 0:tiles, :]).then_inc(stored[u].sem, 16)
                groups(act, SL, group)
                for u in range(SL):
                    act.wait_ge(stored[u].sem, stored[u].at((NG - u) // SL))


def graph_layers(nc, x, src, dst, edge_weight, w, out):
    class Kept:
        pass

    k = Kept()
    nodes = [nc.dram_tensor(f"nodes{n}", (N, C), F32, kind="Internal").ap() for n in (1, 2, 3)]
    rooted = nc.dram_tensor("rooted", (N, C), F32, kind="Internal").ap()
    sums = [nc.dram_tensor(f"sums{n}", (EP, C), F32, kind="Internal").ap() for n in range(7)]
    with ExitStack() as top:
        with stage(nc):
            constants(nc, top, k)
        with ExitStack() as sorting:
            with stage(nc):
                key_columns(nc, top, sorting, k, src, dst, edge_weight)
            with stage(nc):
                sort_edges(nc, top, k)
        with stage(nc):
            position_columns(nc, top, k)
        with stage(nc):
            load_weights(nc, top, k, w)
        end = k.node_end
        with stage(nc):
            attention_pass(nc, top, k, "att0", 8, x, "other", x, sums[0], True, 32 ** -0.5, bias=k.row["bs"])
        with stage(nc):
            node_pass(nc, top, k, "node0", "attention", x, end["dst"], sums[0], k.row["bs"], nodes[0], matrix=k.w["Ws"])
        with stage(nc):
            sum_pass(nc, top, k, "hyp1", "dst", nodes[0], "other", sums[1], matrix=k.w["W1"], scaled=True)
        with stage(nc):
            sum_pass(nc, top, k, "hyp2", "src", sums[1], "other_end", sums[2], scaled=True, bias=k.row["b1"], prelu=True)
        with stage(nc):
            sum_pass(nc, top, k, "hyp3", "dst", sums[2], "other_end", sums[3], matrix=k.w["W2"], scaled=True)
        with stage(nc):
            sum_pass(nc, top, k, "hyp4", "src", sums[3], "other_end", sums[4], scaled=True, bias=k.row["b2"])
        with stage(nc):
            node_pass(nc, top, k, "node1", "hyper", nodes[0], end["src"], sums[4], k.row["b2"], nodes[1])
        with stage(nc):
            attention_pass(nc, top, k, "att2", 4, nodes[1], "other", nodes[1], sums[5], False, 1.0)
        with stage(nc):
            node_pass(nc, top, k, "node2", "plain", nodes[1], end["dst"], sums[5], k.row["zero"], nodes[2])
        with stage(nc):
            sum_pass(nc, top, k, "rel3", "dst", nodes[2], "other", sums[6], matrix=k.wT["W_rel"], weighted=True,
                     bias=k.row["b_rel"])
        with ExitStack() as last:
            stat_rows = last.enter_context(nc.sbuf_tensor("stat_rows", [1, 2, C], F32))
            with stage(nc):
                node_pass(nc, top, k, "node3", "root", nodes[2], end["dst"], sums[6], k.row["b_rel"], rooted,
                          matrix=k.wT["W_root"], stat_rows=stat_rows)
            with stage(nc):
                final_pass(nc, top, k, nodes[2], rooted, stat_rows, w["gamma"], w["beta"], out)


_INS = ["x", "src", "dst", "edge_weight", "L0_gnn_Wq", "L0_gnn_bq", "L0_gnn_Wk", "L0_gnn_bk", "L0_gnn_Wv", "L0_gnn_bv",
        "L0_gnn_Ws", "L0_gnn_bs", "L1_gnn_W1", "L1_gnn_b1", "L1_gnn_W2", "L1_gnn_b2", "L1_gnn_a", "L2_gnn_W",
        "L2_gnn_att", "L3_gnn_W_rel", "L3_gnn_b_rel", "L3_gnn_W_root", "L3_gnn_gamma", "L3_gnn_beta"]


def kernel(**inputs):
    import numpy as _np
    import concourse.bacc as _bacc
    from concourse import mybir as _mybir
    from concourse.bass_utils import run_bass_kernel_spmd as _run

    nc = _bacc.Bacc("TRN2", target_bir_lowering=False, num_devices=1)
    arrays, args = {}, {}
    for name in _INS:
        a = _np.ascontiguousarray(inputs[name])
        arrays[f"in_{name}_dram"] = a
        args[name] = nc.dram_tensor(f"in_{name}_dram", a.shape, _mybir.dt.from_np(a.dtype), kind="ExternalInput").ap()
    out = nc.dram_tensor("out_0_dram", (N, C), F32, kind="ExternalOutput").ap()
    weights = {n.split("_gnn_")[1]: a for n, a in args.items() if "_gnn_" in n}
    graph_layers(nc, args["x"], args["src"], args["dst"], args["edge_weight"], weights, out)
    r = _run(nc, [arrays], core_ids=[0])
    return r.results[0]["out_0_dram"]
```

```python
from contextlib import ExitStack, contextmanager

import concourse.bass as bass
from concourse import mybir

ALU = mybir.AluOpType
ACT = mybir.ActivationFunctionType
F32 = mybir.dt.float32
BF16 = mybir.dt.bfloat16
FP16 = mybir.dt.float16
I32 = mybir.dt.int32

P = 128
N = 50000
E = 25000
C = 256
H = C // P
CH = 512
TPC = CH // P
NCH = -(-E // CH)
EP = NCH * CH
NT = EP // P
KR = NT // 2
HI = -(-(N + 1) // P)
G = 6
NG = N // (P * G)
TAIL = N - NG * P * G
SKIP = float(1 << 20)
BIG = 1e30
EPS = 1e-5
REC = 4
META = 5 * TPC


class Tally:

    def __init__(self, nc, name, per=1, lead=0):
        self.sem = nc.alloc_semaphore(name)
        self.per = per
        self.lead = lead

    def open(self, engine):
        engine.sem_inc(self.sem, self.lead * self.per)

    def at(self, rnd, step=None):
        return (rnd + self.lead) * self.per + (self.per if step is None else step)

    def free(self, rnd):
        return rnd * self.per + self.per


@contextmanager
def stage(nc):
    before = nc.snapshot_sems()
    yield
    nc.clear_and_free_semaphores(nc.allocated_since(before))
    nc.all_engine_barrier()


def rounds(engine, count, unroll, body, peel=0):
    for turn in range(peel):
        for u in range(unroll):
            body(turn * unroll + u, u, turn)
    if count // unroll > peel:
        with engine.Fori(peel, count // unroll) as i:
            for u in range(unroll):
                body(i * unroll + u, u, i)
    for u in range(count % unroll):
        body(count // unroll * unroll + u, u, count // unroll)


def later(turn, than=0):
    return not isinstance(turn, int) or turn > than


def constants(nc, top, k):
    k.ident = top.enter_context(nc.sbuf_tensor("ident", [P, P], F32))
    k.ident_bf = top.enter_context(nc.sbuf_tensor("ident_bf", [P, P], BF16))
    k.eps = top.enter_context(nc.sbuf_tensor("eps", [P, 1], F32))
    zeroed = nc.alloc_semaphore("ident_zeroed")
    made = nc.alloc_semaphore("ident_made")
    with nc.Block() as block:
        @block.gpsimd
        def _(pool):
            pool.memset(k.eps[:], EPS)
            pool.memset(k.ident[:], 0.0).then_inc(zeroed, 1)
            pool.wait_ge(zeroed, 1)
            pool.affine_select(out=k.ident[:], in_=k.ident[:], compare_op=ALU.not_equal, fill=1.0, base=0,
                               pattern=[[-1, P]], channel_multiplier=1).then_inc(made, 1)
            pool.wait_ge(made, 1)
            pool.tensor_copy(k.ident_bf[:], k.ident[:])


def key_columns(nc, top, ctx_sort, k, src, dst, edge_weight):
    k.edge = {f: ctx_sort.enter_context(nc.sbuf_tensor(f"edge_{f}", [P, NT, 3], F32)) for f in ("src", "dst")}
    k.cols = {f: ctx_sort.enter_context(nc.sbuf_tensor(f"col_{f}", [P, NT], F32))
              for f in ("src_hi", "src_lo", "dst_hi", "dst_lo")}
    TURN = (("src", (k.edge["src"][:, :, 0], k.edge["dst"][:, :, 1])),
            ("dst", (k.edge["dst"][:, :, 0], k.edge["src"][:, :, 1])),
            ("w", (k.edge["src"][:, :, 2], k.edge["dst"][:, :, 2])),
            *((f, (k.cols[f][:],)) for f in k.cols))
    k.key_rows = {f: nc.dram_tensor(f"keys_{f}", (EP,), F32, kind="Internal").ap() for f in ("src", "dst")}
    full = E // (2 * P)
    rest = E - full * 2 * P
    with ExitStack() as ctx:
        raw = {f: ctx.enter_context(nc.sbuf_tensor(f"raw_{f}", [KR, 2 * P], I32)) for f in ("src", "dst")}
        part = {f: ctx.enter_context(nc.sbuf_tensor(f"part_{f}", [KR, 2 * P], I32))
                for f in ("src_hi", "src_lo", "dst_hi", "dst_lo")}
        rows = {f: ctx.enter_context(nc.sbuf_tensor(f"row_{f}", [KR, 2 * P], F32)) for f, _ in TURN}
        ps = ctx.enter_context(nc.psum_tensor("keys_T", [P, 2, 4, P], F32))
        s_padded = nc.alloc_semaphore("keys_padded")
        s_loaded = nc.alloc_semaphore("keys_loaded")
        s_parts = nc.alloc_semaphore("keys_parts")
        s_float = nc.alloc_semaphore("keys_float")
        s_turned = nc.alloc_semaphore("keys_turned")
        s_kept = nc.alloc_semaphore("keys_kept")
        s_stored = nc.alloc_semaphore("keys_stored")
        with nc.Block() as block:
            @block.sync
            def _(sp):
                sp.wait_ge(s_padded, 3)
                for tile, ap in ((raw["src"], src), (raw["dst"], dst), (rows["w"], edge_weight)):
                    sp.dma_start(tile[0:full, :], ap[0:full * 2 * P].rearrange("(r c) -> r c", c=2 * P)
                                 ).then_inc(s_loaded, 16)
                    sp.dma_start(tile[full:full + 1, 0:rest], ap[full * 2 * P:E].rearrange("(r c) -> r c", r=1)
                                 ).then_inc(s_loaded, 16)
                sp.wait_ge(s_float, 6)
                for f in ("src", "dst"):
                    sp.dma_start(k.key_rows[f].rearrange("(r c) -> r c", c=2 * P), rows[f][:]).then_inc(s_stored, 16)
                sp.wait_ge(s_stored, 32)

            @block.vector
            def _(dve):
                dve.memset(raw["src"][:], N).then_inc(s_padded, 1)
                dve.memset(raw["dst"][:], N).then_inc(s_padded, 1)
                dve.memset(rows["w"][:], 0.0).then_inc(s_padded, 1)
                dve.wait_ge(s_loaded, 6 * 16)
                for f in ("src", "dst"):
                    dve.tensor_scalar(part[f + "_hi"][:], raw[f][:], 7, None, ALU.arith_shift_right).then_inc(s_parts, 1)
                    dve.tensor_scalar(part[f + "_lo"][:], raw[f][:], P - 1, None, ALU.bitwise_and).then_inc(s_parts, 1)
                dve.wait_ge(s_parts, 4)
                for f in ("src", "dst"):
                    dve.tensor_copy(rows[f][:], raw[f][:]).then_inc(s_float, 1)
                    dve.tensor_copy(rows[f + "_hi"][:], part[f + "_hi"][:]).then_inc(s_float, 1)
                    dve.tensor_copy(rows[f + "_lo"][:], part[f + "_lo"][:]).then_inc(s_float, 1)
                for n, (f, outs) in enumerate(TURN):
                    dve.wait_ge(s_turned, n + 1)
                    for c in range(2):
                        for out in outs:
                            ins = dve.tensor_copy(out[:, c:NT:2], ps[:, n % 2, c, 0:KR])
                    ins.then_inc(s_kept, 1)

            @block.tensor
            def _(pe):
                pe.wait_ge(s_float, 6)
                for n, (f, _) in enumerate(TURN):
                    if n >= 2:
                        pe.wait_ge(s_kept, n - 1)
                    for c in range(2):
                        ins = pe.transpose(ps[:, n % 2, c, 0:KR], rows[f][:, c * P:(c + 1) * P], k.ident[0:KR, 0:KR])
                    ins.then_inc(s_turned, 1)


def sort_edges(nc, top, k):
    KEYS = ("dst", "src")
    k.records = {f: nc.dram_tensor(f"records_{f}", (EP + 1, REC), F32, kind="Internal").ap() for f in KEYS}
    k.node_end = {f: nc.dram_tensor(f"node_end_{f}", (HI * P,), I32, kind="Internal").ap() for f in KEYS}
    with ExitStack() as ctx:
        def sb(name, shape, dt):
            return ctx.enter_context(nc.sbuf_tensor(name, shape, dt))

        iota_hi32, iota_lo32 = sb("iota_hi32", [P, HI], I32), sb("iota_lo32", [P, P], I32)
        iota_hi, iota_lo = sb("iota_hi", [P, HI], FP16), sb("iota_lo", [P, P], FP16)
        zero_bf = sb("zero_bf", [P, HI], BF16)
        ones = sb("ones", [P, P], F32)
        upto = sb("upto", [P, P], F32)
        below = sb("below", [P, P], F32)
        first = sb("first", [1, REC], F32)
        cnt = {f: sb(f"cnt_{f}", [P, HI], F32) for f in KEYS}
        incl = {f: sb(f"incl_{f}", [P, HI], F32) for f in KEYS}
        start = {f: sb(f"start_{f}", [P, HI], F32) for f in KEYS}
        end = {f: sb(f"end_{f}", [P, HI], F32) for f in KEYS}
        end_hi = {f: sb(f"end_hi_{f}", [P, HI], BF16) for f in KEYS}
        end_lo = {f: sb(f"end_lo_{f}", [P, HI], BF16) for f in KEYS}
        none = {f: sb(f"none_{f}", [P, HI], F32) for f in KEYS}
        node = {f: sb(f"node_{f}", [P, HI], F32) for f in KEYS}
        node_i = {f: sb(f"node_i_{f}", [P, 4, P], I32) for f in KEYS}
        tot = {f: sb(f"tot_{f}", [1, HI], F32) for f in KEYS}
        run = {f: sb(f"run_{f}", [1, HI], F32) for f in KEYS}
        offs = {f: sb(f"offs_{f}", [1, HI], F32) for f in KEYS}
        ones_row = sb("ones_row", [1, HI], F32)
        s_mk = [nc.alloc_semaphore(f"sort_const{n}") for n in range(3)]

        with nc.Block() as block:
            @block.gpsimd
            def _(pool):
                pool.iota(iota_hi32[:], pattern=[[1, HI]], base=0, channel_multiplier=0).then_inc(s_mk[0], 1)
                pool.iota(iota_lo32[:], pattern=[[1, P]], base=0, channel_multiplier=0).then_inc(s_mk[0], 1)
                pool.memset(ones[:], 1.0).then_inc(s_mk[0], 1)
                pool.wait_ge(s_mk[0], 3)
                pool.affine_select(out=upto[:], in_=ones[:], compare_op=ALU.is_ge, fill=0.0, base=0,
                                   pattern=[[1, P]], channel_multiplier=-1).then_inc(s_mk[1], 1)
                pool.affine_select(out=below[:], in_=ones[:], compare_op=ALU.is_gt, fill=0.0, base=0,
                                   pattern=[[-1, P]], channel_multiplier=1).then_inc(s_mk[1], 1)

            @block.vector
            def _(dve):
                dve.memset(zero_bf[:], 0.0)
                dve.memset(ones_row[:], 1.0)
                dve.memset(first[:], -1.0).then_inc(s_mk[2], 1)
                dve.wait_ge(s_mk[1], 2)
                dve.tensor_copy(iota_hi[:], iota_hi32[:])
                dve.tensor_copy(iota_lo[:], iota_lo32[:])

        one_hi = [{f: sb(f"one_hi{u}_{f}", [P, HI], BF16) for f in KEYS} for u in range(2)]
        one_lo = [{f: sb(f"one_lo{u}_{f}", [P, P], BF16) for f in KEYS} for u in range(2)]

        with ExitStack() as st:
            hist = {f: st.enter_context(nc.psum_tensor(f"hist_{f}", [P, 512], F32)) for f in KEYS}
            made = Tally(nc, "count_made", 2)
            used = Tally(nc, "count_used", 2, lead=2)
            done = nc.alloc_semaphore("count_done")
            with nc.Block() as block:
                @block.vector
                def _(dve):
                    def tile(t, u, turn):
                        dve.wait_ge(used.sem, used.at(t - 2))
                        for f in KEYS:
                            dve.tensor_scalar(one_hi[u][f][:], iota_hi[:], k.cols[f + "_hi"][:, bass.ds(t, 1)], None,
                                              ALU.is_equal)
                            dve.tensor_scalar(one_lo[u][f][:], iota_lo[:], k.cols[f + "_lo"][:, bass.ds(t, 1)], None,
                                              ALU.is_equal).then_inc(made.sem, 1)
                    rounds(dve, NT, 2, tile)
                    dve.wait_ge(done, 2)
                    for f in KEYS:
                        dve.tensor_copy(cnt[f][:], hist[f][:, 0:HI])

                @block.tensor
                def _(pe):
                    used.open(pe)
                    for f in KEYS:
                        pe.matmul(hist[f][:, 0:HI], zero_bf[:, 0:P], zero_bf[:], start=True, stop=False)

                    def tile(t, u, turn):
                        for n, f in enumerate(KEYS):
                            pe.wait_ge(made.sem, made.at(t, n + 1))
                            pe.matmul(hist[f][:, 0:HI], one_lo[u][f][:], one_hi[u][f][:], start=False, stop=False
                                      ).then_inc(used.sem, 1)
                    rounds(pe, NT, 2, tile)
                    for f in KEYS:
                        pe.matmul(hist[f][:, 0:HI], zero_bf[:, 0:P], zero_bf[:], start=False, stop=True
                                  ).then_inc(done, 1)

        with ExitStack() as st:
            tot_ps = {f: st.enter_context(nc.psum_tensor(f"tot_ps_{f}", [1, 512], F32)) for f in KEYS}
            incl_ps = {f: st.enter_context(nc.psum_tensor(f"incl_ps_{f}", [P, 512], F32)) for f in KEYS}
            turn_ps = {f: st.enter_context(nc.psum_tensor(f"turn_ps_{f}", [P, 4, P], F32)) for f in KEYS}
            summed = nc.alloc_semaphore("pre_summed")
            tot_out = nc.alloc_semaphore("pre_tot")
            ran = nc.alloc_semaphore("pre_ran")
            offs_ok = nc.alloc_semaphore("pre_offs")
            incl_ok = nc.alloc_semaphore("pre_incl")
            copied = nc.alloc_semaphore("pre_copied")
            ended = nc.alloc_semaphore("pre_ended")
            rounded = nc.alloc_semaphore("pre_rounded")
            node_ok = nc.alloc_semaphore("pre_node")
            turned = nc.alloc_semaphore("pre_turned")
            node_int = nc.alloc_semaphore("pre_int")
            stored = nc.alloc_semaphore("pre_stored")
            with nc.Block() as block:
                @block.tensor
                def _(pe):
                    for f in KEYS:
                        pe.matmul(tot_ps[f][:, 0:HI], ones[:, 0:1], cnt[f][:], start=True, stop=True).then_inc(summed, 1)
                    for n, f in enumerate(KEYS):
                        pe.wait_ge(offs_ok, n + 1)
                        pe.matmul(incl_ps[f][:, 0:HI], upto[:], cnt[f][:], start=True, stop=False)
                        pe.matmul(incl_ps[f][:, 0:HI], ones[0:1, :], offs[f][:], start=False, stop=True).then_inc(incl_ok, 1)
                    for n, f in enumerate(KEYS):
                        pe.wait_ge(node_ok, 2 * n + 2)
                        for c in range(4):
                            w = min(P, HI - c * P)
                            ins = pe.transpose(turn_ps[f][0:w, c, :], node[f][:, c * P:c * P + w], k.ident[:])
                        ins.then_inc(turned, 1)

                @block.vector
                def _(dve):
                    for n, f in enumerate(KEYS):
                        dve.wait_ge(summed, n + 1)
                        dve.tensor_copy(tot[f][:], tot_ps[f][:, 0:HI]).then_inc(tot_out, 1)
                        dve.wait_ge(tot_out, n + 1)
                        dve.tensor_tensor_scan(run[f][:], ones_row[:], tot[f][:], 0.0, ALU.mult, ALU.add).then_inc(ran, 1)
                        dve.wait_ge(ran, n + 1)
                        dve.tensor_tensor(offs[f][:], run[f][:], tot[f][:], ALU.subtract).then_inc(offs_ok, 1)
                    for n, f in enumerate(KEYS):
                        dve.wait_ge(incl_ok, n + 1)
                        dve.tensor_copy(incl[f][:], incl_ps[f][:, 0:HI]).then_inc(copied, 1)
                        dve.wait_ge(copied, n + 1)
                        dve.scalar_tensor_tensor(start[f][:], incl[f][:], 1.0, cnt[f][:], ALU.add, ALU.subtract)
                        dve.tensor_scalar(end[f][:], incl[f][:], -1.0, None, ALU.add).then_inc(ended, 1)
                        dve.tensor_scalar(none[f][:], cnt[f][:], 0.0, SKIP, ALU.is_equal, ALU.mult).then_inc(node_ok, 1)
                        dve.wait_ge(ended, n + 1)
                        dve.tensor_copy(end_hi[f][:], end[f][:]).then_inc(rounded, 1)
                        dve.wait_ge(node_ok, 2 * n + 1)
                        dve.tensor_tensor(node[f][:], end[f][:], none[f][:], ALU.add).then_inc(node_ok, 1)
                        dve.wait_ge(rounded, n + 1)
                        dve.tensor_tensor(end_lo[f][:], end[f][:], end_hi[f][:], ALU.subtract)
                    for n, f in enumerate(KEYS):
                        dve.wait_ge(turned, n + 1)
                        dve.tensor_copy(node_i[f][:, 0:3, :], turn_ps[f][:, 0:3, :])
                        w = HI - 3 * P
                        dve.tensor_copy(node_i[f][0:w, 3, :], turn_ps[f][0:w, 3, :]).then_inc(node_int, 1)

                @block.sync
                def _(sp):
                    for n, f in enumerate(KEYS):
                        sp.dma_start(k.records[f][0:1, :], first[:]).then_inc(stored, 16)
                    for n, f in enumerate(KEYS):
                        sp.wait_ge(node_int, n + 1)
                        for c in range(4):
                            w = min(P, HI - c * P)
                            sp.dma_start(k.node_end[f][c * P * P:(c * P + w) * P].rearrange("(h l) -> h l", l=P),
                                         node_i[f][0:w, c, :]).then_inc(stored, 16)
                    sp.wait_ge(stored, 16 * 10)

        with ExitStack() as st:
            def sb2(name, shape, dt):
                return st.enter_context(nc.sbuf_tensor(name, shape, dt))

            OTHER = {"dst": "src", "src": "dst"}
            AHEAD = 4
            key_row = [{f: sb2(f"key_row{u}_{f}", [P, P], F32) for f in KEYS} for u in range(AHEAD)]
            lo_T = [{f: sb2(f"lo_T{u}_{f}", [P, P], F32) for f in KEYS} for u in range(2)]
            lo_Tb = [{f: sb2(f"lo_Tb{u}_{f}", [P, P], BF16) for f in KEYS} for u in range(2)]
            table = [{f: sb2(f"table{u}_{f}", [P, HI], F32) for f in KEYS} for u in range(2)]
            same = {f: sb2(f"same_{f}", [P, P], F32) for f in KEYS}
            junk = {f: [sb2(f"junk{n}_{f}", [P, HI], F32) for n in range(2)] for f in KEYS}
            before = [{f: sb2(f"before{u}_{f}", [P, 1], F32) for f in KEYS} for u in range(2)]
            rank = [{f: sb2(f"rank{u}_{f}", [P, 1], I32) for f in KEYS} for u in range(2)]
            rank_f = [{f: sb2(f"rank_f{u}_{f}", [P, 1], F32) for f in KEYS} for u in range(2)]
            rec = [{f: sb2(f"rec{u}_{f}", [P, REC], F32) for f in KEYS} for u in range(2)]
            count_ps = {f: st.enter_context(nc.psum_tensor(f"count_ps_{f}", [P, 512], F32)) for f in KEYS}
            turn_bf = {f: st.enter_context(nc.psum_tensor(f"turn_bf_{f}", [P, 1024], BF16)) for f in KEYS}
            at_ps = {f: st.enter_context(nc.psum_tensor(f"at_ps_{f}", [P, 512], F32)) for f in KEYS}
            end_ps = {f: st.enter_context(nc.psum_tensor(f"end_ps_{f}", [P, 512], F32)) for f in KEYS}
            row_in = [Tally(nc, f"rank_row_in{u}", 32) for u in range(AHEAD)]
            made = Tally(nc, "rank_made", 2)
            turned = Tally(nc, "rank_turned", 2)
            copied = Tally(nc, "rank_copied", 2)
            looked = Tally(nc, "rank_looked", 2)
            counted = Tally(nc, "rank_counted", 2, lead=2)
            picked = Tally(nc, "rank_picked", 2)
            row_used = Tally(nc, "rank_row_used", 2, lead=AHEAD)
            ranked = Tally(nc, "rank_ranked", 2, lead=2)
            integer = Tally(nc, "rank_integer", 2)
            packed = Tally(nc, "rank_packed", 2)
            sent = [Tally(nc, f"rank_sent{u}", 32) for u in range(2)]
            opened = nc.alloc_semaphore("rank_opened")
            beat = nc.alloc_semaphore("rank_beat")
            with nc.Block() as block:
                @block.sync
                def _(sp):
                    def tile(t, u, turn):
                        sp.wait_ge(row_used.sem, row_used.at(t - AHEAD))
                        for f in KEYS:
                            sp.dma_start(key_row[u][f][:],
                                         k.key_rows[f][bass.ds(t * P, P)].partition_broadcast(P)
                                         ).then_inc(row_in[u].sem, 16)
                    rounds(sp, NT, AHEAD, tile)

                @block.vector
                def _(dve):
                    row_used.open(dve)
                    ranked.open(dve)

                    def make(t, u):
                        dve.wait_ge(counted.sem, counted.at(t - 2))
                        dve.wait_ge(ranked.sem, ranked.at(t - 2))
                        for f in KEYS:
                            dve.tensor_scalar(one_hi[u][f][:], iota_hi[:], k.cols[f + "_hi"][:, bass.ds(t, 1)], None,
                                              ALU.is_equal)
                            dve.tensor_scalar(one_lo[u][f][:], iota_lo[:], k.cols[f + "_lo"][:, bass.ds(t, 1)], None,
                                              ALU.is_equal).then_inc(made.sem, 1)

                    def pick(t, slot, turn):
                        u, rec_turn = slot % 2, turn * 2 + slot // 2
                        dve.wait_ge(row_in[slot].sem, row_in[slot].at(turn))
                        for f in KEYS:
                            dve.scalar_tensor_tensor(same[f][:], key_row[slot][f][:], k.edge[f][:, bass.ds(t, 1), 0],
                                                     below[:], ALU.is_equal, ALU.mult, accum_out=before[u][f][:]
                                                     ).then_inc(row_used.sem, 1)
                        for n, f in enumerate(KEYS):
                            dve.wait_ge(looked.sem, looked.at(t, n + 1))
                            dve.wait_ge(packed.sem, packed.at(t))
                            dve.tensor_tensor_reduce(junk[f][1][:], end_ps[f][:, 0:HI], one_hi[u][f][:], 1.0, 0.0,
                                                     ALU.mult, ALU.add, rec[u][OTHER[f]][:, 3:4]).then_inc(picked.sem, 1)
                            dve.wait_ge(row_used.sem, row_used.at(t, n + 1))
                            dve.tensor_tensor_reduce(junk[f][0][:], at_ps[f][:, 0:HI], one_hi[u][f][:], 1.0,
                                                     before[u][f][:], ALU.mult, ALU.add, rank_f[u][f][:]
                                                     ).then_inc(ranked.sem, 1)

                    dve.wait_ge(opened, 1)
                    make(0, 0)

                    def tile(t, slot, turn):
                        make(t + 1, (slot + 1) % 2)
                        pick(t, slot, turn)
                    rounds(dve, NT - 1, AHEAD, tile)
                    pick(NT - 1, (NT - 1) % AHEAD, (NT - 1) // AHEAD)

                @block.scalar
                def _(act):
                    def records(t, u, turn):
                        if later(turn):
                            act.wait_ge(sent[u].sem, sent[u].at(turn - 1))
                        act.wait_ge(opened, 1)
                        for f in KEYS:
                            act.copy(rec[u][f][:, 0:3], k.edge[f][:, bass.ds(t, 1), :].rearrange("p a w -> p (a w)")
                                     ).then_inc(packed.sem, 1)

                    def tile(t, u, turn):
                        act.wait_ge(counted.sem, counted.at(t - 1))
                        for n, f in enumerate(KEYS):
                            act.copy(table[u][f][:], count_ps[f][:, 0:HI])
                            act.wait_ge(turned.sem, turned.at(t, n + 1))
                            act.copy(lo_T[u][f][:], turn_bf[f][:, 0:P])
                            act.copy(lo_Tb[u][f][:], turn_bf[f][:, 0:P]).then_inc(copied.sem, 1)
                    act.wait_ge(opened, 1)

                    def both(t, u, turn):
                        records(t, u, turn)
                        tile(t + 1, (u + 1) % 2, None)
                    tile(0, 0, 0)
                    rounds(act, NT - 1, 2, both, peel=1)
                    records(NT - 1, (NT - 1) % 2, (NT - 1) // 2)

                @block.tensor
                def _(pe):
                    for f in KEYS:
                        pe.matmul(count_ps[f][:, 0:HI], k.ident[:], start[f][:], start=True, stop=True
                                  ).then_inc(counted.sem, 2)
                    pe.wait_ge(counted.sem, 4)
                    pe.sem_inc(opened, 1)

                    def tile(t, u, turn):
                        for n, f in enumerate(KEYS):
                            pe.wait_ge(made.sem, made.at(t, n + 1))
                            pe.transpose(turn_bf[f][:, 0:P], one_lo[u][f][:], k.ident_bf[:]).then_inc(turned.sem, 1)
                        for n, f in enumerate(KEYS):
                            pe.wait_ge(ranked.sem, ranked.at(t - 1, n + 1))
                            pe.wait_ge(copied.sem, copied.at(t, n + 1))
                            pe.matmul(at_ps[f][:, 0:HI], lo_T[u][f][:], table[u][f][:], start=True, stop=True)
                            pe.matmul(count_ps[f][:, 0:HI], one_lo[u][f][:], one_hi[u][f][:], start=False, stop=True,
                                      skip_group_check=True).then_inc(counted.sem, 1)
                            pe.matmul(end_ps[f][:, 0:HI], lo_Tb[u][f][:], end_hi[f][:], start=True, stop=False)
                            pe.matmul(end_ps[f][:, 0:HI], lo_Tb[u][f][:], end_lo[f][:], start=False, stop=True
                                      ).then_inc(looked.sem, 1)
                    rounds(pe, NT, 2, tile)

                @block.gpsimd
                def _(pool):
                    last = pool.to_reg(EP)

                    def tile(t, u, turn):
                        if later(turn):
                            pool.wait_ge(sent[u].sem, sent[u].at(turn - 1))
                        pool.wait_ge(ranked.sem, ranked.at(t))
                        pool.sem_inc(beat, 1)
                        for f in KEYS:
                            pool.tensor_copy(rank[u][f][:], rank_f[u][f][:]).then_inc(integer.sem, 1)
                        for n, f in enumerate(KEYS):
                            pool.wait_ge(integer.sem, integer.at(t, n + 1))
                            pool.sem_inc(beat, 1)
                            pool.indirect_dma_start(
                                out=k.records[f], out_offset=bass.IndirectOffsetOnAxis(ap=rank[u][f][:, 0:1], axis=0),
                                in_=rec[u][f][:], in_offset=None, bounds_check=last, oob_is_err=False
                            ).then_inc(sent[u].sem, 16)
                    rounds(pool, NT, 2, tile, peel=1)
                    for u in range(2):
                        pool.wait_ge(sent[u].sem, sent[u].at(NT // 2 - 1))


def position_columns(nc, top, k):
    k.keep = {f: nc.dram_tensor(f"keep_{f}", (EP,), BF16, kind="Internal").ap() for f in ("dst", "src")}
    size = {f: nc.dram_tensor(f"size_{f}", (EP,), F32, kind="Internal").ap() for f in ("dst", "src")}
    k.reset = nc.dram_tensor("reset", (EP,), F32, kind="Internal").ap()
    k.meta = {f: nc.dram_tensor(f"meta_{f}", (P, NCH, META), I32, kind="Internal").ap() for f in ("dst", "src")}
    k.META_AT = {"key": 0, "other": TPC, "other_end": 2 * TPC, "inv": 3 * TPC, "weight": 4 * TPC}
    HALF = EP // 2
    with ExitStack() as ctx:
        meta = {f: ctx.enter_context(nc.sbuf_tensor(f"meta_sb_{f}", [P, NCH, META], I32)) for f in k.keep}

        def field(f, what):
            at = k.META_AT[what]
            return meta[f][:, :, at:at + TPC]

        FIELDS = [(f, w, field(f, n)) for f in k.keep for w, n in ((0, "key"), (1, "other"), (3, "other_end"), (2, "weight"))]
        reset = ctx.enter_context(nc.sbuf_tensor("reset_rows", [KR, 2 * P], F32))
        here = {f: ctx.enter_context(nc.sbuf_tensor(f"here_{f}", [KR, 2 * P, REC], F32)) for f in k.keep}
        prev = {f: ctx.enter_context(nc.sbuf_tensor(f"prev_{f}", [KR, 2 * P, REC], F32)) for f in k.keep}
        keep = {f: ctx.enter_context(nc.sbuf_tensor(f"keep_rows_{f}", [KR, 2 * P], BF16)) for f in k.keep}
        fld = [ctx.enter_context(nc.sbuf_tensor(f"field{n}", [KR, 2 * P], F32)) for n in range(len(FIELDS))]
        line = ctx.enter_context(nc.sbuf_tensor("keep_line", [1, HALF], BF16))
        ones = ctx.enter_context(nc.sbuf_tensor("ones_line", [1, HALF], BF16))
        sizes = ctx.enter_context(nc.sbuf_tensor("size_line", [1, HALF], F32))
        size_rows = {f: ctx.enter_context(nc.sbuf_tensor(f"size_rows_{f}", [KR, 2 * P], F32)) for f in k.keep}
        inv_rows = {f: ctx.enter_context(nc.sbuf_tensor(f"inv_rows_{f}", [KR, 2 * P], F32)) for f in k.keep}
        ps = ctx.enter_context(nc.psum_tensor("fields_T", [P, 2, 4, P], F32))
        carry = ctx.enter_context(nc.sbuf_tensor("size_carry", [1, 1], F32))
        TURN = [(fld[n], out) for n, (_, _, out) in enumerate(FIELDS)] + [(inv_rows[f], field(f, "inv")) for f in k.keep]
        s_reset = nc.alloc_semaphore("pos_reset")
        s_meta = nc.alloc_semaphore("pos_meta")
        s_carry = nc.alloc_semaphore("pos_carry")
        s_in = nc.alloc_semaphore("pos_in")
        s_keep = nc.alloc_semaphore("pos_keep")
        s_keep_out = nc.alloc_semaphore("pos_keep_out")
        s_line = nc.alloc_semaphore("pos_line")
        s_sized = nc.alloc_semaphore("pos_sized")
        s_size_out = nc.alloc_semaphore("pos_size_out")
        s_size_in = nc.alloc_semaphore("pos_size_in")
        s_field = nc.alloc_semaphore("pos_field")
        s_turned = nc.alloc_semaphore("pos_turned")
        s_kept = nc.alloc_semaphore("pos_kept")
        s_node = nc.alloc_semaphore("pos_node")
        with nc.Block() as block:
            @block.sync
            def _(sp):
                for f in k.keep:
                    flat = k.records[f].rearrange("r c -> (r c)")
                    sp.dma_start(here[f][:], flat[REC:REC + EP * REC].rearrange("(r c w) -> r c w", c=2 * P, w=REC)
                                 ).then_inc(s_in, 16)
                    sp.dma_start(prev[f][:], flat[0:EP * REC].rearrange("(r c w) -> r c w", c=2 * P, w=REC)
                                 ).then_inc(s_in, 16)
                for n, f in enumerate(k.keep):
                    sp.wait_ge(s_keep, n + 1)
                    sp.dma_start(k.keep[f].rearrange("(r c) -> r c", c=2 * P), keep[f][:]).then_inc(s_keep_out, 16)
                sp.wait_ge(s_keep_out, 32)
                step = 0
                for f in k.keep:
                    for h in range(2):
                        if step:
                            sp.wait_ge(s_sized, step)
                            sp.wait_ge(s_size_out, 16 * step)
                        sp.dma_start(line[:], k.keep[f][h * HALF:(h + 1) * HALF].rearrange("(r c) -> r c", r=1)
                                     ).then_inc(s_line, 16)
                        sp.wait_ge(s_sized, step + 1)
                        sp.dma_start(size[f][h * HALF:(h + 1) * HALF].rearrange("(r c) -> r c", r=1), sizes[:]
                                     ).then_inc(s_size_out, 16)
                        step += 1
                sp.wait_ge(s_size_out, 16 * 4)
                for f in k.keep:
                    sp.dma_start(size_rows[f][:], size[f].rearrange("(r c) -> r c", c=2 * P)).then_inc(s_size_in, 16)
                sp.wait_ge(s_reset, 1)
                sp.dma_start(k.reset.rearrange("(r c) -> r c", c=2 * P), reset[:]).then_inc(s_meta, 16)
                sp.wait_ge(s_kept, len(TURN))
                for f in k.keep:
                    sp.dma_start(k.meta[f], meta[f][:]).then_inc(s_meta, 16)
                sp.wait_ge(s_meta, 48)

            @block.vector
            def _(dve):
                dve.memset(ones[:], 1.0)
                dve.wait_ge(s_in, 64)
                for f in k.keep:
                    dve.tensor_tensor(keep[f][:], here[f][:, :, 0], prev[f][:, :, 0], ALU.is_equal).then_inc(s_keep, 1)
                dve.wait_ge(s_keep, 1)
                dve.tensor_scalar(reset[:], keep["dst"][:], -1.0, BIG, ALU.add, ALU.mult).then_inc(s_reset, 1)
                for n, (f, w, _) in enumerate(FIELDS):
                    if w in (0, 1):
                        dve.tensor_scalar(fld[n][:], here[f][:, :, w], float(N - 1), None, ALU.min).then_inc(s_field, 1)
                    else:
                        dve.tensor_copy(fld[n][:], here[f][:, :, w]).then_inc(s_field, 1)
                step = 0
                for f in k.keep:
                    for h in range(2):
                        dve.wait_ge(s_line, 16 * (step + 1))
                        if h == 1:
                            dve.tensor_copy(carry[:], sizes[:, HALF - 1:HALF]).then_inc(s_carry, 1)
                            dve.wait_ge(s_carry, step // 2 + 1)
                        if step:
                            dve.wait_ge(s_size_out, 16 * step)
                        dve.tensor_tensor_scan(sizes[:], line[:], ones[:], carry[:] if h else 0.0,
                                               ALU.mult, ALU.add).then_inc(s_sized, 1)
                        step += 1
                dve.wait_ge(s_size_in, 32)
                for f in k.keep:
                    dve.reciprocal(inv_rows[f][:], size_rows[f][:]).then_inc(s_field, 1)
                for n, (_, out) in enumerate(TURN):
                    dve.wait_ge(s_turned, n + 1)
                    is_float = n >= len(FIELDS) or FIELDS[n][1] == 2
                    for c in range(2):
                        to = (out.bitcast(F32) if is_float else out).rearrange("p a (b c) -> p a b c", c=2)[:, :, :, c]
                        ins = dve.tensor_copy(to, ps[:, n % 2, c, 0:KR].rearrange("p (a b) -> p a b", b=TPC // 2))
                    ins.then_inc(s_kept, 1)

            @block.tensor
            def _(pe):
                for n, (rows, _) in enumerate(TURN):
                    pe.wait_ge(s_field, n + 1)
                    if n >= 2:
                        pe.wait_ge(s_kept, n - 1)
                    for c in range(2):
                        ins = pe.transpose(ps[:, n % 2, c, 0:KR], rows[:, c * P:(c + 1) * P], k.ident[0:KR, 0:KR])
                    ins.then_inc(s_turned, 1)


def load_weights(nc, top, k, w):
    def sb(name, shape, dt=F32, ctx=top):
        return ctx.enter_context(nc.sbuf_tensor(name, shape, dt))

    PLAIN = ("Wq", "Wk", "Wv", "Ws", "W1", "W2", "W")
    TURNED = ("W", "W_rel", "W_root")
    COLS, ROWS = ("bq", "bk", "bv"), ("bs", "b1", "b2", "b_rel")
    k.w = {f: sb(f"w_{f}", [P, H, C]) for f in PLAIN}
    k.wT = {f: sb(f"wT_{f}", [P, H, C]) for f in TURNED}
    k.col = {f: sb(f"bias_{f}", [P, H]) for f in COLS}
    k.row = {f: sb(f"row_{f}", [P, C]) for f in ROWS}
    k.row["zero"] = sb("row_zero", [P, C])
    k.slope = sb("slope", [P, 1])
    HEADS2 = w["att"].shape[0]
    CPH = C // HEADS2
    k.w_att = sb("w_att", [P, H, 2, HEADS2])
    s_zero = nc.alloc_semaphore("w_zero")
    s_in = nc.alloc_semaphore("w_in")
    s_turned = nc.alloc_semaphore("w_turned")
    s_kept = nc.alloc_semaphore("w_kept")
    with ExitStack() as ctx:
        raw = {f: sb(f"raw_{f}", [P, H, C], ctx=ctx) for f in TURNED if f not in PLAIN}
        att = sb("att_blocks", [P, H, 2, HEADS2], ctx=ctx)
        ps = ctx.enter_context(nc.psum_tensor("w_ps", [P, 4, H, C], F32))
        with nc.Block() as block:
            @block.sync
            def _(sp):
                n = 0
                for f, t in [(f, k.w[f]) for f in PLAIN] + list(raw.items()):
                    sp.dma_start(t[:], w[f].rearrange("(h p) c -> p h c", p=P)).then_inc(s_in, 16)
                    n += 16
                for f in ROWS:
                    sp.dma_start(k.row[f][:], w[f].partition_broadcast(P)).then_inc(s_in, 16)
                    n += 16
                sp.dma_start(k.slope[:], w["a"].partition_broadcast(P)).then_inc(s_in, 16)
                with nc.allow_non_contiguous_dma(reason="columns of a few words"):
                    for f in COLS:
                        sp.dma_start(k.col[f][:], w[f].rearrange("(h p) -> p h", p=P)).then_inc(s_in, 16)
                        n += 16
                    sp.wait_ge(s_zero, 1)
                    for h in range(HEADS2):
                        lo = h * CPH % P
                        for s in range(2):
                            sp.dma_start(att[lo:lo + CPH, h * CPH // P, s, h:h + 1],
                                         w["att"][h, s * CPH:(s + 1) * CPH].rearrange("(c o) -> c o", o=1)
                                         ).then_inc(s_in, 16)
                            n += 16
                sp.wait_ge(s_in, n + 16)

            ALL_IN = 16 * (len(PLAIN) + len(raw) + len(ROWS) + 1 + len(COLS) + 2 * HEADS2)

            @block.tensor
            def _(pe):
                pe.wait_ge(s_in, ALL_IN)
                for n, f in enumerate(TURNED):
                    t = k.w.get(f, raw.get(f))
                    for a in range(H):
                        for b in range(H):
                            ins = pe.transpose(ps[:, n, a, b * P:(b + 1) * P], t[:, b, a * P:(a + 1) * P], k.ident[:])
                    ins.then_inc(s_turned, 1)
                for a in range(H):
                    for b in range(H):
                        ins = pe.matmul(ps[:, 3, a, 0:2 * HEADS2], k.w["W"][:, b, a * P:(a + 1) * P],
                                        att[:, b, :, :].rearrange("p s h -> p (s h)"), start=(b == 0), stop=(b == H - 1))
                ins.then_inc(s_turned, 1)

            @block.vector
            def _(dve):
                dve.memset(k.row["zero"][:], 0.0)
                dve.memset(att[:], 0.0).then_inc(s_zero, 1)
                dve.wait_ge(s_in, ALL_IN)
                for h in range(H):
                    dve.tensor_tensor(k.w["Ws"][:, h, h * P:(h + 1) * P], k.w["Ws"][:, h, h * P:(h + 1) * P], k.ident[:],
                                      ALU.add)
                for n, f in enumerate(TURNED):
                    dve.wait_ge(s_turned, n + 1)
                    dve.tensor_copy(k.wT[f][:], ps[:, n, :, :])
                dve.wait_ge(s_turned, len(TURNED) + 1)
                dve.tensor_copy(k.w_att[:].rearrange("p h s n -> p h (s n)"), ps[:, 3, :, 0:2 * HEADS2])


def sum_pass(nc, top, k, name, order, table, what, out, matrix=None, weighted=False, scaled=False, bias=None,
             prelu=False):
    SL = 6
    WB = 2
    IDX, INV, WGT = k.META_AT[what], k.META_AT["inv"], k.META_AT["weight"]
    with ExitStack() as ctx:
        def sb(n, shape, dt=F32):
            return [ctx.enter_context(nc.sbuf_tensor(f"{name}_{n}{u}", shape, dt)) for u in range(SL)]

        meta, keep, rows = sb("meta", [P, META], I32), sb("keep", [P, CH], BF16), sb("rows", [P, TPC, C])
        acc, res = sb("acc", [P, H, CH]), sb("res", [P, TPC, C])
        neg = ctx.enter_context(nc.sbuf_tensor(f"{name}_neg", [P, TPC, C], F32))
        turn_ps = [ctx.enter_context(nc.psum_tensor(f"{name}_turn{u}", [P, H, CH], F32)) for u in range(WB)]
        row_ps = [ctx.enter_context(nc.psum_tensor(f"{name}_row{u}", [P, TPC, C], F32)) for u in range(WB)]
        loaded = [Tally(nc, f"{name}_loaded{u}", 32) for u in range(SL)]
        gathered = [Tally(nc, f"{name}_gathered{u}", 16 * TPC) for u in range(SL)]
        weighed = Tally(nc, f"{name}_weighed")
        turned = Tally(nc, f"{name}_turned", H, lead=SL)
        summed = Tally(nc, f"{name}_summed", H, lead=SL)
        mapped = Tally(nc, f"{name}_mapped", 2, lead=SL)
        affine = Tally(nc, f"{name}_affine")
        bent = Tally(nc, f"{name}_bent")
        kept = Tally(nc, f"{name}_kept", 1, lead=SL)
        stored = [Tally(nc, f"{name}_stored{u}", 16) for u in range(SL)]
        zeroed = nc.alloc_semaphore(f"{name}_zeroed")
        beat = nc.alloc_semaphore(f"{name}_beat")
        with nc.Block() as block:
            @block.sync
            def _(sp):
                def chunk(c, u, turn):
                    sp.wait_ge(kept.sem, kept.at(c - SL))
                    sp.dma_start(meta[u][:], k.meta[order][:, bass.ds(c, 1), :].rearrange("p a w -> p (a w)")
                                 ).then_inc(loaded[u].sem, 16)
                    sp.dma_start(keep[u][:], k.keep[order][bass.ds(c * CH, CH)].partition_broadcast(P)
                                 ).then_inc(loaded[u].sem, 16)
                rounds(sp, NCH, SL, chunk)

            @block.gpsimd
            def _(pool):
                last = pool.to_reg(table.shape[0] - 1)

                def chunk(c, u, turn):
                    pool.wait_ge(loaded[u].sem, loaded[u].at(turn))
                    pool.wait_ge(turned.sem, turned.at(c - SL))
                    pool.sem_inc(beat, 1)
                    for t in range(TPC):
                        pool.indirect_dma_start(
                            out=rows[u][:, t, :], out_offset=None, in_=table,
                            in_offset=bass.IndirectOffsetOnAxis(ap=meta[u][:, IDX + t:IDX + t + 1], axis=0),
                            bounds_check=last, oob_is_err=False).then_inc(gathered[u].sem, 16)
                rounds(pool, NCH, SL, chunk)

            @block.tensor
            def _(pe):
                turned.open(pe)
                mapped.open(pe)

                def turn_chunk(c, u, turn):
                    if weighted:
                        pe.wait_ge(weighed.sem, weighed.at(c))
                    else:
                        pe.wait_ge(gathered[u].sem, gathered[u].at(turn))
                    pe.wait_ge(summed.sem, summed.at(c - WB))
                    for h in range(H):
                        for t in range(TPC):
                            ins = pe.transpose(turn_ps[u % WB][:, h, t * P:(t + 1) * P],
                                               rows[u][:, t, h * P:(h + 1) * P], k.ident[:])
                        ins.then_inc(turned.sem, 1)

                def map_chunk(c, u):
                    pe.wait_ge(kept.sem, kept.at(c - WB))
                    pe.wait_ge(summed.sem, summed.at(c))
                    for t in range(TPC):
                        at = slice(t * P, (t + 1) * P)
                        for h in range(H):
                            if matrix is None:
                                ins = pe.transpose(row_ps[u % WB][:, t, h * P:(h + 1) * P], acc[u][:, h, at], k.ident[:])
                            else:
                                ins = pe.matmul(row_ps[u % WB][:, t, :], acc[u][:, h, at], matrix[:, h, :],
                                                start=(h == 0), stop=(h == H - 1))
                        if t % 2:
                            ins.then_inc(mapped.sem, 1)

                def turn_next(c, u, turn):
                    turn_chunk(c + 1, (u + 1) % SL, turn + (u + 1) // SL)
                turn_chunk(0, 0, 0)

                def step(c, u, turn):
                    turn_next(c, u, turn)
                    map_chunk(c, u)
                rounds(pe, NCH - 1, SL, step)
                map_chunk(NCH - 1, (NCH - 1) % SL)

            @block.vector
            def _(dve):
                dve.memset(acc[SL - 1][:], 0.0).then_inc(zeroed, 1)
                summed.open(dve)
                dve.wait_ge(zeroed, 1)
                if bias is not None:
                    kept.open(dve)

                def sum_chunk(c, u, turn):
                    dve.wait_ge(loaded[u].sem, loaded[u].at(turn))
                    dve.wait_ge(mapped.sem, mapped.at(c - SL))
                    dve.wait_ge(summed.sem, summed.at(c - 1))
                    for h in range(H):
                        dve.wait_ge(turned.sem, turned.at(c, h + 1))
                        dve.tensor_tensor_scan(acc[u][:, h, :], keep[u][:], turn_ps[u % WB][:, h, :],
                                               acc[(u - 1) % SL][:, h, CH - 1:CH], ALU.mult, ALU.add
                                               ).then_inc(summed.sem, 1)

                def keep_chunk(c, u, turn):
                    if later(turn):
                        dve.wait_ge(stored[u].sem, stored[u].at(turn - 1))
                    for t in range(TPC):
                        if t % 2 == 0:
                            dve.wait_ge(mapped.sem, mapped.at(c, t // 2 + 1))
                        factor = meta[u][:, INV + t:INV + t + 1].bitcast(F32) if scaled else 1.0
                        ins = dve.scalar_tensor_tensor(res[u][:, t, :], row_ps[u % WB][:, t, :], factor, bias[:],
                                                       ALU.mult, ALU.add)
                    if not prelu:
                        ins.then_inc(kept.sem, 1)
                        return
                    ins.then_inc(affine.sem, 1)
                    dve.wait_ge(affine.sem, affine.at(c))
                    dve.wait_ge(kept.sem, kept.at(c - 1))
                    dve.tensor_scalar(neg[:], res[u][:], 0.0, k.slope[:, 0:1], ALU.min, ALU.mult).then_inc(bent.sem, 1)
                    dve.wait_ge(bent.sem, bent.at(c))
                    dve.scalar_tensor_tensor(res[u][:], res[u][:], 0.0, neg[:], ALU.max, ALU.add).then_inc(kept.sem, 1)

                def step(c, u, turn):
                    sum_chunk(c + 1, (u + 1) % SL, turn + (u + 1) // SL)
                    if bias is not None:
                        keep_chunk(c, u, turn)
                sum_chunk(0, 0, 0)
                rounds(dve, NCH - 1, SL, step, peel=1)
                if bias is not None:
                    keep_chunk(NCH - 1, (NCH - 1) % SL, (NCH - 1) // SL)

            @block.scalar
            def _(act):
                if bias is None:
                    kept.open(act)

                def weigh(c, u, turn):
                    act.wait_ge(gathered[u].sem, gathered[u].at(turn))
                    for t in range(TPC):
                        ins = act.activation(rows[u][:, t, :], rows[u][:, t, :], ACT.Copy,
                                             scale=meta[u][:, WGT + t:WGT + t + 1].bitcast(F32))
                    ins.then_inc(weighed.sem, 1)

                def keep_chunk(c, u, turn):
                    if bias is None:
                        if later(turn):
                            act.wait_ge(stored[u].sem, stored[u].at(turn - 1))
                        for t in range(TPC):
                            if t % 2 == 0:
                                act.wait_ge(mapped.sem, mapped.at(c, t // 2 + 1))
                            ins = act.activation(res[u][:, t, :], row_ps[u % WB][:, t, :], ACT.Copy,
                                                 scale=meta[u][:, INV + t:INV + t + 1].bitcast(F32) if scaled else 1.0)
                        ins.then_inc(kept.sem, 1)
                    act.wait_ge(kept.sem, kept.at(c))
                    act.dma_start(out[bass.ds(c * CH, CH), :].rearrange("(t p) f -> p t f", p=P), res[u][:]
                                  ).then_inc(stored[u].sem, 16)

                if not weighted:
                    rounds(act, NCH, SL, keep_chunk, peel=1)
                else:
                    def step(c, u, turn):
                        weigh(c + 2, (u + 2) % SL, turn + (u + 2) // SL)
                        keep_chunk(c, u, turn)
                    weigh(0, 0, 0)
                    weigh(1, 1, 0)
                    rounds(act, NCH - 2, SL, step, peel=1)
                    for c in (NCH - 2, NCH - 1):
                        keep_chunk(c, c % SL, c // SL)
                for u in range(SL):
                    act.wait_ge(stored[u].sem, stored[u].at((NCH - 1 - u) // SL))


def attention_pass(nc, top, k, name, heads, src_table, src_what, dst_table, out, dot, scale, bias=None):
    SL = 2
    CPH = C // heads
    IDX_S, IDX_D = k.META_AT[src_what], k.META_AT["key"]
    ALPHA = 0.2
    NJ = 3
    with ExitStack() as ctx:
        def sb1(n, shape, dt=F32):
            return ctx.enter_context(nc.sbuf_tensor(f"{name}_{n}", shape, dt))

        def sb(n, shape, dt=F32):
            return [sb1(f"{n}{u}", shape, dt) for u in range(SL)]

        def ps(n, shape):
            return ctx.enter_context(nc.psum_tensor(f"{name}_{n}", shape, F32))

        meta, reset = sb("meta", [P, META], I32), sb("reset", [heads, CH])
        src_rows, dst_rows = sb("src_rows", [P, TPC, C]), sb("dst_rows", [P, TPC, C])
        src_T, dst_T = sb("src_T", [P, H, CH]), sb("dst_T", [P, H, CH])
        query, prod = sb1("query", [P, H, CH]), sb1("prod", [P, H, CH])
        value = sb("value", [P, H, CH])
        top_m = sb("max", [heads, CH + 1])
        shifted = sb1("shifted", [heads, CH])
        score = sb1("score", [heads, 2, CH])
        diff, expo = sb("diff", [heads, 2, CH]), sb("expo", [P, 2, CH])
        den = sb("den", [heads, CH])
        part, acc = sb1("part", [P, H, CH]), sb("acc", [P, H, CH])
        inv = sb("inv", [P, TPC, heads])
        res = sb("res", [P, TPC, C])
        low, up = sb1("low", [P, TPC, C]), sb1("up", [P, TPC, C])
        sel, sel_T, ones = sb1("sel", [P, H, heads]), sb1("sel_T", [P, C]), sb1("ones", [P, C])
        turn_ps = ps("turn", [P, H, CH])
        proj_ps = [ps(f"proj{n}", [P, CH]) for n in range(NJ)]
        score_ps = ps("score_ps", [P, CH])
        back_ps = [ps(f"back{n}", [P, CH]) for n in range(2)]
        T = lambda n, per=1, lead=0: Tally(nc, f"{name}_{n}", per, lead)
        loaded = [T(f"loaded{u}", 32) for u in range(SL)]
        got_src = [T(f"got_src{u}", 16 * TPC) for u in range(SL)]
        got_dst = [T(f"got_dst{u}", 16 * TPC) for u in range(SL)]
        turned = T("turned", 2, lead=SL)
        in_T = T("in_T", 2, lead=SL)
        projected = T("projected", 6 if dot else 2)
        proj_out = T("proj_out", 2 * H if dot else H, lead=SL)
        multiplied = T("multiplied", H, lead=SL)
        scored = T("scored", 1, lead=SL)
        maxed = T("maxed", 2, lead=SL)
        shift_ok = T("shift_ok")
        diffed = T("diffed", 2, lead=SL)
        leaky = T("leaky", 2, lead=SL)
        exped = T("exped", 1, lead=SL)
        summed = T("summed", 1, lead=SL)
        spread = T("spread", H, lead=SL)
        parted = T("parted", H, lead=SL)
        ran = T("ran", H, lead=SL)
        den_T = T("den_T", 1, lead=SL)
        inverted = T("inverted", 2, lead=SL)
        back = T("back", 2, lead=SL)
        divided = T("divided", 2, lead=SL)
        kept = T("kept", 1, lead=SL)
        lowered, elu_e = T("lowered", 1, lead=SL), T("elu_e", 1, lead=SL)
        stored = [T(f"stored{u}", 16) for u in range(SL)]
        setup = [nc.alloc_semaphore(f"{name}_setup{n}") for n in range(4)]
        beat = nc.alloc_semaphore(f"{name}_beat")
        pe_beat = nc.alloc_semaphore(f"{name}_pe_beat")
        with nc.Block() as block:
            @block.gpsimd
            def _(pool):
                pool.wait_ge(setup[0], 1)
                pool.affine_select(out=sel[:], in_=ones[:, 0:H * heads].rearrange("p (a b) -> p a b", a=H),
                                   compare_op=ALU.is_ge, fill=0.0, base=0, pattern=[[P, H], [-CPH, heads]],
                                   channel_multiplier=1).then_inc(setup[1], 1)
                pool.affine_select(out=sel_T[:], in_=ones[:], compare_op=ALU.is_ge, fill=0.0, base=0,
                                   pattern=[[1, C]], channel_multiplier=-CPH).then_inc(setup[1], 1)
                pool.wait_ge(setup[1], 2)
                pool.affine_select(out=sel[:], in_=sel[:], compare_op=ALU.is_ge, fill=0.0, base=CPH - 1,
                                   pattern=[[-P, H], [CPH, heads]], channel_multiplier=-1).then_inc(setup[2], 1)
                pool.affine_select(out=sel_T[:], in_=sel_T[:], compare_op=ALU.is_ge, fill=0.0, base=CPH - 1,
                                   pattern=[[-1, C]], channel_multiplier=CPH).then_inc(setup[2], 1)
                last_s = pool.to_reg(src_table.shape[0] - 1)
                last_d = pool.to_reg(dst_table.shape[0] - 1)

                def chunk(c, u, turn):
                    pool.wait_ge(loaded[u].sem, loaded[u].at(turn))
                    pool.wait_ge(turned.sem, turned.at(c - SL))
                    pool.sem_inc(beat, 1)
                    for rows, table, idx, last, got in ((src_rows, src_table, IDX_S, last_s, got_src),
                                                        (dst_rows, dst_table, IDX_D, last_d, got_dst)):
                        for t in range(TPC):
                            pool.indirect_dma_start(
                                out=rows[u][:, t, :], out_offset=None, in_=table,
                                in_offset=bass.IndirectOffsetOnAxis(ap=meta[u][:, idx + t:idx + t + 1], axis=0),
                                bounds_check=last, oob_is_err=False).then_inc(got[u].sem, 16)
                rounds(pool, NCH, SL, chunk)

            @block.sync
            def _(sp):
                def chunk(c, u, turn):
                    sp.wait_ge(turned.sem, turned.at(c - SL))
                    sp.wait_ge(maxed.sem, maxed.at(c - SL))
                    sp.dma_start(meta[u][:], k.meta["dst"][:, bass.ds(c, 1), :].rearrange("p a w -> p (a w)")
                                 ).then_inc(loaded[u].sem, 16)
                    sp.dma_start(reset[u][:], k.reset[bass.ds(c * CH, CH)].partition_broadcast(heads)
                                 ).then_inc(loaded[u].sem, 16)
                rounds(sp, NCH, SL, chunk)

            @block.tensor
            def _(pe):
                for t in (turned, scored, spread, den_T, back):
                    t.open(pe)
                pe.wait_ge(setup[2], 2)

                def project(c, n, weight, half, rhs):
                    for h in range(H):
                        ins = pe.matmul(proj_ps[n % NJ][:], weight[:, h, half * P:(half + 1) * P], rhs[:, h, :],
                                        start=(h == 0), stop=(h == H - 1))
                    ins.then_inc(projected.sem, 1)

                def turn_rows(c, u, turn, n):
                    rows, got = ((src_rows, got_src), (dst_rows, got_dst))[n]
                    pe.wait_ge(got[u].sem, got[u].at(turn))
                    pe.wait_ge(in_T.sem, in_T.at(c - 1 + n, 2 if n == 0 else 1))
                    for h in range(H):
                        for t in range(TPC):
                            ins = pe.transpose(turn_ps[:, h, t * P:(t + 1) * P], rows[u][:, t, h * P:(h + 1) * P],
                                               k.ident[:])
                    ins.then_inc(turned.sem, 1)

                den_ps = proj_ps[0] if dot else proj_ps[2]

                def front_queries_keys(c, u):
                    pe.wait_ge(in_T.sem, in_T.at(c))
                    pe.wait_ge(proj_out.sem, proj_out.at(c - 1))
                    pe.wait_ge(multiplied.sem, multiplied.at(c - 1))
                    pe.wait_ge(inverted.sem, inverted.at(c - 1, 1))
                    project(c, 0, k.w["Wq"], 0, dst_T[u])
                    project(c, 1, k.w["Wk"], 0, src_T[u])
                    project(c, 2, k.w["Wq"], 1, dst_T[u])
                    pe.wait_ge(proj_out.sem, proj_out.at(c, 1))
                    project(c, 3, k.w["Wk"], 1, src_T[u])

                def front_values(c, u, half):
                    if half == 0:
                        pe.wait_ge(multiplied.sem, multiplied.at(c, 1))
                    else:
                        pe.wait_ge(proj_out.sem, proj_out.at(c, 2))
                    project(c, 4 + half, k.w["Wv"], half, src_T[u])

                def front_scores(c, u):
                    pe.wait_ge(diffed.sem, diffed.at(c - 1))
                    if dot:
                        pe.wait_ge(maxed.sem, maxed.at(c - 1, 1))
                        pe.wait_ge(multiplied.sem, multiplied.at(c))
                        for h in range(H):
                            ins = pe.matmul(score_ps[0:heads, :], sel[:, h, :], prod[:, h, :], start=(h == 0), stop=(h == H - 1))
                    else:
                        pe.wait_ge(leaky.sem, leaky.at(c - 1))
                        pe.wait_ge(in_T.sem, in_T.at(c))
                        for n, rhs in enumerate((src_T[u], dst_T[u])):
                            for h in range(H):
                                ins = pe.matmul(score_ps[0:heads, :], k.w_att[:, h, n, :], rhs[:, h, :],
                                                start=(n == 0 and h == 0), stop=(n == 1 and h == H - 1))
                    ins.then_inc(scored.sem, 1)

                def front_end(c, u, rear_step):
                    if dot:
                        front_queries_keys(c, u)
                        rear_step()
                        front_scores(c, u)
                        front_values(c, u, 0)
                        front_values(c, u, 1)
                    else:
                        front_scores(c, u)
                        rear_step()
                        pe.wait_ge(proj_out.sem, proj_out.at(c - 1))
                        project(c, 0, k.wT["W"], 0, src_T[u])
                        project(c, 1, k.wT["W"], 1, src_T[u])

                def spread_half(c, u, h):
                    at = slice(h * P, (h + 1) * P)
                    if h == 0:
                        pe.wait_ge(exped.sem, exped.at(c))
                        pe.wait_ge(divided.sem, divided.at(c - 1))
                    else:
                        pe.wait_ge(parted.sem, parted.at(c, h))
                        pe.wait_ge(ran.sem, ran.at(c, h))
                    pe.matmul(back_ps[0][:], sel_T[:, at], expo[u][:, 1, :], start=True, stop=True)
                    pe.matmul(back_ps[1][:], sel_T[:, at], expo[u][:, 0, :], start=True, stop=True).then_inc(spread.sem, 1)

                def turn_denominators(c, u):
                    pe.wait_ge(summed.sem, summed.at(c))
                    if dot:
                        pe.wait_ge(multiplied.sem, multiplied.at(c))
                    pe.wait_ge(inverted.sem, inverted.at(c - 1, 1))
                    pe.sem_inc(pe_beat, 1)
                    for t in range(TPC):
                        ins = pe.transpose(den_ps[:, t * heads:(t + 1) * heads], den[u][:, t * P:(t + 1) * P],
                                           k.ident[0:heads, 0:heads])
                    ins.then_inc(den_T.sem, 1)

                def turn_back(c, u):
                    pe.wait_ge(parted.sem, parted.at(c))
                    pe.wait_ge(ran.sem, ran.at(c))
                    for t in range(TPC):
                        for h in range(H):
                            ins = pe.transpose(back_ps[t // 2][:, (t % 2) * C + h * P:(t % 2) * C + (h + 1) * P],
                                               acc[u][:, h, t * P:(t + 1) * P], k.ident[:])
                        if t % 2:
                            ins.then_inc(back.sem, 1)

                turn_rows(0, 0, 0, 0)
                turn_rows(0, 0, 0, 1)
                front_end(0, 0, lambda: None)

                def step(c, u, turn):
                    nxt, nxt_turn = (u + 1) % SL, turn + (u + 1) // SL
                    turn_rows(c + 1, nxt, nxt_turn, 0)
                    spread_half(c, u, 0)
                    turn_rows(c + 1, nxt, nxt_turn, 1)
                    turn_denominators(c, u)
                    spread_half(c, u, 1)
                    front_end(c + 1, nxt, lambda: turn_back(c, u))
                rounds(pe, NCH - 1, SL, step)
                c, u = NCH - 1, (NCH - 1) % SL
                spread_half(c, u, 0)
                turn_denominators(c, u)
                spread_half(c, u, 1)
                turn_back(c, u)

            @block.scalar
            def _(act):
                for t in (in_T, proj_out, exped, elu_e, lowered):
                    t.open(act)

                def copy_turned(c, u, n):
                    act.wait_ge(turned.sem, turned.at(c, n + 1))
                    if n == 0:
                        act.wait_ge(scored.sem, scored.at(c - SL))
                        act.wait_ge(projected.sem, projected.at(c - 1))
                    act.copy((src_T, dst_T)[n][u][:], turn_ps[:]).then_inc(in_T.sem, 1)

                def copy_queries(c):
                    if dot:
                        act.wait_ge(multiplied.sem, multiplied.at(c - 1))
                        for h in range(H):
                            act.wait_ge(projected.sem, projected.at(c, 2 * h + 1))
                            act.activation(query[:, h, :], proj_ps[2 * h % NJ][:], ACT.Identity, bias=k.col["bq"][:, h:h + 1]
                                           ).then_inc(proj_out.sem, 1)

                def copy_values(c, u, h):
                    act.wait_ge(parted.sem, parted.at(c - SL))
                    act.wait_ge(projected.sem, projected.at(c, (5 if dot else 1) + h))
                    if dot:
                        act.activation(value[u][:, h, :], proj_ps[(4 + h) % NJ][:], ACT.Identity,
                                       bias=k.col["bv"][:, h:h + 1]).then_inc(proj_out.sem, 1)
                    else:
                        act.copy(value[u][:, h, :], proj_ps[h][:]).then_inc(proj_out.sem, 1)

                def exponentials(c, u):
                    act.wait_ge(diffed.sem, diffed.at(c))
                    act.wait_ge(summed.sem, summed.at(c - SL))
                    act.wait_ge(spread.sem, spread.at(c - SL))
                    act.activation(expo[u][0:heads], diff[u][:], ACT.Exp, scale=scale).then_inc(exped.sem, 1)

                def elu_parts(c, u):
                    act.wait_ge(divided.sem, divided.at(c))
                    act.wait_ge(kept.sem, kept.at(c - 1))
                    act.activation(low[:], res[u][:], ACT.Relu, scale=-1.0).then_inc(lowered.sem, 1)
                    act.activation(up[:], res[u][:], ACT.Relu)
                    act.wait_ge(lowered.sem, lowered.at(c))
                    act.activation(low[:], low[:], ACT.Exp, scale=-1.0).then_inc(elu_e.sem, 1)

                def store(c, u):
                    act.wait_ge(kept.sem, kept.at(c))
                    act.dma_start(out[bass.ds(c * CH, CH), :].rearrange("(t p) f -> p t f", p=P), res[u][:]
                                  ).then_inc(stored[u].sem, 16)

                def front(c, u, rear_elu=None, rear_store=None):
                    copy_turned(c, u, 0)
                    if rear_elu:
                        rear_elu()
                    copy_turned(c, u, 1)
                    copy_queries(c)
                    copy_values(c, u, 0)
                    exponentials(c, u)
                    copy_values(c, u, 1)
                    if rear_store:
                        rear_store()

                front(0, 0)
                if dot:
                    def step(c, u, turn):
                        front(c + 1, (u + 1) % SL, None, lambda: store(c, u))
                    rounds(act, NCH - 1, SL, step)
                    store(NCH - 1, (NCH - 1) % SL)
                else:
                    front(1, 1)

                    def step(c, u, turn):
                        front(c + 2, u, lambda: elu_parts(c, u), lambda: store(c, u))
                    rounds(act, NCH - 2, SL, step)
                    for c in (NCH - 2, NCH - 1):
                        elu_parts(c, c % SL)
                        store(c, c % SL)
                for u in range(SL):
                    act.wait_ge(stored[u].sem, stored[u].at((NCH - 1 - u) // SL))

            @block.vector
            def _(dve):
                dve.memset(ones[:], 1.0).then_inc(setup[0], 1)
                for e in expo:
                    dve.memset(e[:], 0.0)
                for t in (multiplied, maxed, diffed, leaky, summed, parted, ran, inverted, divided, kept):
                    t.open(dve)
                dve.memset(top_m[SL - 1][:], -BIG)
                dve.memset(den[SL - 1][:], 0.0)
                dve.memset(acc[SL - 1][:], 0.0).then_inc(setup[3], 1)
                dve.wait_ge(setup[3], 1)

                def multiply(c, h):
                    if h == 0:
                        dve.wait_ge(scored.sem, scored.at(c - 1))
                    dve.wait_ge(proj_out.sem, proj_out.at(c, h + 1))
                    dve.wait_ge(projected.sem, projected.at(c, 2 * h + 2))
                    dve.scalar_tensor_tensor(prod[:, h, :], proj_ps[(2 * h + 1) % NJ][:], k.col["bk"][:, h:h + 1],
                                             query[:, h, :], ALU.add, ALU.mult).then_inc(multiplied.sem, 1)

                def exponents(c, u, turn):
                    before = (u - 1) % SL
                    dve.wait_ge(scored.sem, scored.at(c))
                    dve.wait_ge(diffed.sem, diffed.at(c - 1))
                    if dot:
                        scores = score_ps[0:heads, :]
                    else:
                        dve.tensor_scalar(score[:, 0, :], score_ps[0:heads, :], ALPHA, None, ALU.mult).then_inc(leaky.sem, 1)
                        dve.wait_ge(leaky.sem, leaky.at(c, 1))
                        dve.tensor_tensor(score[:, 1, :], score[:, 0, :], score_ps[0:heads, :], ALU.max).then_inc(leaky.sem, 1)
                        dve.wait_ge(leaky.sem, leaky.at(c))
                        scores = score[:, 1, :]
                    dve.wait_ge(loaded[u].sem, loaded[u].at(turn))
                    dve.wait_ge(maxed.sem, maxed.at(c - 1))
                    dve.tensor_copy(top_m[u][:, 0:1], top_m[before][:, CH:CH + 1])
                    dve.tensor_tensor_scan(top_m[u][:, 1:CH + 1], reset[u][:], scores, top_m[before][:, CH:CH + 1],
                                           ALU.add, ALU.max).then_inc(maxed.sem, 1)
                    dve.wait_ge(maxed.sem, maxed.at(c, 1))
                    dve.tensor_tensor(shifted[:], top_m[u][:, 0:CH], reset[u][:], ALU.add).then_inc(maxed.sem, 1)
                    dve.wait_ge(exped.sem, exped.at(c - SL))
                    dve.tensor_tensor(diff[u][:, 1, :], scores, top_m[u][:, 1:CH + 1], ALU.subtract).then_inc(diffed.sem, 1)
                    dve.wait_ge(maxed.sem, maxed.at(c))
                    dve.tensor_tensor(diff[u][:, 0, :], shifted[:], top_m[u][:, 1:CH + 1], ALU.subtract
                                      ).then_inc(diffed.sem, 1)

                def denominators(c, u):
                    before = (u - 1) % SL
                    dve.wait_ge(exped.sem, exped.at(c))
                    dve.wait_ge(den_T.sem, den_T.at(c - SL))
                    dve.wait_ge(summed.sem, summed.at(c - 1))
                    dve.tensor_tensor_scan(den[u][:], expo[u][0:heads, 0, :], expo[u][0:heads, 1, :],
                                           den[before][:, CH - 1:CH], ALU.mult, ALU.add).then_inc(summed.sem, 1)

                def invert(c, u):
                    dve.wait_ge(den_T.sem, den_T.at(c))
                    den_ps = (proj_ps[0] if dot else proj_ps[2])[:, 0:TPC * heads].rearrange("p (t n) -> p t n", n=heads)
                    dve.wait_ge(divided.sem, divided.at(c - SL))
                    dve.tensor_scalar(inv[u][:], den_ps, 0.0 if dot else 1e-16, None, ALU.add).then_inc(inverted.sem, 1)
                    dve.wait_ge(inverted.sem, inverted.at(c, 1))
                    dve.reciprocal(inv[u][:], inv[u][:]).then_inc(inverted.sem, 1)

                def numerators(c, u, h):
                    before = (u - 1) % SL
                    if h == 0:
                        dve.wait_ge(proj_out.sem, proj_out.at(c))
                        dve.wait_ge(back.sem, back.at(c - SL))
                        dve.wait_ge(ran.sem, ran.at(c - 1))
                    dve.wait_ge(spread.sem, spread.at(c, h + 1))
                    dve.tensor_tensor(part[:, h, :], back_ps[0][:], value[u][:, h, :], ALU.mult).then_inc(parted.sem, 1)
                    dve.wait_ge(parted.sem, parted.at(c, h + 1))
                    dve.tensor_tensor_scan(acc[u][:, h, :], back_ps[1][:], part[:, h, :], acc[before][:, h, CH - 1:CH],
                                           ALU.mult, ALU.add).then_inc(ran.sem, 1)

                def divide(c, u, turn):
                    dve.wait_ge(inverted.sem, inverted.at(c))
                    if later(turn):
                        dve.wait_ge(stored[u].sem, stored[u].at(turn - 1))
                    for n in range(2):
                        dve.wait_ge(back.sem, back.at(c, n + 1))
                        for t in range(2):
                            ins = dve.tensor_tensor(
                                res[u][:, 2 * n + t, :].rearrange("p (n c) -> p n c", n=heads),
                                back_ps[n][:, t * C:(t + 1) * C].rearrange("p (n c) -> p n c", n=heads),
                                inv[u][:, 2 * n + t, :].unsqueeze(2).to_broadcast([P, heads, CPH]), ALU.mult)
                        ins.then_inc(divided.sem, 1)

                def finish(c, u):
                    if dot:
                        dve.wait_ge(divided.sem, divided.at(c))
                        dve.tensor_tensor(res[u][:], res[u][:], bias[:].unsqueeze(1).to_broadcast([P, TPC, C]), ALU.add
                                          ).then_inc(kept.sem, 1)
                    else:
                        dve.wait_ge(elu_e.sem, elu_e.at(c))
                        dve.scalar_tensor_tensor(res[u][:], low[:], -1.0, up[:], ALU.add, ALU.add).then_inc(kept.sem, 1)

                if dot:
                    multiply(0, 0)
                    multiply(0, 1)
                exponents(0, 0, 0)

                def step(c, u, turn):
                    nxt, nxt_turn = (u + 1) % SL, turn + (u + 1) // SL
                    denominators(c, u)
                    numerators(c, u, 0)
                    invert(c, u)
                    numerators(c, u, 1)
                    if dot:
                        multiply(c + 1, 0)
                        multiply(c + 1, 1)
                    divide(c, u, turn)
                    exponents(c + 1, nxt, nxt_turn)
                    if dot:
                        finish(c, u)
                    elif not isinstance(c, int) or c:
                        finish(c - 1, (u - 1) % SL)
                rounds(dve, NCH - 1, SL, step, peel=1)
                c, u, turn = NCH - 1, (NCH - 1) % SL, (NCH - 1) // SL
                denominators(c, u)
                numerators(c, u, 0)
                invert(c, u)
                numerators(c, u, 1)
                if not dot:
                    finish(c - 1, (u - 1) % SL)
                divide(c, u, turn)
                finish(c, u)


def groups(engine, unroll, body, peel=0):
    rounds(engine, NG, unroll, lambda g, u, turn: body(g, u, turn, P, G), peel)
    body(NG, NG % unroll, NG // unroll, TAIL, 1)


def node_rows(table, g, parts, tiles):
    return table[bass.ds(g * (P * G), parts * tiles), :].rearrange("(p j) f -> p j f", j=tiles)


def node_pass(nc, top, k, name, kind, table, ends, sums, default, out, matrix=None, stat_rows=None):
    SL = 4
    AHEAD = SL - 1
    use_mm = matrix is not None
    norm = kind != "root"
    hyper = kind == "hyper"
    PAIRS = G // 2
    with ExitStack() as ctx:
        def sb1(n, shape, dt=F32):
            return ctx.enter_context(nc.sbuf_tensor(f"{name}_{n}", shape, dt))

        def sb(n, shape, dt=F32, slots=SL):
            return [sb1(f"{n}{u}", shape, dt) for u in range(slots)]

        x, g_in, idx = sb("x", [P, G, C]), sb("g", [P, G, C]), sb("idx", [P, G], I32)
        res = sb("res", [P, G, C])
        x_T = sb("x_T", [P, PAIRS, 2, C], slots=2)
        half = sb("half", [P, G, C], slots=2)
        stats, mean_var = sb1("stats", [P, G, 6]), sb("mean_var", [P, G, 2])
        std, rstd, shift = sb("std", [P, G]), sb("rstd", [P, G]), sb("shift", [P, G])
        part, one_col, zero_col = sb("part", [P, 2, C], slots=2), sb1("one_col", [P, 1]), sb1("zero_col", [P, 1])
        neg_slope = sb1("neg_slope", [P, 1])
        turn_ps = [ctx.enter_context(nc.psum_tensor(f"{name}_turn{n}", [P, 2, C], F32)) for n in range(PAIRS)]
        y_ps = [ctx.enter_context(nc.psum_tensor(f"{name}_y{n}", [P, 2, C], F32)) for n in range(PAIRS)]
        stat_ps = ctx.enter_context(nc.psum_tensor(f"{name}_stat", [P, 2 * C], F32))
        T = lambda n, per=1, lead=0: Tally(nc, f"{name}_{n}", per, lead)
        loaded = [T(f"loaded{u}", 32) for u in range(SL)]
        gathered = [T(f"gathered{u}", 16 * G) for u in range(SL)]
        filled = T("filled", 1)
        turned = T("turned", PAIRS, lead=SL)
        in_T = T("in_T", PAIRS, lead=SL)
        mapped = T("mapped", PAIRS, lead=SL)
        added = T("added", PAIRS, lead=SL)
        bent = T("bent", 1, lead=SL)
        split = T("split", 1)
        ready = T("ready", 1, lead=SL)
        stat_ok = T("stat_ok", 1)
        aggregated = T("aggregated", 1)
        rooted = T("rooted", 1)
        inverted = T("inverted", 2)
        kept = T("kept", 1)
        squared = T("squared", 1)
        reduced = T("reduced", 2, lead=SL)
        totalled = T("totalled", 1, lead=SL)
        total = T("total", 1)
        stored = [T(f"stored{u}", 16) for u in range(SL)]
        s_set = nc.alloc_semaphore(f"{name}_set")
        beat = nc.alloc_semaphore(f"{name}_beat")
        dve_beat = nc.alloc_semaphore(f"{name}_dve_beat")

        def npairs(tiles):
            return -(-tiles // 2)

        def all_added(tiles):
            return npairs(tiles) if use_mm else PAIRS

        def pair_tiles(n, tiles):
            return range(2 * n, min(2 * n + 2, tiles))

        def rows_used(g):
            return (ready.sem, ready.at(g)) if hyper else (added.sem, added.at(g))

        def fill(engine, g, u):
            engine.wait_ge(*rows_used(g - SL))
            src = default[:].unsqueeze(1).to_broadcast([P, G, C])
            copy = engine.copy if hyper else engine.tensor_copy
            copy(g_in[u][:], src).then_inc(filled.sem, 1)

        def pipeline(engine, ahead, here, behind, fills=False, late=False):
            def step(g, u, turn, first=False):
                if fills:
                    fill(engine, g + AHEAD, (u + AHEAD) % SL)
                ahead(g + 1, (u + 1) % SL, turn + (u + 1) // SL, P, G)
                if late:
                    here(g, u, turn, P, G)
                if not first:
                    behind(g - 1, (u - 1) % SL, turn if u else turn - 1, P, G)
                if not late:
                    here(g, u, turn, P, G)
            if fills:
                for g in range(AHEAD):
                    fill(engine, g, g % SL)
            ahead(0, 0, 0, P, G)
            step(0, 0, 0, first=True)
            for g in range(1, SL):
                step(g, g % SL, g // SL)
            rest = (NG - 1) // SL
            with engine.Fori(1, rest) as i:
                for u in range(SL):
                    step(i * SL + u, u, i)
            for g in range(rest * SL, NG - 1):
                step(g, g % SL, g // SL)
            def at(g):
                return g, g % SL, g // SL
            ahead(*at(NG), TAIL, 1)
            behind(*at(NG - 2), P, G)
            here(*at(NG - 1), P, G)
            behind(*at(NG - 1), P, G)
            here(*at(NG), TAIL, 1)
            behind(*at(NG), TAIL, 1)

        def nothing(g, u, turn, parts, tiles):
            pass

        with nc.Block() as block:
            @block.sync
            def _(sp):
                def group(g, u, turn, parts, tiles):
                    sp.wait_ge(*rows_used(g - SL))
                    sp.dma_start(x[u][0:parts, 0:tiles, :], node_rows(table, g, parts, tiles)).then_inc(loaded[u].sem, 16)
                    sp.dma_start(idx[u][0:parts, 0:tiles],
                                 ends[bass.ds(g * (P * G), parts * tiles)].rearrange("(p j) -> p j", j=tiles)
                                 ).then_inc(loaded[u].sem, 16)
                groups(sp, SL, group)

            @block.gpsimd
            def _(pool):
                last = pool.to_reg(EP - 1)

                def group(g, u, turn, parts, tiles):
                    pool.wait_ge(loaded[u].sem, loaded[u].at(turn))
                    pool.wait_ge(filled.sem, filled.at(g))
                    pool.sem_inc(beat, 1)
                    for j in range(tiles):
                        pool.indirect_dma_start(
                            out=g_in[u][0:parts, j, :], out_offset=None, in_=sums,
                            in_offset=bass.IndirectOffsetOnAxis(ap=idx[u][0:parts, j:j + 1], axis=0),
                            bounds_check=last, oob_is_err=False).then_inc(gathered[u].sem, 16)
                groups(pool, SL, group)

            @block.tensor
            def _(pe):
                turned.open(pe)
                mapped.open(pe)
                totalled.open(pe)
                pe.wait_ge(s_set, 1)
                if not norm:
                    pe.matmul(stat_ps[0:1, :], zero_col[:], part[0][:].rearrange("p s f -> p (s f)"), start=True, stop=False)

                def turn_group(g, u, turn, parts, tiles):
                    pe.wait_ge(loaded[u].sem, loaded[u].at(turn))
                    for n in range(npairs(tiles)):
                        pe.wait_ge(in_T.sem, in_T.at(g - 1, n + 1))
                        for j in pair_tiles(n, tiles):
                            for h in range(H):
                                ins = pe.transpose(turn_ps[n][:, j % 2, h * P:h * P + parts],
                                                   x[u][0:parts, j, h * P:(h + 1) * P], k.ident[0:parts, 0:parts])
                        ins.then_inc(turned.sem, 1)

                def map_group(g, u, turn, parts, tiles):
                    for n in range(npairs(tiles)):
                        pe.wait_ge(added.sem, added.at(g - 1, n + 1))
                        pe.wait_ge(in_T.sem, in_T.at(g, n + 1))
                        for j in pair_tiles(n, tiles):
                            for h in range(H):
                                ins = pe.matmul(y_ps[n][0:parts, j % 2, :], x_T[u % 2][:, n, j % 2, h * P:h * P + parts],
                                                matrix[:, h, :], start=(h == 0), stop=(h == H - 1))
                        ins.then_inc(mapped.sem, 1)

                def total_group(g, u, turn, parts, tiles):
                    pe.wait_ge(reduced.sem, reduced.at(g))
                    pe.matmul(stat_ps[0:1, :], one_col[0:parts, :], part[u % 2][0:parts].rearrange("p s f -> p (s f)"),
                              start=False, stop=False).then_inc(totalled.sem, 1)

                if use_mm:
                    pipeline(pe, turn_group, map_group, nothing if norm else total_group, late=True)
                if not norm:
                    pe.matmul(stat_ps[0:1, :], zero_col[:], part[0][:].rearrange("p s f -> p (s f)"), start=False, stop=True
                              ).then_inc(total.sem, 1)

            @block.scalar
            def _(act):
                in_T.open(act)

                def ahead(g, u, turn, parts, tiles):
                    if use_mm:
                        for n in range(npairs(tiles)):
                            act.wait_ge(mapped.sem, mapped.at(g - 2, n + 1))
                            act.wait_ge(turned.sem, turned.at(g, n + 1))
                            w = len(pair_tiles(n, tiles))
                            if parts == P:
                                act.copy(x_T[u % 2][:, n, 0:w, :], turn_ps[n][:, 0:w, :]).then_inc(in_T.sem, 1)
                            else:
                                for h in range(H):
                                    ins = act.copy(x_T[u % 2][:, n, 0, h * P:h * P + parts],
                                                   turn_ps[n][:, 0, h * P:h * P + parts])
                                ins.then_inc(in_T.sem, 1)
                    if hyper:
                        at = (slice(0, parts), slice(0, tiles))
                        act.wait_ge(added.sem, added.at(g))
                        act.wait_ge(ready.sem, ready.at(g - 2))
                        act.activation(half[u % 2][at], res[u][at], ACT.Relu, scale=-1.0).then_inc(split.sem, 1)

                def here(g, u, turn, parts, tiles):
                    at = (slice(0, parts), slice(0, tiles))
                    if norm:
                        act.wait_ge(aggregated.sem, aggregated.at(g))
                        act.activation(std[u][at], mean_var[u][0:parts, 0:tiles, 1], ACT.Sqrt,
                                       bias=k.eps[0:parts, :]).then_inc(rooted.sem, 1)
                    else:
                        act.wait_ge(added.sem, added.at(g, all_added(tiles)))
                        act.wait_ge(reduced.sem, reduced.at(g - 2))
                        act.activation(half[u % 2][at], res[u][at], ACT.Square).then_inc(squared.sem, 1)
                        store(g, u, parts, tiles)

                def behind(g, u, turn, parts, tiles):
                    act.wait_ge(inverted.sem, inverted.at(g))
                    for j in range(tiles):
                        ins = act.activation(res[u][0:parts, j, :], res[u][0:parts, j, :], ACT.Identity,
                                             bias=shift[u][0:parts, j:j + 1], scale=rstd[u][0:parts, j:j + 1])
                    ins.then_inc(kept.sem, 1)
                    act.wait_ge(kept.sem, kept.at(g))
                    store(g, u, parts, tiles)

                def store(g, u, parts, tiles):
                    act.dma_start(node_rows(out, g, parts, tiles), res[u][0:parts, 0:tiles, :]).then_inc(stored[u].sem, 16)

                pipeline(act, ahead, here, behind if norm else nothing, fills=hyper)
                for u in range(SL):
                    act.wait_ge(stored[u].sem, stored[u].at((NG - u) // SL))

            @block.vector
            def _(dve):
                for t in (ready, added, bent, reduced):
                    t.open(dve)
                dve.memset(part[0][:], 0.0)
                dve.memset(zero_col[:], 0.0)
                dve.tensor_scalar(neg_slope[:], k.slope[:], -1.0, None, ALU.mult)
                dve.memset(one_col[:], 1.0).then_inc(s_set, 1)
                dve.wait_ge(s_set, 1)

                def add(g, u, turn, parts, tiles):
                    at = (slice(0, parts), slice(0, tiles))
                    dve.wait_ge(gathered[u].sem, gathered[u].at(turn) if tiles == G else gathered[u].at(turn, 16 * tiles))
                    if later(turn):
                        dve.wait_ge(stored[u].sem, stored[u].at(turn - 1))
                    if use_mm:
                        for n in range(npairs(tiles)):
                            w = len(pair_tiles(n, tiles))
                            dve.wait_ge(mapped.sem, mapped.at(g, n + 1))
                            dve.tensor_tensor(res[u][0:parts, 2 * n:2 * n + w, :], y_ps[n][0:parts, 0:w, :],
                                              g_in[u][0:parts, 2 * n:2 * n + w, :], ALU.add).then_inc(added.sem, 1)
                    else:
                        dve.wait_ge(loaded[u].sem, loaded[u].at(turn))
                        dve.tensor_tensor(res[u][at], g_in[u][at], x[u][at], ALU.add).then_inc(added.sem, PAIRS)
                    dve.wait_ge(added.sem, added.at(g, all_added(tiles)))
                    if hyper:
                        dve.scalar_tensor_tensor(g_in[u][at], res[u][at], 0.0, x[u][at], ALU.max, ALU.add
                                                 ).then_inc(bent.sem, 1)

                def statistics(g, u, turn, parts, tiles):
                    at = (slice(0, parts), slice(0, tiles))
                    if hyper:
                        dve.wait_ge(split.sem, split.at(g))
                        dve.wait_ge(bent.sem, bent.at(g))
                        dve.scalar_tensor_tensor(res[u][at], half[u % 2][at], neg_slope[0:parts, 0:1], g_in[u][at],
                                                 ALU.mult, ALU.add).then_inc(ready.sem, 1)
                        dve.wait_ge(ready.sem, ready.at(g))
                    if norm:
                        for j in range(tiles):
                            ins = dve.bn_stats(stats[0:parts, j, :], res[u][0:parts, j, :])
                        ins.then_inc(stat_ok.sem, 1)
                        dve.wait_ge(stat_ok.sem, stat_ok.at(g))
                        dve.sem_inc(dve_beat, 1)
                        for j in range(tiles):
                            ins = dve.bn_aggr(mean_var[u][0:parts, j, :], stats[0:parts, j, :])
                        ins.then_inc(aggregated.sem, 1)
                    else:
                        dve.wait_ge(totalled.sem, totalled.at(g - 2))
                        dve.tensor_reduce(part[u % 2][0:parts, 0, :], res[u][at].rearrange("p j f -> p f j"),
                                          mybir.AxisListType.X, ALU.add)

                def add_up_squares(g, u, turn, parts, tiles):
                    at = (slice(0, parts), slice(0, tiles))
                    dve.wait_ge(squared.sem, squared.at(g))
                    dve.tensor_reduce(part[u % 2][0:parts, 1, :], half[u % 2][at].rearrange("p j f -> p f j"),
                                      mybir.AxisListType.X, ALU.add).then_inc(reduced.sem, 2)

                def add_and_statistics(g, u, turn, parts, tiles):
                    add(g, u, turn, parts, tiles)
                    statistics(g, u, turn, parts, tiles)

                def invert(g, u, turn, parts, tiles):
                    at = (slice(0, parts), slice(0, tiles))
                    dve.wait_ge(rooted.sem, rooted.at(g))
                    dve.reciprocal(rstd[u][at], std[u][at]).then_inc(inverted.sem, 1)
                    dve.wait_ge(inverted.sem, inverted.at(g, 1))
                    dve.scalar_tensor_tensor(shift[u][at], mean_var[u][0:parts, 0:tiles, 0], -1.0, rstd[u][at],
                                             ALU.mult, ALU.mult).then_inc(inverted.sem, 1)

                if hyper:
                    pipeline(dve, add, statistics, invert)
                else:
                    pipeline(dve, nothing, add_and_statistics, invert if norm else add_up_squares, fills=True)
                if not norm:
                    dve.wait_ge(total.sem, 1)
                    dve.tensor_copy(stat_rows[:], stat_ps[0:1, :].rearrange("p (s f) -> p s f", s=2))


def final_pass(nc, top, k, table, rooted_rows, stat_rows, gamma, beta, out):
    SL = 3
    name = "final"
    with ExitStack() as ctx:
        def sb1(n, shape, dt=F32):
            return ctx.enter_context(nc.sbuf_tensor(f"{name}_{n}", shape, dt))

        def sb(n, shape, dt=F32):
            return [sb1(f"{n}{u}", shape, dt) for u in range(SL)]

        x, y, res = sb("x", [P, G, C]), sb("y", [P, G, C]), sb("res", [P, G, C])
        stats, mean_var = sb1("stats", [P, G, 6]), sb1("mean_var", [P, G, 2])
        std, rstd, shift = sb1("std", [P, G]), sb1("rstd", [P, G]), sb1("shift", [P, G])
        gb = sb1("gamma_beta", [1, 2, C])
        mom = sb1("moments", [1, 2, C])
        sq, bn_var, bn_std, bn_inv, fac, mf = (sb1(n, [1, C]) for n in ("mean_sq", "bn_var", "bn_std", "bn_inv", "fac", "mf"))
        coef = sb1("coef", [1, 2, C])
        coefs = sb1("coefs", [P, 2, C])
        ones_row = sb1("ones_row", [1, P])
        ps = ctx.enter_context(nc.psum_tensor(f"{name}_ps", [P, 2, C], F32))
        T = lambda n, per=1, lead=0: Tally(nc, f"{name}_{n}", per, lead)
        s_in, s_prep, s_root, s_ps = (nc.alloc_semaphore(f"{name}_{n}") for n in ("in", "prep", "root", "ps"))
        s_co = nc.alloc_semaphore(f"{name}_co")
        dve_beat = nc.alloc_semaphore(f"{name}_dve_beat")
        loaded = [T(f"loaded{u}", 32) for u in range(SL)]
        scaled, shifted = T("scaled"), T("shifted")
        once, twice = T("once", lead=0), T("twice", lead=SL)
        stat_ok, aggregated, rooted = T("stat_ok"), T("aggregated"), T("rooted")
        inverted, kept = T("inverted", 2), T("kept", 1, lead=SL)
        stored = [T(f"stored{u}", 16) for u in range(SL)]
        with nc.Block() as block:
            @block.sync
            def _(sp):
                sp.dma_start(gb[:, 0, :], gamma.rearrange("(o f) -> o f", o=1)).then_inc(s_in, 16)
                sp.dma_start(gb[:, 1, :], beta.rearrange("(o f) -> o f", o=1)).then_inc(s_in, 16)

                def group(g, u, turn, parts, tiles):
                    sp.wait_ge(twice.sem, twice.at(g - SL))
                    for t, to in ((table, x), (rooted_rows, y)):
                        sp.dma_start(to[u][0:parts, 0:tiles, :], node_rows(t, g, parts, tiles)).then_inc(loaded[u].sem, 16)
                groups(sp, SL, group)

            @block.tensor
            def _(pe):
                pe.wait_ge(s_prep, 8)
                pe.matmul(ps[:].rearrange("p s f -> p (s f)"), ones_row[:], coef[:].rearrange("p s f -> p (s f)"),
                          start=True, stop=True).then_inc(s_ps, 1)

            @block.gpsimd
            def _(pool):
                pool.wait_ge(s_co, 1)

                def group(g, u, turn, parts, tiles):
                    at = (slice(0, parts), slice(0, tiles))
                    pool.wait_ge(loaded[u].sem, loaded[u].at(turn))
                    pool.tensor_tensor(y[u][at], y[u][at], coefs[0:parts, 0, :].unsqueeze(1).to_broadcast([parts, tiles, C]),
                                       ALU.mult).then_inc(scaled.sem, 1)
                    pool.wait_ge(scaled.sem, scaled.at(g))
                    pool.tensor_tensor(y[u][at], y[u][at], coefs[0:parts, 1, :].unsqueeze(1).to_broadcast([parts, tiles, C]),
                                       ALU.add).then_inc(shifted.sem, 1)
                groups(pool, SL, group)

            @block.vector
            def _(dve):
                twice.open(dve)
                dve.memset(ones_row[:], 1.0)
                dve.tensor_scalar(mom[:], stat_rows[:], 1.0 / N, None, ALU.mult).then_inc(s_prep, 1)
                dve.wait_ge(s_prep, 1)
                dve.tensor_tensor(sq[:], mom[:, 0, :], mom[:, 0, :], ALU.mult).then_inc(s_prep, 1)
                dve.wait_ge(s_prep, 2)
                dve.tensor_tensor(bn_var[:], mom[:, 1, :], sq[:], ALU.subtract).then_inc(s_prep, 1)
                dve.wait_ge(s_root, 1)
                dve.reciprocal(bn_inv[:], bn_std[:]).then_inc(s_prep, 1)
                dve.wait_ge(s_prep, 4)
                dve.wait_ge(s_in, 32)
                dve.tensor_tensor(coef[:, 0, :], bn_inv[:], gb[:, 0, :], ALU.mult).then_inc(s_prep, 1)
                dve.wait_ge(s_prep, 5)
                dve.tensor_tensor(mf[:], mom[:, 0, :], coef[:, 0, :], ALU.mult).then_inc(s_prep, 1)
                dve.wait_ge(s_prep, 6)
                dve.tensor_tensor(coef[:, 1, :], gb[:, 1, :], mf[:], ALU.subtract).then_inc(s_prep, 2)
                dve.wait_ge(s_ps, 1)
                dve.tensor_copy(coefs[:], ps[:]).then_inc(s_co, 1)

                def group(g, u, turn, parts, tiles):
                    at = (slice(0, parts), slice(0, tiles))
                    dve.wait_ge(shifted.sem, shifted.at(g))
                    if later(turn):
                        dve.wait_ge(stored[u].sem, stored[u].at(turn - 1))
                    dve.scalar_tensor_tensor(res[u][at], y[u][at], 0.0, x[u][at], ALU.max, ALU.add).then_inc(once.sem, 1)
                    dve.wait_ge(once.sem, once.at(g))
                    dve.scalar_tensor_tensor(res[u][at], res[u][at], 0.0, x[u][at], ALU.max, ALU.add).then_inc(twice.sem, 1)
                    dve.wait_ge(twice.sem, twice.at(g))
                    for j in range(tiles):
                        ins = dve.bn_stats(stats[0:parts, j, :], res[u][0:parts, j, :])
                    ins.then_inc(stat_ok.sem, 1)
                    dve.wait_ge(stat_ok.sem, stat_ok.at(g))
                    dve.sem_inc(dve_beat, 1)
                    for j in range(tiles):
                        ins = dve.bn_aggr(mean_var[0:parts, j, :], stats[0:parts, j, :])
                    ins.then_inc(aggregated.sem, 1)
                    dve.wait_ge(rooted.sem, rooted.at(g))
                    dve.wait_ge(kept.sem, kept.at(g - 1))
                    dve.reciprocal(rstd[0:parts, 0:tiles], std[0:parts, 0:tiles]).then_inc(inverted.sem, 1)
                    dve.wait_ge(inverted.sem, inverted.at(g, 1))
                    dve.scalar_tensor_tensor(shift[0:parts, 0:tiles], mean_var[0:parts, 0:tiles, 0], -1.0,
                                             rstd[0:parts, 0:tiles], ALU.mult, ALU.mult).then_inc(inverted.sem, 1)
                groups(dve, SL, group, peel=1)

            @block.scalar
            def _(act):
                kept.open(act)
                act.wait_ge(s_prep, 3)
                act.activation(bn_std[:], bn_var[:], ACT.Sqrt, bias=k.eps[0:1, :]).then_inc(s_root, 1)

                def group(g, u, turn, parts, tiles):
                    act.wait_ge(aggregated.sem, aggregated.at(g))
                    act.activation(std[0:parts, 0:tiles], mean_var[0:parts, 0:tiles, 1], ACT.Sqrt,
                                   bias=k.eps[0:parts, :]).then_inc(rooted.sem, 1)
                    act.wait_ge(inverted.sem, inverted.at(g))
                    for j in range(tiles):
                        ins = act.activation(res[u][0:parts, j, :], res[u][0:parts, j, :], ACT.Identity,
                                             bias=shift[0:parts, j:j + 1], scale=rstd[0:parts, j:j + 1])
                    ins.then_inc(kept.sem, 1)
                    act.wait_ge(kept.sem, kept.at(g))
                    act.dma_start(node_rows(out, g, parts, tiles), res[u][0:parts, 0:tiles, :]).then_inc(stored[u].sem, 16)
                groups(act, SL, group)
                for u in range(SL):
                    act.wait_ge(stored[u].sem, stored[u].at((NG - u) // SL))


def graph_layers(nc, x, src, dst, edge_weight, w, out):
    class Kept:
        pass

    k = Kept()
    nodes = [nc.dram_tensor(f"nodes{n}", (N, C), F32, kind="Internal").ap() for n in (1, 2, 3)]
    rooted = nc.dram_tensor("rooted", (N, C), F32, kind="Internal").ap()
    sums = [nc.dram_tensor(f"sums{n}", (EP, C), F32, kind="Internal").ap() for n in range(7)]
    with ExitStack() as top:
        with stage(nc):
            constants(nc, top, k)
        with ExitStack() as sorting:
            with stage(nc):
                key_columns(nc, top, sorting, k, src, dst, edge_weight)
            with stage(nc):
                sort_edges(nc, top, k)
        with stage(nc):
            position_columns(nc, top, k)
        with stage(nc):
            load_weights(nc, top, k, w)
        end = k.node_end
        with stage(nc):
            attention_pass(nc, top, k, "att0", 8, x, "other", x, sums[0], True, 32 ** -0.5, bias=k.row["bs"])
        with stage(nc):
            node_pass(nc, top, k, "node0", "attention", x, end["dst"], sums[0], k.row["bs"], nodes[0], matrix=k.w["Ws"])
        with stage(nc):
            sum_pass(nc, top, k, "hyp1", "dst", nodes[0], "other", sums[1], matrix=k.w["W1"], scaled=True)
        with stage(nc):
            sum_pass(nc, top, k, "hyp2", "src", sums[1], "other_end", sums[2], scaled=True, bias=k.row["b1"], prelu=True)
        with stage(nc):
            sum_pass(nc, top, k, "hyp3", "dst", sums[2], "other_end", sums[3], matrix=k.w["W2"], scaled=True)
        with stage(nc):
            sum_pass(nc, top, k, "hyp4", "src", sums[3], "other_end", sums[4], scaled=True, bias=k.row["b2"])
        with stage(nc):
            node_pass(nc, top, k, "node1", "hyper", nodes[0], end["src"], sums[4], k.row["b2"], nodes[1])
        with stage(nc):
            attention_pass(nc, top, k, "att2", 4, nodes[1], "other", nodes[1], sums[5], False, 1.0)
        with stage(nc):
            node_pass(nc, top, k, "node2", "plain", nodes[1], end["dst"], sums[5], k.row["zero"], nodes[2])
        with stage(nc):
            sum_pass(nc, top, k, "rel3", "dst", nodes[2], "other", sums[6], matrix=k.wT["W_rel"], weighted=True,
                     bias=k.row["b_rel"])
        with ExitStack() as last:
            stat_rows = last.enter_context(nc.sbuf_tensor("stat_rows", [1, 2, C], F32))
            with stage(nc):
                node_pass(nc, top, k, "node3", "root", nodes[2], end["dst"], sums[6], k.row["b_rel"], rooted,
                          matrix=k.wT["W_root"], stat_rows=stat_rows)
            with stage(nc):
                final_pass(nc, top, k, nodes[2], rooted, stat_rows, w["gamma"], w["beta"], out)


_INS = ["x", "src", "dst", "edge_weight", "L0_gnn_Wq", "L0_gnn_bq", "L0_gnn_Wk", "L0_gnn_bk", "L0_gnn_Wv", "L0_gnn_bv",
        "L0_gnn_Ws", "L0_gnn_bs", "L1_gnn_W1", "L1_gnn_b1", "L1_gnn_W2", "L1_gnn_b2", "L1_gnn_a", "L2_gnn_W",
        "L2_gnn_att", "L3_gnn_W_rel", "L3_gnn_b_rel", "L3_gnn_W_root", "L3_gnn_gamma", "L3_gnn_beta"]


def kernel(**inputs):
    import numpy as _np
    import concourse.bacc as _bacc
    from concourse import mybir as _mybir
    from concourse.bass_utils import run_bass_kernel_spmd as _run

    nc = _bacc.Bacc("TRN2", target_bir_lowering=False, num_devices=1)
    arrays, args = {}, {}
    for name in _INS:
        a = _np.ascontiguousarray(inputs[name])
        arrays[f"in_{name}_dram"] = a
        args[name] = nc.dram_tensor(f"in_{name}_dram", a.shape, _mybir.dt.from_np(a.dtype), kind="ExternalInput").ap()
    out = nc.dram_tensor("out_0_dram", (N, C), F32, kind="ExternalOutput").ap()
    weights = {n.split("_gnn_")[1]: a for n, a in args.items() if "_gnn_" in n}
    graph_layers(nc, args["x"], args["src"], args["dst"], args["edge_weight"], weights, out)
    r = _run(nc, [arrays], core_ids=[0])
    return r.results[0]["out_0_dram"]
```

```python
from contextlib import ExitStack, contextmanager
from functools import partial

import concourse.bass as bass
from concourse import mybir

ALU = mybir.AluOpType
ACT = mybir.ActivationFunctionType
F32 = mybir.dt.float32
BF16 = mybir.dt.bfloat16
FP16 = mybir.dt.float16
I32 = mybir.dt.int32

P = 128
N = 50000
E = 25000
C = 256
H = C // P
CH = 512
TPC = CH // P
NCH = -(-E // CH)
EP = NCH * CH
NT = EP // P
KR = NT // 2
HI = -(-(N + 1) // P)
G = 6
NG = N // (P * G)
TAIL = N - NG * P * G
SKIP = float(1 << 20)
BIG = 1e30
EPS = 1e-5
LIFT = 2.0 ** 15
REC = 4
META = 5 * TPC


class Tally:

    def __init__(self, nc, name, per=1, lead=0):
        self.sem = nc.alloc_semaphore(name)
        self.per = per
        self.lead = lead

    def open(self, engine):
        engine.sem_inc(self.sem, self.lead * self.per)

    def at(self, rnd, step=None):
        return (rnd + self.lead) * self.per + (self.per if step is None else step)


@contextmanager
def stage(nc):
    before = nc.snapshot_sems()
    yield
    nc.clear_and_free_semaphores(nc.allocated_since(before))
    nc.all_engine_barrier()


def rounds(engine, count, unroll, body, peel=0):
    for turn in range(peel):
        for u in range(unroll):
            body(turn * unroll + u, u, turn)
    if count // unroll > peel:
        with engine.Fori(peel, count // unroll) as i:
            for u in range(unroll):
                body(i * unroll + u, u, i)
    for u in range(count % unroll):
        body(count // unroll * unroll + u, u, count // unroll)


def later(turn, than=0):
    return not isinstance(turn, int) or turn > than


def constants(nc, top, k):
    k.ident = top.enter_context(nc.sbuf_tensor("ident", [P, P], F32))
    k.ident_bf = top.enter_context(nc.sbuf_tensor("ident_bf", [P, P], BF16))
    k.eps = top.enter_context(nc.sbuf_tensor("eps", [P, 1], F32))
    zeroed = nc.alloc_semaphore("ident_zeroed")
    made = nc.alloc_semaphore("ident_made")
    with nc.Block() as block:
        @block.gpsimd
        def _(pool):
            pool.memset(k.eps[:], EPS)
            pool.memset(k.ident[:], 0.0).then_inc(zeroed, 1)
            pool.wait_ge(zeroed, 1)
            pool.affine_select(out=k.ident[:], in_=k.ident[:], compare_op=ALU.not_equal, fill=1.0, base=0,
                               pattern=[[-1, P]], channel_multiplier=1).then_inc(made, 1)
            pool.wait_ge(made, 1)
            pool.tensor_copy(k.ident_bf[:], k.ident[:])


def key_columns(nc, top, ctx_sort, k, src, dst, edge_weight):
    k.edge = {f: ctx_sort.enter_context(nc.sbuf_tensor(f"edge_{f}", [P, NT, 3], F32)) for f in ("src", "dst")}
    k.cols = {f: ctx_sort.enter_context(nc.sbuf_tensor(f"col_{f}", [P, NT], F32))
              for f in ("src_hi", "src_lo", "dst_hi", "dst_lo")}
    TURN = (("src", (k.edge["src"][:, :, 0], k.edge["dst"][:, :, 1])),
            ("dst", (k.edge["dst"][:, :, 0], k.edge["src"][:, :, 1])),
            ("w", (k.edge["src"][:, :, 2], k.edge["dst"][:, :, 2])),
            *((f, (k.cols[f][:],)) for f in k.cols))
    k.key_rows = {f: nc.dram_tensor(f"keys_{f}", (EP,), F32, kind="Internal").ap() for f in ("src", "dst")}
    full = E // (2 * P)
    rest = E - full * 2 * P
    with ExitStack() as ctx:
        raw = {f: ctx.enter_context(nc.sbuf_tensor(f"raw_{f}", [KR, 2 * P], I32)) for f in ("src", "dst")}
        part = {f: ctx.enter_context(nc.sbuf_tensor(f"part_{f}", [KR, 2 * P], I32))
                for f in ("src_hi", "src_lo", "dst_hi", "dst_lo")}
        rows = {f: ctx.enter_context(nc.sbuf_tensor(f"row_{f}", [KR, 2 * P], F32)) for f, _ in TURN}
        ps = ctx.enter_context(nc.psum_tensor("keys_T", [P, 2, 4, P], F32))
        s_padded = nc.alloc_semaphore("keys_padded")
        s_loaded = nc.alloc_semaphore("keys_loaded")
        s_parts = nc.alloc_semaphore("keys_parts")
        s_float = nc.alloc_semaphore("keys_float")
        s_turned = nc.alloc_semaphore("keys_turned")
        s_kept = nc.alloc_semaphore("keys_kept")
        s_stored = nc.alloc_semaphore("keys_stored")
        with nc.Block() as block:
            @block.sync
            def _(sp):
                sp.wait_ge(s_padded, 3)
                for tile, ap in ((raw["src"], src), (raw["dst"], dst), (rows["w"], edge_weight)):
                    sp.dma_start(tile[0:full, :], ap[0:full * 2 * P].rearrange("(r c) -> r c", c=2 * P)
                                 ).then_inc(s_loaded, 16)
                    sp.dma_start(tile[full:full + 1, 0:rest], ap[full * 2 * P:E].rearrange("(r c) -> r c", r=1)
                                 ).then_inc(s_loaded, 16)
                sp.wait_ge(s_float, 6)
                for f in ("src", "dst"):
                    sp.dma_start(k.key_rows[f].rearrange("(r c) -> r c", c=2 * P), rows[f][:]).then_inc(s_stored, 16)
                sp.wait_ge(s_stored, 32)

            @block.vector
            def _(dve):
                dve.memset(raw["src"][:], N).then_inc(s_padded, 1)
                dve.memset(raw["dst"][:], N).then_inc(s_padded, 1)
                dve.memset(rows["w"][:], 0.0).then_inc(s_padded, 1)
                dve.wait_ge(s_loaded, 6 * 16)
                for f in ("src", "dst"):
                    dve.tensor_scalar(part[f + "_hi"][:], raw[f][:], 7, None, ALU.arith_shift_right).then_inc(s_parts, 1)
                    dve.tensor_scalar(part[f + "_lo"][:], raw[f][:], P - 1, None, ALU.bitwise_and).then_inc(s_parts, 1)
                dve.wait_ge(s_parts, 4)
                for f in ("src", "dst"):
                    dve.tensor_copy(rows[f][:], raw[f][:]).then_inc(s_float, 1)
                    dve.tensor_copy(rows[f + "_hi"][:], part[f + "_hi"][:]).then_inc(s_float, 1)
                    dve.tensor_copy(rows[f + "_lo"][:], part[f + "_lo"][:]).then_inc(s_float, 1)
                for n, (f, outs) in enumerate(TURN):
                    dve.wait_ge(s_turned, n + 1)
                    for c in range(2):
                        for out in outs:
                            ins = dve.tensor_copy(out[:, c:NT:2], ps[:, n % 2, c, 0:KR])
                    ins.then_inc(s_kept, 1)

            @block.tensor
            def _(pe):
                pe.wait_ge(s_float, 6)
                for n, (f, _) in enumerate(TURN):
                    if n >= 2:
                        pe.wait_ge(s_kept, n - 1)
                    for c in range(2):
                        ins = pe.transpose(ps[:, n % 2, c, 0:KR], rows[f][:, c * P:(c + 1) * P], k.ident[0:KR, 0:KR])
                    ins.then_inc(s_turned, 1)


def sort_edges(nc, top, k):
    KEYS = ("dst", "src")
    SLOTS = 4
    k.records = {f: nc.dram_tensor(f"records_{f}", (EP + 1, REC), F32, kind="Internal").ap() for f in KEYS}
    k.node_end = {f: nc.dram_tensor(f"node_end_{f}", (HI * P,), I32, kind="Internal").ap() for f in KEYS}
    with ExitStack() as ctx:
        def sb(name, shape, dt):
            return ctx.enter_context(nc.sbuf_tensor(name, shape, dt))

        iota_hi32, iota_lo32 = sb("iota_hi32", [P, HI], I32), sb("iota_lo32", [P, P], I32)
        iota_hi, iota_lo = sb("iota_hi", [P, HI], FP16), sb("iota_lo", [P, P], FP16)
        zero_bf = sb("zero_bf", [P, HI], BF16)
        lift, minus_lift = sb("lift", [P, P], BF16), sb("minus_lift", [P, 1], F32)
        ones = sb("ones", [P, P], F32)
        upto = sb("upto", [P, P], F32)
        below = sb("below", [P, P], F32)
        first = sb("first", [1, REC], F32)
        cnt = {f: sb(f"cnt_{f}", [P, HI], F32) for f in KEYS}
        incl = {f: sb(f"incl_{f}", [P, HI], F32) for f in KEYS}
        start = {f: sb(f"start_{f}", [P, HI], F32) for f in KEYS}
        end = {f: sb(f"end_{f}", [P, HI], F32) for f in KEYS}
        end_hi = {f: sb(f"end_hi_{f}", [P, HI], BF16) for f in KEYS}
        end_lo = {f: sb(f"end_lo_{f}", [P, HI], BF16) for f in KEYS}
        none = {f: sb(f"none_{f}", [P, HI], F32) for f in KEYS}
        node = {f: sb(f"node_{f}", [P, HI], F32) for f in KEYS}
        node_i = {f: sb(f"node_i_{f}", [P, 4, P], I32) for f in KEYS}
        tot = {f: sb(f"tot_{f}", [1, HI], F32) for f in KEYS}
        run = {f: sb(f"run_{f}", [1, HI], F32) for f in KEYS}
        offs = {f: sb(f"offs_{f}", [1, HI], F32) for f in KEYS}
        ones_row = sb("ones_row", [1, HI], F32)
        s_mk = [nc.alloc_semaphore(f"sort_const{n}") for n in range(3)]

        with nc.Block() as block:
            @block.gpsimd
            def _(pool):
                pool.iota(iota_hi32[:], pattern=[[1, HI]], base=0, channel_multiplier=0).then_inc(s_mk[0], 1)
                pool.iota(iota_lo32[:], pattern=[[1, P]], base=0, channel_multiplier=0).then_inc(s_mk[0], 1)
                pool.memset(ones[:], 1.0).then_inc(s_mk[0], 1)
                pool.wait_ge(s_mk[0], 3)
                pool.affine_select(out=upto[:], in_=ones[:], compare_op=ALU.is_ge, fill=0.0, base=0,
                                   pattern=[[1, P]], channel_multiplier=-1).then_inc(s_mk[1], 1)
                pool.affine_select(out=below[:], in_=ones[:], compare_op=ALU.is_gt, fill=0.0, base=0,
                                   pattern=[[-1, P]], channel_multiplier=1).then_inc(s_mk[1], 1)

            @block.vector
            def _(dve):
                dve.memset(zero_bf[:], 0.0)
                dve.memset(minus_lift[:], -LIFT)
                dve.tensor_scalar(lift[:], k.ident_bf[:], LIFT, None, ALU.mult)
                dve.memset(ones_row[:], 1.0)
                dve.memset(first[:], -1.0).then_inc(s_mk[2], 1)
                dve.wait_ge(s_mk[1], 2)
                dve.tensor_copy(iota_hi[:], iota_hi32[:])
                dve.tensor_copy(iota_lo[:], iota_lo32[:])

        one_hi = [{f: sb(f"one_hi{u}_{f}", [P, HI], BF16) for f in KEYS} for u in range(SLOTS)]
        one_lo = [{f: sb(f"one_lo{u}_{f}", [P, P], BF16) for f in KEYS} for u in range(SLOTS)]

        with ExitStack() as st:
            hist = {f: st.enter_context(nc.psum_tensor(f"hist_{f}", [P, 512], F32)) for f in KEYS}
            made = Tally(nc, "count_made", 2)
            used = Tally(nc, "count_used", 2, lead=SLOTS)
            done = nc.alloc_semaphore("count_done")
            with nc.Block() as block:
                @block.vector
                def _(dve):
                    def tile(t, u, turn):
                        dve.wait_ge(used.sem, used.at(t - SLOTS))
                        for f in KEYS:
                            dve.tensor_scalar(one_hi[u][f][:], iota_hi[:], k.cols[f + "_hi"][:, bass.ds(t, 1)], None,
                                              ALU.is_equal)
                            dve.tensor_scalar(one_lo[u][f][:], iota_lo[:], k.cols[f + "_lo"][:, bass.ds(t, 1)], None,
                                              ALU.is_equal).then_inc(made.sem, 1)
                    rounds(dve, NT, SLOTS, tile)
                    dve.wait_ge(done, 2)
                    for f in KEYS:
                        dve.tensor_copy(cnt[f][:], hist[f][:, 0:HI])

                @block.tensor
                def _(pe):
                    used.open(pe)
                    for f in KEYS:
                        pe.matmul(hist[f][:, 0:HI], zero_bf[:, 0:P], zero_bf[:], start=True, stop=False)

                    def tile(t, u, turn):
                        for n, f in enumerate(KEYS):
                            pe.wait_ge(made.sem, made.at(t, n + 1))
                            pe.matmul(hist[f][:, 0:HI], one_lo[u][f][:], one_hi[u][f][:], start=False, stop=False
                                      ).then_inc(used.sem, 1)
                    rounds(pe, NT, SLOTS, tile)
                    for f in KEYS:
                        pe.matmul(hist[f][:, 0:HI], zero_bf[:, 0:P], zero_bf[:], start=False, stop=True
                                  ).then_inc(done, 1)

        with ExitStack() as st:
            tot_ps = {f: st.enter_context(nc.psum_tensor(f"tot_ps_{f}", [1, 512], F32)) for f in KEYS}
            incl_ps = {f: st.enter_context(nc.psum_tensor(f"incl_ps_{f}", [P, 512], F32)) for f in KEYS}
            turn_ps = {f: st.enter_context(nc.psum_tensor(f"turn_ps_{f}", [P, 4, P], F32)) for f in KEYS}
            summed = nc.alloc_semaphore("pre_summed")
            tot_out = nc.alloc_semaphore("pre_tot")
            ran = nc.alloc_semaphore("pre_ran")
            offs_ok = nc.alloc_semaphore("pre_offs")
            incl_ok = nc.alloc_semaphore("pre_incl")
            copied = nc.alloc_semaphore("pre_copied")
            ended = nc.alloc_semaphore("pre_ended")
            rounded = nc.alloc_semaphore("pre_rounded")
            node_ok = nc.alloc_semaphore("pre_node")
            turned = nc.alloc_semaphore("pre_turned")
            node_int = nc.alloc_semaphore("pre_int")
            stored = nc.alloc_semaphore("pre_stored")
            with nc.Block() as block:
                @block.tensor
                def _(pe):
                    for f in KEYS:
                        pe.matmul(tot_ps[f][:, 0:HI], ones[:, 0:1], cnt[f][:], start=True, stop=True).then_inc(summed, 1)
                    for n, f in enumerate(KEYS):
                        pe.wait_ge(offs_ok, n + 1)
                        pe.matmul(incl_ps[f][:, 0:HI], upto[:], cnt[f][:], start=True, stop=False)
                        pe.matmul(incl_ps[f][:, 0:HI], ones[0:1, :], offs[f][:], start=False, stop=True).then_inc(incl_ok, 1)
                    for n, f in enumerate(KEYS):
                        pe.wait_ge(node_ok, 2 * n + 2)
                        for c in range(4):
                            w = min(P, HI - c * P)
                            ins = pe.transpose(turn_ps[f][0:w, c, :], node[f][:, c * P:c * P + w], k.ident[:])
                        ins.then_inc(turned, 1)

                @block.vector
                def _(dve):
                    for n, f in enumerate(KEYS):
                        dve.wait_ge(summed, n + 1)
                        dve.tensor_copy(tot[f][:], tot_ps[f][:, 0:HI]).then_inc(tot_out, 1)
                        dve.wait_ge(tot_out, n + 1)
                        dve.tensor_tensor_scan(run[f][:], ones_row[:], tot[f][:], 0.0, ALU.mult, ALU.add).then_inc(ran, 1)
                        dve.wait_ge(ran, n + 1)
                        dve.tensor_tensor(offs[f][:], run[f][:], tot[f][:], ALU.subtract).then_inc(offs_ok, 1)
                    for n, f in enumerate(KEYS):
                        dve.wait_ge(incl_ok, n + 1)
                        dve.tensor_copy(incl[f][:], incl_ps[f][:, 0:HI]).then_inc(copied, 1)
                        dve.wait_ge(copied, n + 1)
                        dve.scalar_tensor_tensor(start[f][:], incl[f][:], 1.0, cnt[f][:], ALU.add, ALU.subtract)
                        dve.tensor_scalar(end[f][:], incl[f][:], -1.0, None, ALU.add).then_inc(ended, 1)
                        dve.tensor_scalar(none[f][:], cnt[f][:], 0.0, SKIP, ALU.is_equal, ALU.mult).then_inc(node_ok, 1)
                        dve.wait_ge(ended, n + 1)
                        dve.tensor_copy(end_hi[f][:], end[f][:]).then_inc(rounded, 1)
                        dve.wait_ge(node_ok, 2 * n + 1)
                        dve.tensor_tensor(node[f][:], end[f][:], none[f][:], ALU.add).then_inc(node_ok, 1)
                        dve.wait_ge(rounded, n + 1)
                        dve.tensor_tensor(end_lo[f][:], end[f][:], end_hi[f][:], ALU.subtract)
                    for n, f in enumerate(KEYS):
                        dve.wait_ge(turned, n + 1)
                        dve.tensor_copy(node_i[f][:, 0:3, :], turn_ps[f][:, 0:3, :])
                        w = HI - 3 * P
                        dve.tensor_copy(node_i[f][0:w, 3, :], turn_ps[f][0:w, 3, :]).then_inc(node_int, 1)

                @block.sync
                def _(sp):
                    for n, f in enumerate(KEYS):
                        sp.dma_start(k.records[f][0:1, :], first[:]).then_inc(stored, 16)
                    for n, f in enumerate(KEYS):
                        sp.wait_ge(node_int, n + 1)
                        for c in range(4):
                            w = min(P, HI - c * P)
                            sp.dma_start(k.node_end[f][c * P * P:(c * P + w) * P].rearrange("(h l) -> h l", l=P),
                                         node_i[f][0:w, c, :]).then_inc(stored, 16)
                    sp.wait_ge(stored, 16 * 10)

        with ExitStack() as st:
            def sb2(name, shape, dt):
                return st.enter_context(nc.sbuf_tensor(name, shape, dt))

            OTHER = {"dst": "src", "src": "dst"}
            key_row = [{f: sb2(f"key_row{u}_{f}", [P, P], F32) for f in KEYS} for u in range(SLOTS)]
            lo_T = [{f: sb2(f"lo_T{u}_{f}", [P, P], F32) for f in KEYS} for u in range(2)]
            lo_Tb = [{f: sb2(f"lo_Tb{u}_{f}", [P, P], BF16) for f in KEYS} for u in range(2)]
            table = [{f: sb2(f"table{u}_{f}", [P, HI], F32) for f in KEYS} for u in range(2)]
            same = {f: sb2(f"same_{f}", [P, P], F32) for f in KEYS}
            junk = {f: sb2(f"junk_{f}", [P, HI], F32) for f in KEYS}
            junk_end = {f: sb2(f"junk_end_{f}", [P, HI], F32) for f in KEYS}
            before = [{f: sb2(f"before{u}_{f}", [P, 1], F32) for f in KEYS} for u in range(SLOTS)]
            rank = [{f: sb2(f"rank{u}_{f}", [P, 1], I32) for f in KEYS} for u in range(SLOTS)]
            rank_f = [{f: sb2(f"rank_f{u}_{f}", [P, 1], F32) for f in KEYS} for u in range(SLOTS)]
            rec = [{f: sb2(f"rec{u}_{f}", [P, REC], F32) for f in KEYS} for u in range(SLOTS)]
            count_ps = {f: st.enter_context(nc.psum_tensor(f"count_ps_{f}", [P, 512], F32)) for f in KEYS}
            turn_bf = {f: st.enter_context(nc.psum_tensor(f"turn_bf_{f}", [P, 1024], BF16)) for f in KEYS}
            at_ps = {f: st.enter_context(nc.psum_tensor(f"at_ps_{f}", [P, 512], F32)) for f in KEYS}
            end_ps = {f: st.enter_context(nc.psum_tensor(f"end_ps_{f}", [P, 512], F32)) for f in KEYS}
            row_in = [Tally(nc, f"rank_row_in{u}", 32) for u in range(SLOTS)]
            made = Tally(nc, "rank_made", 2)
            turned = Tally(nc, "rank_turned", 2)
            copied = Tally(nc, "rank_copied", 2, lead=1)
            tabled = Tally(nc, "rank_tabled", 2)
            looked = Tally(nc, "rank_looked", 2, lead=SLOTS)
            counted = Tally(nc, "rank_counted", 2, lead=2)
            picked = Tally(nc, "rank_picked", 2, lead=1)
            row_used = Tally(nc, "rank_row_used", 2, lead=SLOTS)
            ranked = Tally(nc, "rank_ranked", 2, lead=SLOTS)
            integer = Tally(nc, "rank_integer", 2, lead=SLOTS)
            packed = Tally(nc, "rank_packed", 2)
            sent = [Tally(nc, f"rank_sent{u}", 32) for u in range(SLOTS)]
            opened = nc.alloc_semaphore("rank_opened")
            beat = nc.alloc_semaphore("rank_beat")
            with nc.Block() as block:
                @block.sync
                def _(sp):
                    def tile(t, u, turn):
                        sp.wait_ge(row_used.sem, row_used.at(t - SLOTS))
                        for f in KEYS:
                            sp.dma_start(key_row[u][f][:],
                                         k.key_rows[f][bass.ds(t * P, P)].partition_broadcast(P)
                                         ).then_inc(row_in[u].sem, 16)
                    rounds(sp, NT, SLOTS, tile)

                @block.vector
                def _(dve):
                    row_used.open(dve)
                    ranked.open(dve)

                    def make(t, u):
                        dve.wait_ge(looked.sem, looked.at(t - SLOTS))
                        dve.wait_ge(ranked.sem, ranked.at(t - SLOTS))
                        for f in KEYS:
                            dve.tensor_scalar(one_hi[u][f][:], iota_hi[:], k.cols[f + "_hi"][:, bass.ds(t, 1)], None,
                                              ALU.is_equal)
                            dve.tensor_scalar(one_lo[u][f][:], iota_lo[:], k.cols[f + "_lo"][:, bass.ds(t, 1)], None,
                                              ALU.is_equal).then_inc(made.sem, 1)

                    def pick(t, u, turn):
                        dve.wait_ge(row_in[u].sem, row_in[u].at(turn))
                        dve.wait_ge(integer.sem, integer.at(t - SLOTS))
                        for f in KEYS:
                            dve.scalar_tensor_tensor(same[f][:], key_row[u][f][:], k.edge[f][:, bass.ds(t, 1), 0],
                                                     below[:], ALU.is_equal, ALU.mult, accum_out=before[u][f][:]
                                                     ).then_inc(row_used.sem, 1)
                        for n, f in enumerate(KEYS):
                            dve.wait_ge(counted.sem, counted.at(t, n + 1))
                            dve.wait_ge(row_used.sem, row_used.at(t, n + 1))
                            dve.tensor_tensor_reduce(junk[f][:], at_ps[f][:, 0:HI], one_hi[u][f][:], 1.0,
                                                     before[u][f][:], ALU.mult, ALU.add, rank_f[u][f][:]
                                                     ).then_inc(ranked.sem, 1)

                    dve.wait_ge(opened, 1)
                    make(0, 0)
                    make(1, 1)

                    def tile(t, u, turn):
                        make(t + 2, (u + 2) % SLOTS)
                        pick(t, u, turn)
                    rounds(dve, NT - 2, SLOTS, tile)
                    for t in (NT - 2, NT - 1):
                        pick(t, t % SLOTS, t // SLOTS)

                @block.scalar
                def _(act):
                    def records(t, u, turn):
                        if later(turn):
                            act.wait_ge(sent[u].sem, sent[u].at(turn - 1))
                        act.wait_ge(opened, 1)
                        for f in KEYS:
                            act.copy(rec[u][f][:, 0:3], k.edge[f][:, bass.ds(t, 1), :].rearrange("p a w -> p (a w)")
                                     ).then_inc(packed.sem, 1)

                    def copy_turned(t, u):
                        for n, f in enumerate(KEYS):
                            act.wait_ge(looked.sem, looked.at(t - 2, n + 1))
                            act.wait_ge(turned.sem, turned.at(t, n + 1))
                            act.copy(lo_T[u % 2][f][:], turn_bf[f][:, 0:P])
                            act.copy(lo_Tb[u % 2][f][:], turn_bf[f][:, 0:P]).then_inc(copied.sem, 1)

                    def copy_table(t, u):
                        for n, f in enumerate(KEYS):
                            act.wait_ge(counted.sem, counted.at(t - 1, n + 1))
                            act.copy(table[u % 2][f][:], count_ps[f][:, 0:HI]).then_inc(tabled.sem, 1)

                    act.wait_ge(opened, 1)

                    def ends(t, u):
                        for n, f in enumerate(KEYS):
                            act.wait_ge(looked.sem, looked.at(t, n + 1))
                            act.activation(junk_end[f][:], end_ps[f][:, 0:HI], ACT.Relu, bias=minus_lift[:],
                                           accum_out=rec[u][OTHER[f]][:, 3:4]).then_inc(picked.sem, 1)

                    def tile(t, u, turn):
                        records(t, u, turn)
                        copy_turned(t + 1, u + 1)
                        copy_table(t + 1, u + 1)
                        ends(t, u)
                    picked.open(act)
                    copied.open(act)
                    copy_turned(0, 0)
                    copy_table(0, 0)
                    rounds(act, NT - 1, SLOTS, tile, peel=1)
                    records(NT - 1, (NT - 1) % SLOTS, (NT - 1) // SLOTS)
                    ends(NT - 1, (NT - 1) % SLOTS)

                @block.tensor
                def _(pe):
                    for f in KEYS:
                        pe.matmul(count_ps[f][:, 0:HI], k.ident[:], start[f][:], start=True, stop=True
                                  ).then_inc(counted.sem, 2)
                    pe.wait_ge(counted.sem, 4)
                    looked.open(pe)
                    pe.sem_inc(opened, 1)

                    def turn_tile(t, u):
                        for n, f in enumerate(KEYS):
                            pe.wait_ge(copied.sem, copied.at(t - 1, n + 1))
                            pe.wait_ge(made.sem, made.at(t, n + 1))
                            pe.transpose(turn_bf[f][:, 0:P], one_lo[u][f][:], k.ident_bf[:]).then_inc(turned.sem, 1)

                    def look_up(t, u):
                        for n, f in enumerate(KEYS):
                            pe.wait_ge(ranked.sem, ranked.at(t - 1, n + 1))
                            pe.wait_ge(copied.sem, copied.at(t, n + 1))
                            pe.wait_ge(tabled.sem, tabled.at(t, n + 1))
                            pe.matmul(at_ps[f][:, 0:HI], lo_T[u % 2][f][:], table[u % 2][f][:], start=True, stop=True)
                            pe.matmul(count_ps[f][:, 0:HI], one_lo[u][f][:], one_hi[u][f][:], start=False, stop=True,
                                      skip_group_check=True).then_inc(counted.sem, 1)
                            pe.wait_ge(picked.sem, picked.at(t - 1, n + 1))
                            pe.matmul(end_ps[f][:, 0:HI], lo_Tb[u % 2][f][:], end_hi[f][:], start=True, stop=False)
                            pe.matmul(end_ps[f][:, 0:HI], lo_Tb[u % 2][f][:], end_lo[f][:], start=False, stop=False)
                            pe.matmul(end_ps[f][:, 0:HI], lift[:], one_hi[u][f][:], start=False, stop=True
                                      ).then_inc(looked.sem, 1)

                    def tile(t, u, turn):
                        turn_tile(t + 1, (u + 1) % SLOTS)
                        look_up(t, u)
                    turn_tile(0, 0)
                    rounds(pe, NT - 1, SLOTS, tile)
                    look_up(NT - 1, (NT - 1) % SLOTS)

                @block.gpsimd
                def _(pool):
                    integer.open(pool)
                    last = pool.to_reg(EP)

                    def tile(t, u, turn):
                        if later(turn):
                            pool.wait_ge(sent[u].sem, sent[u].at(turn - 1))
                        pool.wait_ge(picked.sem, picked.at(t))
                        pool.wait_ge(ranked.sem, ranked.at(t))
                        pool.sem_inc(beat, 1)
                        for f in KEYS:
                            pool.tensor_copy(rank[u][f][:], rank_f[u][f][:]).then_inc(integer.sem, 1)
                        for n, f in enumerate(KEYS):
                            pool.wait_ge(integer.sem, integer.at(t, n + 1))
                            pool.sem_inc(beat, 1)
                            pool.indirect_dma_start(
                                out=k.records[f], out_offset=bass.IndirectOffsetOnAxis(ap=rank[u][f][:, 0:1], axis=0),
                                in_=rec[u][f][:], in_offset=None, bounds_check=last, oob_is_err=False
                            ).then_inc(sent[u].sem, 16)
                    rounds(pool, NT, SLOTS, tile, peel=1)
                    for u in range(SLOTS):
                        pool.wait_ge(sent[u].sem, sent[u].at(NT // SLOTS - 1))


def position_columns(nc, top, k):
    k.keep = {f: nc.dram_tensor(f"keep_{f}", (EP,), BF16, kind="Internal").ap() for f in ("dst", "src")}
    size = {f: nc.dram_tensor(f"size_{f}", (EP,), F32, kind="Internal").ap() for f in ("dst", "src")}
    k.reset = nc.dram_tensor("reset", (EP,), F32, kind="Internal").ap()
    k.meta = {f: nc.dram_tensor(f"meta_{f}", (P, NCH, META), I32, kind="Internal").ap() for f in ("dst", "src")}
    k.META_AT = {"key": 0, "other": TPC, "other_end": 2 * TPC, "inv": 3 * TPC, "weight": 4 * TPC}
    HALF = EP // 2
    with ExitStack() as ctx:
        meta = {f: ctx.enter_context(nc.sbuf_tensor(f"meta_sb_{f}", [P, NCH, META], I32)) for f in k.keep}

        def field(f, what):
            at = k.META_AT[what]
            return meta[f][:, :, at:at + TPC]

        FIELDS = [(f, w, field(f, n)) for f in k.keep for w, n in ((0, "key"), (1, "other"), (3, "other_end"), (2, "weight"))]
        reset = ctx.enter_context(nc.sbuf_tensor("reset_rows", [KR, 2 * P], F32))
        here = {f: ctx.enter_context(nc.sbuf_tensor(f"here_{f}", [KR, 2 * P, REC], F32)) for f in k.keep}
        prev = {f: ctx.enter_context(nc.sbuf_tensor(f"prev_{f}", [KR, 2 * P, REC], F32)) for f in k.keep}
        keep = {f: ctx.enter_context(nc.sbuf_tensor(f"keep_rows_{f}", [KR, 2 * P], BF16)) for f in k.keep}
        fld = [ctx.enter_context(nc.sbuf_tensor(f"field{n}", [KR, 2 * P], F32)) for n in range(len(FIELDS))]
        line = ctx.enter_context(nc.sbuf_tensor("keep_line", [2, HALF], BF16))
        ones = ctx.enter_context(nc.sbuf_tensor("ones_line", [2, HALF], BF16))
        sizes = ctx.enter_context(nc.sbuf_tensor("size_line", [2, HALF], F32))
        size_rows = {f: ctx.enter_context(nc.sbuf_tensor(f"size_rows_{f}", [KR, 2 * P], F32)) for f in k.keep}
        inv_rows = {f: ctx.enter_context(nc.sbuf_tensor(f"inv_rows_{f}", [KR, 2 * P], F32)) for f in k.keep}
        ps = ctx.enter_context(nc.psum_tensor("fields_T", [P, 2, 4, P], F32))
        carry = ctx.enter_context(nc.sbuf_tensor("size_carry", [2, 1], F32))
        TURN = [(fld[n], out) for n, (_, _, out) in enumerate(FIELDS)] + [(inv_rows[f], field(f, "inv")) for f in k.keep]
        s_reset = nc.alloc_semaphore("pos_reset")
        s_meta = nc.alloc_semaphore("pos_meta")
        s_carry = nc.alloc_semaphore("pos_carry")
        s_in = nc.alloc_semaphore("pos_in")
        s_keep = nc.alloc_semaphore("pos_keep")
        s_keep_out = nc.alloc_semaphore("pos_keep_out")
        s_line = nc.alloc_semaphore("pos_line")
        s_sized = nc.alloc_semaphore("pos_sized")
        s_size_out = nc.alloc_semaphore("pos_size_out")
        s_size_in = nc.alloc_semaphore("pos_size_in")
        s_field = nc.alloc_semaphore("pos_field")
        s_turned = nc.alloc_semaphore("pos_turned")
        s_kept = nc.alloc_semaphore("pos_kept")
        s_node = nc.alloc_semaphore("pos_node")
        with nc.Block() as block:
            @block.sync
            def _(sp):
                for f in k.keep:
                    flat = k.records[f].rearrange("r c -> (r c)")
                    sp.dma_start(here[f][:], flat[REC:REC + EP * REC].rearrange("(r c w) -> r c w", c=2 * P, w=REC)
                                 ).then_inc(s_in, 16)
                    sp.dma_start(prev[f][:], flat[0:EP * REC].rearrange("(r c w) -> r c w", c=2 * P, w=REC)
                                 ).then_inc(s_in, 16)
                for n, f in enumerate(k.keep):
                    sp.wait_ge(s_keep, n + 1)
                    sp.dma_start(k.keep[f].rearrange("(r c) -> r c", c=2 * P), keep[f][:]).then_inc(s_keep_out, 16)
                sp.wait_ge(s_keep_out, 32)
                for h in range(2):
                    if h:
                        sp.wait_ge(s_sized, 1)
                    for n, f in enumerate(k.keep):
                        sp.dma_start(line[n:n + 1, :], k.keep[f][h * HALF:(h + 1) * HALF].rearrange("(r c) -> r c", r=1)
                                     ).then_inc(s_line, 16)
                    sp.wait_ge(s_sized, h + 1)
                    for n, f in enumerate(k.keep):
                        sp.dma_start(size[f][h * HALF:(h + 1) * HALF].rearrange("(r c) -> r c", r=1), sizes[n:n + 1, :]
                                     ).then_inc(s_size_out, 16)
                sp.wait_ge(s_size_out, 16 * 4)
                for f in k.keep:
                    sp.dma_start(size_rows[f][:], size[f].rearrange("(r c) -> r c", c=2 * P)).then_inc(s_size_in, 16)
                sp.wait_ge(s_reset, 1)
                sp.dma_start(k.reset.rearrange("(r c) -> r c", c=2 * P), reset[:]).then_inc(s_meta, 16)
                sp.wait_ge(s_kept, len(TURN))
                for f in k.keep:
                    sp.dma_start(k.meta[f], meta[f][:]).then_inc(s_meta, 16)
                sp.wait_ge(s_meta, 48)

            @block.vector
            def _(dve):
                dve.memset(ones[:], 1.0)
                dve.wait_ge(s_in, 64)
                for f in k.keep:
                    dve.tensor_tensor(keep[f][:], here[f][:, :, 0], prev[f][:, :, 0], ALU.is_equal).then_inc(s_keep, 1)
                dve.wait_ge(s_keep, 1)
                dve.tensor_scalar(reset[:], keep["dst"][:], -1.0, BIG, ALU.add, ALU.mult).then_inc(s_reset, 1)
                for n, (f, w, _) in enumerate(FIELDS):
                    if w in (0, 1):
                        dve.tensor_scalar(fld[n][:], here[f][:, :, w], float(N - 1), None, ALU.min).then_inc(s_field, 1)
                    else:
                        dve.tensor_copy(fld[n][:], here[f][:, :, w]).then_inc(s_field, 1)
                for h in range(2):
                    dve.wait_ge(s_line, 32 * (h + 1))
                    if h:
                        dve.tensor_copy(carry[:], sizes[:, HALF - 1:HALF]).then_inc(s_carry, 1)
                        dve.wait_ge(s_carry, 1)
                        dve.wait_ge(s_size_out, 32)
                    dve.tensor_tensor_scan(sizes[:], line[:], ones[:], carry[:] if h else 0.0,
                                           ALU.mult, ALU.add).then_inc(s_sized, 1)
                dve.wait_ge(s_size_in, 32)
                for f in k.keep:
                    dve.reciprocal(inv_rows[f][:], size_rows[f][:]).then_inc(s_field, 1)
                for n, (_, out) in enumerate(TURN):
                    dve.wait_ge(s_turned, n + 1)
                    is_float = n >= len(FIELDS) or FIELDS[n][1] == 2
                    for c in range(2):
                        to = (out.bitcast(F32) if is_float else out).rearrange("p a (b c) -> p a b c", c=2)[:, :, :, c]
                        ins = dve.tensor_copy(to, ps[:, n % 2, c, 0:KR].rearrange("p (a b) -> p a b", b=TPC // 2))
                    ins.then_inc(s_kept, 1)

            @block.tensor
            def _(pe):
                for n, (rows, _) in enumerate(TURN):
                    pe.wait_ge(s_field, n + 1)
                    if n >= 2:
                        pe.wait_ge(s_kept, n - 1)
                    for c in range(2):
                        ins = pe.transpose(ps[:, n % 2, c, 0:KR], rows[:, c * P:(c + 1) * P], k.ident[0:KR, 0:KR])
                    ins.then_inc(s_turned, 1)


def load_weights(nc, top, k, w):
    def sb(name, shape, dt=F32, ctx=top):
        return ctx.enter_context(nc.sbuf_tensor(name, shape, dt))

    PLAIN = ("Wq", "Wk", "Wv", "Ws", "W1", "W2", "W")
    TURNED = ("W", "W_rel", "W_root")
    COLS, ROWS = ("bq", "bk", "bv"), ("bs", "b1", "b2", "b_rel")
    k.w = {f: sb(f"w_{f}", [P, H, C]) for f in PLAIN}
    k.wT = {f: sb(f"wT_{f}", [P, H, C]) for f in TURNED}
    k.col = {f: sb(f"bias_{f}", [P, H]) for f in COLS}
    k.row = {f: sb(f"row_{f}", [P, C]) for f in ROWS}
    k.row["zero"] = sb("row_zero", [P, C])
    k.slope = sb("slope", [P, 1])
    HEADS2 = w["att"].shape[0]
    CPH = C // HEADS2
    k.w_att = sb("w_att", [P, H, 2, HEADS2])
    s_zero = nc.alloc_semaphore("w_zero")
    s_in = nc.alloc_semaphore("w_in")
    s_turned = nc.alloc_semaphore("w_turned")
    s_kept = nc.alloc_semaphore("w_kept")
    with ExitStack() as ctx:
        raw = {f: sb(f"raw_{f}", [P, H, C], ctx=ctx) for f in TURNED if f not in PLAIN}
        att = sb("att_blocks", [P, H, 2, HEADS2], ctx=ctx)
        ps = ctx.enter_context(nc.psum_tensor("w_ps", [P, 4, H, C], F32))
        with nc.Block() as block:
            @block.sync
            def _(sp):
                n = 0
                for f, t in [(f, k.w[f]) for f in PLAIN] + list(raw.items()):
                    sp.dma_start(t[:], w[f].rearrange("(h p) c -> p h c", p=P)).then_inc(s_in, 16)
                    n += 16
                for f in ROWS:
                    sp.dma_start(k.row[f][:], w[f].partition_broadcast(P)).then_inc(s_in, 16)
                    n += 16
                sp.dma_start(k.slope[:], w["a"].partition_broadcast(P)).then_inc(s_in, 16)
                with nc.allow_non_contiguous_dma(reason="columns of a few words"):
                    for f in COLS:
                        sp.dma_start(k.col[f][:], w[f].rearrange("(h p) -> p h", p=P)).then_inc(s_in, 16)
                        n += 16
                    sp.wait_ge(s_zero, 1)
                    for h in range(HEADS2):
                        lo = h * CPH % P
                        for s in range(2):
                            sp.dma_start(att[lo:lo + CPH, h * CPH // P, s, h:h + 1],
                                         w["att"][h, s * CPH:(s + 1) * CPH].rearrange("(c o) -> c o", o=1)
                                         ).then_inc(s_in, 16)
                            n += 16
                sp.wait_ge(s_in, n + 16)

            ALL_IN = 16 * (len(PLAIN) + len(raw) + len(ROWS) + 1 + len(COLS) + 2 * HEADS2)

            @block.tensor
            def _(pe):
                pe.wait_ge(s_in, ALL_IN)
                for n, f in enumerate(TURNED):
                    t = k.w.get(f, raw.get(f))
                    for a in range(H):
                        for b in range(H):
                            ins = pe.transpose(ps[:, n, a, b * P:(b + 1) * P], t[:, b, a * P:(a + 1) * P], k.ident[:])
                    ins.then_inc(s_turned, 1)
                for a in range(H):
                    for b in range(H):
                        ins = pe.matmul(ps[:, 3, a, 0:2 * HEADS2], k.w["W"][:, b, a * P:(a + 1) * P],
                                        att[:, b, :, :].rearrange("p s h -> p (s h)"), start=(b == 0), stop=(b == H - 1))
                ins.then_inc(s_turned, 1)

            @block.vector
            def _(dve):
                dve.memset(k.row["zero"][:], 0.0)
                dve.memset(att[:], 0.0).then_inc(s_zero, 1)
                dve.wait_ge(s_in, ALL_IN)
                for h in range(H):
                    dve.tensor_tensor(k.w["Ws"][:, h, h * P:(h + 1) * P], k.w["Ws"][:, h, h * P:(h + 1) * P], k.ident[:],
                                      ALU.add)
                for n, f in enumerate(TURNED):
                    dve.wait_ge(s_turned, n + 1)
                    dve.tensor_copy(k.wT[f][:], ps[:, n, :, :])
                dve.wait_ge(s_turned, len(TURNED) + 1)
                dve.tensor_copy(k.w_att[:].rearrange("p h s n -> p h (s n)"), ps[:, 3, :, 0:2 * HEADS2])


def sum_pass(nc, top, k, name, order, table, what, out, matrix=None, weighted=False, scaled=False, bias=None,
             prelu=False):
    SL = 6
    WB = 2
    IDX, INV, WGT = k.META_AT[what], k.META_AT["inv"], k.META_AT["weight"]
    with ExitStack() as ctx:
        def sb(n, shape, dt=F32):
            return [ctx.enter_context(nc.sbuf_tensor(f"{name}_{n}{u}", shape, dt)) for u in range(SL)]

        meta, keep, rows = sb("meta", [P, META], I32), sb("keep", [P, CH], BF16), sb("rows", [P, TPC, C])
        acc, res = sb("acc", [P, H, CH]), sb("res", [P, TPC, C])
        neg = ctx.enter_context(nc.sbuf_tensor(f"{name}_neg", [P, TPC, C], F32))
        turn_ps = [ctx.enter_context(nc.psum_tensor(f"{name}_turn{u}", [P, H, CH], F32)) for u in range(WB)]
        row_ps = [ctx.enter_context(nc.psum_tensor(f"{name}_row{u}", [P, TPC, C], F32)) for u in range(WB)]
        loaded = [Tally(nc, f"{name}_loaded{u}", 32) for u in range(SL)]
        gathered = [Tally(nc, f"{name}_gathered{u}", 16 * TPC) for u in range(SL)]
        weighed = Tally(nc, f"{name}_weighed")
        turned = Tally(nc, f"{name}_turned", H, lead=SL)
        summed = Tally(nc, f"{name}_summed", H, lead=SL)
        mapped = Tally(nc, f"{name}_mapped", 2, lead=SL)
        affine = Tally(nc, f"{name}_affine")
        bent = Tally(nc, f"{name}_bent")
        kept = Tally(nc, f"{name}_kept", 1, lead=SL)
        stored = [Tally(nc, f"{name}_stored{u}", 16) for u in range(SL)]
        zeroed = nc.alloc_semaphore(f"{name}_zeroed")
        beat = nc.alloc_semaphore(f"{name}_beat")
        with nc.Block() as block:
            @block.sync
            def _(sp):
                def chunk(c, u, turn):
                    sp.wait_ge(kept.sem, kept.at(c - SL))
                    sp.dma_start(meta[u][:], k.meta[order][:, bass.ds(c, 1), :].rearrange("p a w -> p (a w)")
                                 ).then_inc(loaded[u].sem, 16)
                    sp.dma_start(keep[u][:], k.keep[order][bass.ds(c * CH, CH)].partition_broadcast(P)
                                 ).then_inc(loaded[u].sem, 16)
                rounds(sp, NCH, SL, chunk)

            @block.gpsimd
            def _(pool):
                last = pool.to_reg(table.shape[0] - 1)

                def chunk(c, u, turn):
                    pool.wait_ge(loaded[u].sem, loaded[u].at(turn))
                    pool.wait_ge(turned.sem, turned.at(c - SL))
                    pool.sem_inc(beat, 1)
                    for t in range(TPC):
                        pool.indirect_dma_start(
                            out=rows[u][:, t, :], out_offset=None, in_=table,
                            in_offset=bass.IndirectOffsetOnAxis(ap=meta[u][:, IDX + t:IDX + t + 1], axis=0),
                            bounds_check=last, oob_is_err=False).then_inc(gathered[u].sem, 16)
                rounds(pool, NCH, SL, chunk)

            @block.tensor
            def _(pe):
                turned.open(pe)
                mapped.open(pe)

                def turn_chunk(c, u, turn):
                    if weighted:
                        pe.wait_ge(weighed.sem, weighed.at(c))
                    else:
                        pe.wait_ge(gathered[u].sem, gathered[u].at(turn))
                    pe.wait_ge(summed.sem, summed.at(c - WB))
                    for h in range(H):
                        for t in range(TPC):
                            ins = pe.transpose(turn_ps[u % WB][:, h, t * P:(t + 1) * P],
                                               rows[u][:, t, h * P:(h + 1) * P], k.ident[:])
                        ins.then_inc(turned.sem, 1)

                def map_chunk(c, u):
                    pe.wait_ge(kept.sem, kept.at(c - WB))
                    pe.wait_ge(summed.sem, summed.at(c))
                    for t in range(TPC):
                        at = slice(t * P, (t + 1) * P)
                        for h in range(H):
                            if matrix is None:
                                ins = pe.transpose(row_ps[u % WB][:, t, h * P:(h + 1) * P], acc[u][:, h, at], k.ident[:])
                            else:
                                ins = pe.matmul(row_ps[u % WB][:, t, :], acc[u][:, h, at], matrix[:, h, :],
                                                start=(h == 0), stop=(h == H - 1))
                        if t % 2:
                            ins.then_inc(mapped.sem, 1)

                def turn_next(c, u, turn):
                    turn_chunk(c + 1, (u + 1) % SL, turn + (u + 1) // SL)
                turn_chunk(0, 0, 0)

                def step(c, u, turn):
                    turn_next(c, u, turn)
                    map_chunk(c, u)
                rounds(pe, NCH - 1, SL, step)
                map_chunk(NCH - 1, (NCH - 1) % SL)

            @block.vector
            def _(dve):
                dve.memset(acc[SL - 1][:], 0.0).then_inc(zeroed, 1)
                summed.open(dve)
                dve.wait_ge(zeroed, 1)
                if bias is not None:
                    kept.open(dve)

                def sum_chunk(c, u, turn):
                    dve.wait_ge(loaded[u].sem, loaded[u].at(turn))
                    dve.wait_ge(mapped.sem, mapped.at(c - SL))
                    dve.wait_ge(summed.sem, summed.at(c - 1))
                    for h in range(H):
                        dve.wait_ge(turned.sem, turned.at(c, h + 1))
                        dve.tensor_tensor_scan(acc[u][:, h, :], keep[u][:], turn_ps[u % WB][:, h, :],
                                               acc[(u - 1) % SL][:, h, CH - 1:CH], ALU.mult, ALU.add
                                               ).then_inc(summed.sem, 1)

                def keep_chunk(c, u, turn):
                    if later(turn):
                        dve.wait_ge(stored[u].sem, stored[u].at(turn - 1))
                    for t in range(TPC):
                        if t % 2 == 0:
                            dve.wait_ge(mapped.sem, mapped.at(c, t // 2 + 1))
                        factor = meta[u][:, INV + t:INV + t + 1].bitcast(F32) if scaled else 1.0
                        ins = dve.scalar_tensor_tensor(res[u][:, t, :], row_ps[u % WB][:, t, :], factor, bias[:],
                                                       ALU.mult, ALU.add)
                    if not prelu:
                        ins.then_inc(kept.sem, 1)
                        return
                    ins.then_inc(affine.sem, 1)
                    dve.wait_ge(affine.sem, affine.at(c))
                    dve.wait_ge(kept.sem, kept.at(c - 1))
                    dve.tensor_scalar(neg[:], res[u][:], 0.0, k.slope[:, 0:1], ALU.min, ALU.mult).then_inc(bent.sem, 1)
                    dve.wait_ge(bent.sem, bent.at(c))
                    dve.scalar_tensor_tensor(res[u][:], res[u][:], 0.0, neg[:], ALU.max, ALU.add).then_inc(kept.sem, 1)

                def step(c, u, turn):
                    sum_chunk(c + 1, (u + 1) % SL, turn + (u + 1) // SL)
                    if bias is not None:
                        keep_chunk(c, u, turn)
                sum_chunk(0, 0, 0)
                rounds(dve, NCH - 1, SL, step, peel=1)
                if bias is not None:
                    keep_chunk(NCH - 1, (NCH - 1) % SL, (NCH - 1) // SL)

            @block.scalar
            def _(act):
                if bias is None:
                    kept.open(act)

                def weigh(c, u, turn):
                    act.wait_ge(gathered[u].sem, gathered[u].at(turn))
                    for t in range(TPC):
                        ins = act.activation(rows[u][:, t, :], rows[u][:, t, :], ACT.Copy,
                                             scale=meta[u][:, WGT + t:WGT + t + 1].bitcast(F32))
                    ins.then_inc(weighed.sem, 1)

                def keep_chunk(c, u, turn):
                    if bias is None:
                        if later(turn):
                            act.wait_ge(stored[u].sem, stored[u].at(turn - 1))
                        for t in range(TPC):
                            if t % 2 == 0:
                                act.wait_ge(mapped.sem, mapped.at(c, t // 2 + 1))
                            ins = act.activation(res[u][:, t, :], row_ps[u % WB][:, t, :], ACT.Copy,
                                                 scale=meta[u][:, INV + t:INV + t + 1].bitcast(F32) if scaled else 1.0)
                        ins.then_inc(kept.sem, 1)
                    act.wait_ge(kept.sem, kept.at(c))
                    act.dma_start(out[bass.ds(c * CH, CH), :].rearrange("(t p) f -> p t f", p=P), res[u][:]
                                  ).then_inc(stored[u].sem, 16)

                if not weighted:
                    rounds(act, NCH, SL, keep_chunk, peel=1)
                else:
                    def step(c, u, turn):
                        weigh(c + 2, (u + 2) % SL, turn + (u + 2) // SL)
                        keep_chunk(c, u, turn)
                    weigh(0, 0, 0)
                    weigh(1, 1, 0)
                    rounds(act, NCH - 2, SL, step, peel=1)
                    for c in (NCH - 2, NCH - 1):
                        keep_chunk(c, c % SL, c // SL)
                for u in range(SL):
                    act.wait_ge(stored[u].sem, stored[u].at((NCH - 1 - u) // SL))


def attention_pass(nc, top, k, name, heads, src_table, src_what, dst_table, out, dot, scale, bias=None):
    SL = 2
    CPH = C // heads
    IDX_S, IDX_D = k.META_AT[src_what], k.META_AT["key"]
    ALPHA = 0.2
    NJ = 3
    with ExitStack() as ctx:
        def sb1(n, shape, dt=F32):
            return ctx.enter_context(nc.sbuf_tensor(f"{name}_{n}", shape, dt))

        def sb(n, shape, dt=F32):
            return [sb1(f"{n}{u}", shape, dt) for u in range(SL)]

        def ps(n, shape):
            return ctx.enter_context(nc.psum_tensor(f"{name}_{n}", shape, F32))

        meta, reset = sb("meta", [P, META], I32), sb("reset", [heads, CH])
        src_rows, dst_rows = sb("src_rows", [P, TPC, C]), sb("dst_rows", [P, TPC, C])
        src_T, dst_T = sb("src_T", [P, H, CH]), sb("dst_T", [P, H, CH])
        query, prod = sb1("query", [P, H, CH]), sb1("prod", [P, H, CH])
        value = sb("value", [P, H, CH])
        top_m = sb("max", [heads, CH + 1])
        shifted = sb1("shifted", [heads, CH])
        score = sb1("score", [heads, 2, CH])
        diff, expo = sb("diff", [heads, 2, CH]), sb("expo", [P, 2, CH])
        den = sb("den", [heads, CH])
        part, acc = sb1("part", [P, H, CH]), sb("acc", [P, H, CH])
        inv = sb("inv", [P, TPC, heads])
        res = sb("res", [P, TPC, C])
        low, up = sb1("low", [P, TPC, C]), sb1("up", [P, TPC, C])
        sel, sel_T, ones = sb1("sel", [P, H, heads]), sb1("sel_T", [P, C]), sb1("ones", [P, C])
        turn_ps = ps("turn", [P, H, CH])
        proj_ps = [ps(f"proj{n}", [P, CH]) for n in range(NJ)]
        score_ps = ps("score_ps", [P, CH])
        back_ps = [ps(f"back{n}", [P, CH]) for n in range(2)]
        T = lambda n, per=1, lead=0: Tally(nc, f"{name}_{n}", per, lead)
        loaded = [T(f"loaded{u}", 32) for u in range(SL)]
        got_src = [T(f"got_src{u}", 16 * TPC) for u in range(SL)]
        got_dst = [T(f"got_dst{u}", 16 * TPC) for u in range(SL)]
        turned = T("turned", 2, lead=SL)
        in_T = T("in_T", 2, lead=SL)
        projected = T("projected", 6 if dot else 2)
        proj_out = T("proj_out", 2 * H if dot else H, lead=SL)
        multiplied = T("multiplied", H, lead=SL)
        scored = T("scored", 1, lead=SL)
        maxed = T("maxed", 2, lead=SL)
        diffed = T("diffed", 2, lead=SL)
        leaky = T("leaky", 2, lead=SL)
        exped = T("exped", 1, lead=SL)
        summed = T("summed", 1, lead=SL)
        spread = T("spread", H, lead=SL)
        parted = T("parted", H, lead=SL)
        ran = T("ran", H, lead=SL)
        den_T = T("den_T", 1, lead=SL)
        inverted = T("inverted", 2, lead=SL)
        back = T("back", 2, lead=SL)
        divided = T("divided", 2, lead=SL)
        kept = T("kept", 1, lead=SL)
        lowered, elu_e = T("lowered", 1, lead=SL), T("elu_e", 1, lead=SL)
        stored = [T(f"stored{u}", 16) for u in range(SL)]
        setup = [nc.alloc_semaphore(f"{name}_setup{n}") for n in range(4)]
        beat = nc.alloc_semaphore(f"{name}_beat")
        pe_beat = nc.alloc_semaphore(f"{name}_pe_beat")
        with nc.Block() as block:
            @block.gpsimd
            def _(pool):
                pool.wait_ge(setup[0], 1)
                pool.affine_select(out=sel[:], in_=ones[:, 0:H * heads].rearrange("p (a b) -> p a b", a=H),
                                   compare_op=ALU.is_ge, fill=0.0, base=0, pattern=[[P, H], [-CPH, heads]],
                                   channel_multiplier=1).then_inc(setup[1], 1)
                pool.affine_select(out=sel_T[:], in_=ones[:], compare_op=ALU.is_ge, fill=0.0, base=0,
                                   pattern=[[1, C]], channel_multiplier=-CPH).then_inc(setup[1], 1)
                pool.wait_ge(setup[1], 2)
                pool.affine_select(out=sel[:], in_=sel[:], compare_op=ALU.is_ge, fill=0.0, base=CPH - 1,
                                   pattern=[[-P, H], [CPH, heads]], channel_multiplier=-1).then_inc(setup[2], 1)
                pool.affine_select(out=sel_T[:], in_=sel_T[:], compare_op=ALU.is_ge, fill=0.0, base=CPH - 1,
                                   pattern=[[-1, C]], channel_multiplier=CPH).then_inc(setup[2], 1)
                last_s = pool.to_reg(src_table.shape[0] - 1)
                last_d = pool.to_reg(dst_table.shape[0] - 1)

                def chunk(c, u, turn):
                    pool.wait_ge(loaded[u].sem, loaded[u].at(turn))
                    pool.wait_ge(turned.sem, turned.at(c - SL))
                    pool.sem_inc(beat, 1)
                    for rows, table, idx, last, got in ((src_rows, src_table, IDX_S, last_s, got_src),
                                                        (dst_rows, dst_table, IDX_D, last_d, got_dst)):
                        for t in range(TPC):
                            pool.indirect_dma_start(
                                out=rows[u][:, t, :], out_offset=None, in_=table,
                                in_offset=bass.IndirectOffsetOnAxis(ap=meta[u][:, idx + t:idx + t + 1], axis=0),
                                bounds_check=last, oob_is_err=False).then_inc(got[u].sem, 16)
                rounds(pool, NCH, SL, chunk)

            @block.sync
            def _(sp):
                def chunk(c, u, turn):
                    sp.wait_ge(turned.sem, turned.at(c - SL))
                    sp.wait_ge(maxed.sem, maxed.at(c - SL))
                    sp.dma_start(meta[u][:], k.meta["dst"][:, bass.ds(c, 1), :].rearrange("p a w -> p (a w)")
                                 ).then_inc(loaded[u].sem, 16)
                    sp.dma_start(reset[u][:], k.reset[bass.ds(c * CH, CH)].partition_broadcast(heads)
                                 ).then_inc(loaded[u].sem, 16)
                rounds(sp, NCH, SL, chunk)

            @block.tensor
            def _(pe):
                for t in (turned, scored, spread, den_T, back):
                    t.open(pe)
                pe.wait_ge(setup[2], 2)

                def project(c, n, weight, half, rhs):
                    for h in range(H):
                        ins = pe.matmul(proj_ps[n % NJ][:], weight[:, h, half * P:(half + 1) * P], rhs[:, h, :],
                                        start=(h == 0), stop=(h == H - 1))
                    ins.then_inc(projected.sem, 1)

                def turn_rows(c, u, turn, n):
                    rows, got = ((src_rows, got_src), (dst_rows, got_dst))[n]
                    pe.wait_ge(got[u].sem, got[u].at(turn))
                    pe.wait_ge(in_T.sem, in_T.at(c - 1 + n, 2 if n == 0 else 1))
                    for h in range(H):
                        for t in range(TPC):
                            ins = pe.transpose(turn_ps[:, h, t * P:(t + 1) * P], rows[u][:, t, h * P:(h + 1) * P],
                                               k.ident[:])
                    ins.then_inc(turned.sem, 1)

                den_ps = proj_ps[0] if dot else proj_ps[2]

                def front_queries_keys(c, u):
                    pe.wait_ge(in_T.sem, in_T.at(c))
                    pe.wait_ge(proj_out.sem, proj_out.at(c - 1))
                    pe.wait_ge(multiplied.sem, multiplied.at(c - 1))
                    pe.wait_ge(inverted.sem, inverted.at(c - 1, 1))
                    project(c, 0, k.w["Wq"], 0, dst_T[u])
                    project(c, 1, k.w["Wk"], 0, src_T[u])
                    project(c, 2, k.w["Wq"], 1, dst_T[u])
                    pe.wait_ge(proj_out.sem, proj_out.at(c, 1))
                    project(c, 3, k.w["Wk"], 1, src_T[u])

                def front_values(c, u, half):
                    if half == 0:
                        pe.wait_ge(multiplied.sem, multiplied.at(c, 1))
                    else:
                        pe.wait_ge(proj_out.sem, proj_out.at(c, 2))
                    project(c, 4 + half, k.w["Wv"], half, src_T[u])

                def front_scores(c, u):
                    pe.wait_ge(diffed.sem, diffed.at(c - 1))
                    if dot:
                        pe.wait_ge(maxed.sem, maxed.at(c - 1, 1))
                        pe.wait_ge(multiplied.sem, multiplied.at(c))
                        for h in range(H):
                            ins = pe.matmul(score_ps[0:heads, :], sel[:, h, :], prod[:, h, :], start=(h == 0), stop=(h == H - 1))
                    else:
                        pe.wait_ge(leaky.sem, leaky.at(c - 1))
                        pe.wait_ge(in_T.sem, in_T.at(c))
                        for n, rhs in enumerate((src_T[u], dst_T[u])):
                            for h in range(H):
                                ins = pe.matmul(score_ps[0:heads, :], k.w_att[:, h, n, :], rhs[:, h, :],
                                                start=(n == 0 and h == 0), stop=(n == 1 and h == H - 1))
                    ins.then_inc(scored.sem, 1)

                def front_end(c, u, rear_step):
                    if dot:
                        front_queries_keys(c, u)
                        rear_step()
                        front_scores(c, u)
                        front_values(c, u, 0)
                        front_values(c, u, 1)
                    else:
                        front_scores(c, u)
                        rear_step()
                        pe.wait_ge(proj_out.sem, proj_out.at(c - 1))
                        project(c, 0, k.wT["W"], 0, src_T[u])
                        project(c, 1, k.wT["W"], 1, src_T[u])

                def spread_half(c, u, h):
                    at = slice(h * P, (h + 1) * P)
                    if h == 0:
                        pe.wait_ge(exped.sem, exped.at(c))
                        pe.wait_ge(divided.sem, divided.at(c - 1))
                    else:
                        pe.wait_ge(parted.sem, parted.at(c, h))
                        pe.wait_ge(ran.sem, ran.at(c, h))
                    pe.matmul(back_ps[0][:], sel_T[:, at], expo[u][:, 1, :], start=True, stop=True)
                    pe.matmul(back_ps[1][:], sel_T[:, at], expo[u][:, 0, :], start=True, stop=True).then_inc(spread.sem, 1)

                def turn_denominators(c, u):
                    pe.wait_ge(summed.sem, summed.at(c))
                    if dot:
                        pe.wait_ge(multiplied.sem, multiplied.at(c))
                    pe.wait_ge(inverted.sem, inverted.at(c - 1, 1))
                    pe.sem_inc(pe_beat, 1)
                    for t in range(TPC):
                        ins = pe.transpose(den_ps[:, t * heads:(t + 1) * heads], den[u][:, t * P:(t + 1) * P],
                                           k.ident[0:heads, 0:heads])
                    ins.then_inc(den_T.sem, 1)

                def turn_back(c, u):
                    pe.wait_ge(parted.sem, parted.at(c))
                    pe.wait_ge(ran.sem, ran.at(c))
                    for t in range(TPC):
                        for h in range(H):
                            ins = pe.transpose(back_ps[t // 2][:, (t % 2) * C + h * P:(t % 2) * C + (h + 1) * P],
                                               acc[u][:, h, t * P:(t + 1) * P], k.ident[:])
                        if t % 2:
                            ins.then_inc(back.sem, 1)

                turn_rows(0, 0, 0, 0)
                turn_rows(0, 0, 0, 1)
                front_end(0, 0, lambda: None)

                def step(c, u, turn):
                    nxt, nxt_turn = (u + 1) % SL, turn + (u + 1) // SL
                    turn_rows(c + 1, nxt, nxt_turn, 0)
                    spread_half(c, u, 0)
                    turn_rows(c + 1, nxt, nxt_turn, 1)
                    turn_denominators(c, u)
                    spread_half(c, u, 1)
                    front_end(c + 1, nxt, lambda: turn_back(c, u))
                rounds(pe, NCH - 1, SL, step)
                c, u = NCH - 1, (NCH - 1) % SL
                spread_half(c, u, 0)
                turn_denominators(c, u)
                spread_half(c, u, 1)
                turn_back(c, u)

            @block.scalar
            def _(act):
                for t in (in_T, proj_out, exped, elu_e, lowered):
                    t.open(act)

                def copy_turned(c, u, n):
                    act.wait_ge(turned.sem, turned.at(c, n + 1))
                    if n == 0:
                        act.wait_ge(scored.sem, scored.at(c - SL))
                        act.wait_ge(projected.sem, projected.at(c - 1))
                    act.copy((src_T, dst_T)[n][u][:], turn_ps[:]).then_inc(in_T.sem, 1)

                def copy_queries(c):
                    if dot:
                        act.wait_ge(multiplied.sem, multiplied.at(c - 1))
                        for h in range(H):
                            act.wait_ge(projected.sem, projected.at(c, 2 * h + 1))
                            act.activation(query[:, h, :], proj_ps[2 * h % NJ][:], ACT.Identity, bias=k.col["bq"][:, h:h + 1]
                                           ).then_inc(proj_out.sem, 1)

                def copy_values(c, u, h):
                    act.wait_ge(parted.sem, parted.at(c - SL))
                    act.wait_ge(projected.sem, projected.at(c, (5 if dot else 1) + h))
                    if dot:
                        act.activation(value[u][:, h, :], proj_ps[(4 + h) % NJ][:], ACT.Identity,
                                       bias=k.col["bv"][:, h:h + 1]).then_inc(proj_out.sem, 1)
                    else:
                        act.copy(value[u][:, h, :], proj_ps[h][:]).then_inc(proj_out.sem, 1)

                def exponentials(c, u):
                    act.wait_ge(diffed.sem, diffed.at(c))
                    act.wait_ge(summed.sem, summed.at(c - SL))
                    act.wait_ge(spread.sem, spread.at(c - SL))
                    act.activation(expo[u][0:heads], diff[u][:], ACT.Exp, scale=scale).then_inc(exped.sem, 1)

                def elu_parts(c, u):
                    act.wait_ge(divided.sem, divided.at(c))
                    act.wait_ge(kept.sem, kept.at(c - 1))
                    act.activation(low[:], res[u][:], ACT.Relu, scale=-1.0).then_inc(lowered.sem, 1)
                    act.activation(up[:], res[u][:], ACT.Relu)
                    act.wait_ge(lowered.sem, lowered.at(c))
                    act.activation(low[:], low[:], ACT.Exp, scale=-1.0).then_inc(elu_e.sem, 1)

                def store(c, u):
                    act.wait_ge(kept.sem, kept.at(c))
                    act.dma_start(out[bass.ds(c * CH, CH), :].rearrange("(t p) f -> p t f", p=P), res[u][:]
                                  ).then_inc(stored[u].sem, 16)

                def front(c, u, rear_elu=None, rear_store=None):
                    copy_turned(c, u, 0)
                    if rear_elu:
                        rear_elu()
                    copy_turned(c, u, 1)
                    copy_queries(c)
                    copy_values(c, u, 0)
                    exponentials(c, u)
                    copy_values(c, u, 1)
                    if rear_store:
                        rear_store()

                front(0, 0)
                if dot:
                    def step(c, u, turn):
                        front(c + 1, (u + 1) % SL, None, lambda: store(c, u))
                    rounds(act, NCH - 1, SL, step)
                    store(NCH - 1, (NCH - 1) % SL)
                else:
                    front(1, 1)

                    def step(c, u, turn):
                        def rear():
                            if not isinstance(c, int) or c:
                                store(c - 1, (u - 1) % SL)
                            elu_parts(c, u)
                        front(c + 2, u, rear)
                    rounds(act, NCH - 2, SL, step, peel=1)
                    for c in (NCH - 2, NCH - 1):
                        store(c - 1, (c - 1) % SL)
                        elu_parts(c, c % SL)
                    store(NCH - 1, (NCH - 1) % SL)
                for u in range(SL):
                    act.wait_ge(stored[u].sem, stored[u].at((NCH - 1 - u) // SL))

            @block.vector
            def _(dve):
                dve.memset(ones[:], 1.0).then_inc(setup[0], 1)
                for e in expo:
                    dve.memset(e[:], 0.0)
                for t in (multiplied, maxed, diffed, leaky, summed, parted, ran, inverted, divided, kept):
                    t.open(dve)
                dve.memset(top_m[SL - 1][:], -BIG)
                dve.memset(den[SL - 1][:], 0.0)
                dve.memset(acc[SL - 1][:], 0.0).then_inc(setup[3], 1)
                dve.wait_ge(setup[3], 1)

                def multiply(c, h):
                    if h == 0:
                        dve.wait_ge(scored.sem, scored.at(c - 1))
                    dve.wait_ge(proj_out.sem, proj_out.at(c, h + 1))
                    dve.wait_ge(projected.sem, projected.at(c, 2 * h + 2))
                    dve.scalar_tensor_tensor(prod[:, h, :], proj_ps[(2 * h + 1) % NJ][:], k.col["bk"][:, h:h + 1],
                                             query[:, h, :], ALU.add, ALU.mult).then_inc(multiplied.sem, 1)

                def exponents(c, u, turn):
                    before = (u - 1) % SL
                    dve.wait_ge(scored.sem, scored.at(c))
                    dve.wait_ge(diffed.sem, diffed.at(c - 1))
                    if dot:
                        scores = score_ps[0:heads, :]
                    else:
                        dve.tensor_scalar(score[:, 0, :], score_ps[0:heads, :], ALPHA, None, ALU.mult).then_inc(leaky.sem, 1)
                        dve.wait_ge(leaky.sem, leaky.at(c, 1))
                        dve.tensor_tensor(score[:, 1, :], score[:, 0, :], score_ps[0:heads, :], ALU.max).then_inc(leaky.sem, 1)
                        dve.wait_ge(leaky.sem, leaky.at(c))
                        scores = score[:, 1, :]
                    dve.wait_ge(loaded[u].sem, loaded[u].at(turn))
                    dve.wait_ge(maxed.sem, maxed.at(c - 1))
                    dve.tensor_copy(top_m[u][:, 0:1], top_m[before][:, CH:CH + 1])
                    dve.tensor_tensor_scan(top_m[u][:, 1:CH + 1], reset[u][:], scores, top_m[before][:, CH:CH + 1],
                                           ALU.add, ALU.max).then_inc(maxed.sem, 1)
                    dve.wait_ge(maxed.sem, maxed.at(c, 1))
                    dve.tensor_tensor(shifted[:], top_m[u][:, 0:CH], reset[u][:], ALU.add).then_inc(maxed.sem, 1)
                    dve.wait_ge(exped.sem, exped.at(c - SL))
                    dve.tensor_tensor(diff[u][:, 1, :], scores, top_m[u][:, 1:CH + 1], ALU.subtract).then_inc(diffed.sem, 1)
                    dve.wait_ge(maxed.sem, maxed.at(c))
                    dve.tensor_tensor(diff[u][:, 0, :], shifted[:], top_m[u][:, 1:CH + 1], ALU.subtract
                                      ).then_inc(diffed.sem, 1)

                def denominators(c, u):
                    before = (u - 1) % SL
                    dve.wait_ge(exped.sem, exped.at(c))
                    dve.wait_ge(den_T.sem, den_T.at(c - SL))
                    dve.wait_ge(summed.sem, summed.at(c - 1))
                    dve.tensor_tensor_scan(den[u][:], expo[u][0:heads, 0, :], expo[u][0:heads, 1, :],
                                           den[before][:, CH - 1:CH], ALU.mult, ALU.add).then_inc(summed.sem, 1)

                def invert(c, u):
                    dve.wait_ge(den_T.sem, den_T.at(c))
                    den_ps = (proj_ps[0] if dot else proj_ps[2])[:, 0:TPC * heads].rearrange("p (t n) -> p t n", n=heads)
                    dve.wait_ge(divided.sem, divided.at(c - SL))
                    dve.tensor_scalar(inv[u][:], den_ps, 0.0 if dot else 1e-16, None, ALU.add).then_inc(inverted.sem, 1)
                    dve.wait_ge(inverted.sem, inverted.at(c, 1))
                    dve.reciprocal(inv[u][:], inv[u][:]).then_inc(inverted.sem, 1)

                def numerators(c, u, h):
                    before = (u - 1) % SL
                    if h == 0:
                        dve.wait_ge(proj_out.sem, proj_out.at(c))
                        dve.wait_ge(back.sem, back.at(c - SL))
                        dve.wait_ge(ran.sem, ran.at(c - 1))
                    dve.wait_ge(spread.sem, spread.at(c, h + 1))
                    dve.tensor_tensor(part[:, h, :], back_ps[0][:], value[u][:, h, :], ALU.mult).then_inc(parted.sem, 1)
                    dve.wait_ge(parted.sem, parted.at(c, h + 1))
                    dve.tensor_tensor_scan(acc[u][:, h, :], back_ps[1][:], part[:, h, :], acc[before][:, h, CH - 1:CH],
                                           ALU.mult, ALU.add).then_inc(ran.sem, 1)

                def divide(c, u, turn):
                    dve.wait_ge(inverted.sem, inverted.at(c))
                    if later(turn):
                        dve.wait_ge(stored[u].sem, stored[u].at(turn - 1))
                    for n in range(2):
                        dve.wait_ge(back.sem, back.at(c, n + 1))
                        for t in range(2):
                            ins = dve.tensor_tensor(
                                res[u][:, 2 * n + t, :].rearrange("p (n c) -> p n c", n=heads),
                                back_ps[n][:, t * C:(t + 1) * C].rearrange("p (n c) -> p n c", n=heads),
                                inv[u][:, 2 * n + t, :].unsqueeze(2).to_broadcast([P, heads, CPH]), ALU.mult)
                        ins.then_inc(divided.sem, 1)

                def finish(c, u):
                    if dot:
                        dve.wait_ge(divided.sem, divided.at(c))
                        dve.tensor_tensor(res[u][:], res[u][:], bias[:].unsqueeze(1).to_broadcast([P, TPC, C]), ALU.add
                                          ).then_inc(kept.sem, 1)
                    else:
                        dve.wait_ge(elu_e.sem, elu_e.at(c))
                        dve.scalar_tensor_tensor(res[u][:], low[:], -1.0, up[:], ALU.add, ALU.add).then_inc(kept.sem, 1)

                if dot:
                    multiply(0, 0)
                    multiply(0, 1)
                exponents(0, 0, 0)

                def step(c, u, turn):
                    nxt, nxt_turn = (u + 1) % SL, turn + (u + 1) // SL
                    denominators(c, u)
                    numerators(c, u, 0)
                    invert(c, u)
                    numerators(c, u, 1)
                    if dot:
                        multiply(c + 1, 0)
                        multiply(c + 1, 1)
                        divide(c, u, turn)
                        exponents(c + 1, nxt, nxt_turn)
                        finish(c, u)
                    else:
                        exponents(c + 1, nxt, nxt_turn)
                        divide(c, u, turn)
                        if not isinstance(c, int) or c:
                            finish(c - 1, (u - 1) % SL)
                rounds(dve, NCH - 1, SL, step, peel=1)
                c, u, turn = NCH - 1, (NCH - 1) % SL, (NCH - 1) // SL
                denominators(c, u)
                numerators(c, u, 0)
                invert(c, u)
                numerators(c, u, 1)
                if not dot:
                    finish(c - 1, (u - 1) % SL)
                divide(c, u, turn)
                finish(c, u)


def groups(engine, unroll, body, peel=0):
    rounds(engine, NG, unroll, lambda g, u, turn: body(g, u, turn, P, G), peel)
    body(NG, NG % unroll, NG // unroll, TAIL, 1)


def pipeline(engine, unroll, *step):
    ahead = max(offset for offset, _ in step)

    def plain(g):
        for offset, work in step:
            at = g + offset
            if 0 <= at <= NG:
                work(at, at % unroll, at // unroll, *((P, G) if at < NG else (TAIL, 1)))
    turns = (NG - ahead) // unroll
    for g in range(-ahead, unroll):
        plain(g)
    with engine.Fori(1, turns) as i:
        for u in range(unroll):
            for offset, work in step:
                work(i * unroll + (u + offset), (u + offset) % unroll, i + (u + offset) // unroll, P, G)
    for g in range(turns * unroll, NG + 2):
        plain(g)


def node_rows(table, g, parts, tiles):
    return table[bass.ds(g * (P * G), parts * tiles), :].rearrange("(p j) f -> p j f", j=tiles)


def node_pass(nc, top, k, name, kind, table, ends, sums, default, out, matrix=None, stat_rows=None):
    SL = 4
    AHEAD = SL - 1
    use_mm = matrix is not None
    norm = kind != "root"
    hyper = kind == "hyper"
    PAIRS = G // 2
    with ExitStack() as ctx:
        def sb1(n, shape, dt=F32):
            return ctx.enter_context(nc.sbuf_tensor(f"{name}_{n}", shape, dt))

        def sb(n, shape, dt=F32, slots=SL):
            return [sb1(f"{n}{u}", shape, dt) for u in range(slots)]

        x, g_in, idx = sb("x", [P, G, C]), sb("g", [P, G, C]), sb("idx", [P, G], I32)
        res = sb("res", [P, G, C])
        x_T = sb("x_T", [P, PAIRS, 2, C], slots=2)
        half = sb("half", [P, G, C], slots=2)
        stats, mean_var = sb1("stats", [P, G, 6]), sb("mean_var", [P, G, 2])
        std, rstd, shift = sb("std", [P, G]), sb("rstd", [P, G]), sb("shift", [P, G])
        part, one_col, zero_col = sb("part", [P, 2, C], slots=2), sb1("one_col", [P, 1]), sb1("zero_col", [P, 1])
        neg_slope = sb1("neg_slope", [P, 1])
        turn_ps = [ctx.enter_context(nc.psum_tensor(f"{name}_turn{n}", [P, 2, C], F32)) for n in range(PAIRS)]
        y_ps = [ctx.enter_context(nc.psum_tensor(f"{name}_y{n}", [P, 2, C], F32)) for n in range(PAIRS)]
        stat_ps = ctx.enter_context(nc.psum_tensor(f"{name}_stat", [P, 2 * C], F32))
        T = lambda n, per=1, lead=0: Tally(nc, f"{name}_{n}", per, lead)
        loaded = [T(f"loaded{u}", 32) for u in range(SL)]
        gathered = [T(f"gathered{u}", 16 * G) for u in range(SL)]
        filled = T("filled", 1)
        turned = T("turned", PAIRS, lead=SL)
        in_T = T("in_T", PAIRS, lead=SL)
        mapped = T("mapped", PAIRS, lead=SL)
        added = T("added", PAIRS, lead=SL)
        bent = T("bent", 1, lead=SL)
        split = T("split", 1)
        ready = T("ready", 1, lead=SL)
        stat_ok = T("stat_ok", 1)
        aggregated = T("aggregated", 1)
        rooted = T("rooted", 1)
        inverted = T("inverted", 2)
        kept = T("kept", 1)
        squared = T("squared", 1)
        reduced = T("reduced", 2, lead=SL)
        totalled = T("totalled", 1, lead=SL)
        total = T("total", 1)
        stored = [T(f"stored{u}", 16) for u in range(SL)]
        s_set = nc.alloc_semaphore(f"{name}_set")
        beat = nc.alloc_semaphore(f"{name}_beat")
        dve_beat = nc.alloc_semaphore(f"{name}_dve_beat")

        def npairs(tiles):
            return -(-tiles // 2)

        def all_added(tiles):
            return npairs(tiles) if use_mm else PAIRS

        def pair_tiles(n, tiles):
            return range(2 * n, min(2 * n + 2, tiles))

        def rows_used(g):
            return (ready.sem, ready.at(g)) if hyper else (added.sem, added.at(g))

        def fill(g, u, turn, parts, tiles, engine):
            engine.wait_ge(*rows_used(g - SL))
            src = default[0:parts].unsqueeze(1).to_broadcast([parts, tiles, C])
            copy = engine.copy if hyper else engine.tensor_copy
            copy(g_in[u][0:parts, 0:tiles, :], src).then_inc(filled.sem, 1)

        with nc.Block() as block:
            @block.sync
            def _(sp):
                def group(g, u, turn, parts, tiles):
                    sp.wait_ge(*rows_used(g - SL))
                    sp.dma_start(x[u][0:parts, 0:tiles, :], node_rows(table, g, parts, tiles)).then_inc(loaded[u].sem, 16)
                    sp.dma_start(idx[u][0:parts, 0:tiles],
                                 ends[bass.ds(g * (P * G), parts * tiles)].rearrange("(p j) -> p j", j=tiles)
                                 ).then_inc(loaded[u].sem, 16)
                groups(sp, SL, group)

            @block.gpsimd
            def _(pool):
                last = pool.to_reg(EP - 1)

                def group(g, u, turn, parts, tiles):
                    pool.wait_ge(loaded[u].sem, loaded[u].at(turn))
                    pool.wait_ge(filled.sem, filled.at(g))
                    pool.sem_inc(beat, 1)
                    for j in range(tiles):
                        pool.indirect_dma_start(
                            out=g_in[u][0:parts, j, :], out_offset=None, in_=sums,
                            in_offset=bass.IndirectOffsetOnAxis(ap=idx[u][0:parts, j:j + 1], axis=0),
                            bounds_check=last, oob_is_err=False).then_inc(gathered[u].sem, 16)
                groups(pool, SL, group)

            @block.tensor
            def _(pe):
                turned.open(pe)
                mapped.open(pe)
                totalled.open(pe)
                pe.wait_ge(s_set, 1)
                if not norm:
                    pe.matmul(stat_ps[0:1, :], zero_col[:], part[0][:].rearrange("p s f -> p (s f)"), start=True, stop=False)

                def turn_group(g, u, turn, parts, tiles):
                    pe.wait_ge(loaded[u].sem, loaded[u].at(turn))
                    for n in range(npairs(tiles)):
                        pe.wait_ge(in_T.sem, in_T.at(g - 1, n + 1))
                        for j in pair_tiles(n, tiles):
                            for h in range(H):
                                ins = pe.transpose(turn_ps[n][:, j % 2, h * P:h * P + parts],
                                                   x[u][0:parts, j, h * P:(h + 1) * P], k.ident[0:parts, 0:parts])
                        ins.then_inc(turned.sem, 1)

                def map_group(g, u, turn, parts, tiles):
                    for n in range(npairs(tiles)):
                        pe.wait_ge(added.sem, added.at(g - 1, n + 1))
                        pe.wait_ge(in_T.sem, in_T.at(g, n + 1))
                        for j in pair_tiles(n, tiles):
                            for h in range(H):
                                ins = pe.matmul(y_ps[n][0:parts, j % 2, :], x_T[u % 2][:, n, j % 2, h * P:h * P + parts],
                                                matrix[:, h, :], start=(h == 0), stop=(h == H - 1))
                        ins.then_inc(mapped.sem, 1)

                def total_group(g, u, turn, parts, tiles):
                    pe.wait_ge(reduced.sem, reduced.at(g))
                    pe.matmul(stat_ps[0:1, :], one_col[0:parts, :], part[u % 2][0:parts].rearrange("p s f -> p (s f)"),
                              start=False, stop=False).then_inc(totalled.sem, 1)

                if use_mm:
                    if norm:
                        pipeline(pe, SL, (1, turn_group), (0, map_group))
                    else:
                        pipeline(pe, SL, (1, turn_group), (0, map_group), (-1, total_group))
                if not norm:
                    pe.matmul(stat_ps[0:1, :], zero_col[:], part[0][:].rearrange("p s f -> p (s f)"), start=False, stop=True
                              ).then_inc(total.sem, 1)

            @block.scalar
            def _(act):
                in_T.open(act)

                def copy_turned(g, u, turn, parts, tiles):
                    for n in range(npairs(tiles)):
                        act.wait_ge(mapped.sem, mapped.at(g - 2, n + 1))
                        act.wait_ge(turned.sem, turned.at(g, n + 1))
                        w = len(pair_tiles(n, tiles))
                        if parts == P:
                            act.copy(x_T[u % 2][:, n, 0:w, :], turn_ps[n][:, 0:w, :]).then_inc(in_T.sem, 1)
                        else:
                            for h in range(H):
                                ins = act.copy(x_T[u % 2][:, n, 0, h * P:h * P + parts],
                                               turn_ps[n][:, 0, h * P:h * P + parts])
                            ins.then_inc(in_T.sem, 1)

                def negative_part(g, u, turn, parts, tiles):
                    at = (slice(0, parts), slice(0, tiles))
                    act.wait_ge(added.sem, added.at(g))
                    act.wait_ge(ready.sem, ready.at(g - 2))
                    act.activation(half[u % 2][at], res[u][at], ACT.Relu, scale=-1.0).then_inc(split.sem, 1)

                def square(g, u, turn, parts, tiles):
                    at = (slice(0, parts), slice(0, tiles))
                    act.wait_ge(added.sem, added.at(g, all_added(tiles)))
                    act.wait_ge(reduced.sem, reduced.at(g - 2))
                    act.activation(half[u % 2][at], res[u][at], ACT.Square).then_inc(squared.sem, 1)
                    store(g, u, parts, tiles)

                def root(g, u, turn, parts, tiles):
                    act.wait_ge(aggregated.sem, aggregated.at(g))
                    act.activation(std[u][0:parts, 0:tiles], mean_var[u][0:parts, 0:tiles, 1], ACT.Sqrt,
                                   bias=k.eps[0:parts, :]).then_inc(rooted.sem, 1)

                def norm_rows(g, u, turn, parts, tiles):
                    act.wait_ge(inverted.sem, inverted.at(g))
                    for j in range(tiles):
                        ins = act.activation(res[u][0:parts, j, :], res[u][0:parts, j, :], ACT.Identity,
                                             bias=shift[u][0:parts, j:j + 1], scale=rstd[u][0:parts, j:j + 1])
                    ins.then_inc(kept.sem, 1)
                    act.wait_ge(kept.sem, kept.at(g))
                    store(g, u, parts, tiles)

                def store(g, u, parts, tiles):
                    act.dma_start(node_rows(out, g, parts, tiles), res[u][0:parts, 0:tiles, :]).then_inc(stored[u].sem, 16)

                if kind == "attention":
                    pipeline(act, SL, (1, copy_turned), (-1, norm_rows), (0, root))
                elif kind == "hyper":
                    pipeline(act, SL, (AHEAD, partial(fill, engine=act)), (1, negative_part), (-1, norm_rows), (0, root))
                elif kind == "plain":
                    pipeline(act, SL, (-1, norm_rows), (0, root))
                else:
                    pipeline(act, SL, (1, copy_turned), (0, square))
                for u in range(SL):
                    act.wait_ge(stored[u].sem, stored[u].at((NG - u) // SL))

            @block.vector
            def _(dve):
                for t in (ready, added, bent, reduced):
                    t.open(dve)
                dve.memset(part[0][:], 0.0)
                dve.memset(zero_col[:], 0.0)
                dve.tensor_scalar(neg_slope[:], k.slope[:], -1.0, None, ALU.mult)
                dve.memset(one_col[:], 1.0).then_inc(s_set, 1)
                dve.wait_ge(s_set, 1)

                def add(g, u, turn, parts, tiles):
                    at = (slice(0, parts), slice(0, tiles))
                    dve.wait_ge(gathered[u].sem, gathered[u].at(turn) if tiles == G else gathered[u].at(turn, 16 * tiles))
                    if later(turn):
                        dve.wait_ge(stored[u].sem, stored[u].at(turn - 1))
                    if use_mm:
                        for n in range(npairs(tiles)):
                            w = len(pair_tiles(n, tiles))
                            dve.wait_ge(mapped.sem, mapped.at(g, n + 1))
                            dve.tensor_tensor(res[u][0:parts, 2 * n:2 * n + w, :], y_ps[n][0:parts, 0:w, :],
                                              g_in[u][0:parts, 2 * n:2 * n + w, :], ALU.add).then_inc(added.sem, 1)
                    else:
                        dve.wait_ge(loaded[u].sem, loaded[u].at(turn))
                        dve.tensor_tensor(res[u][at], g_in[u][at], x[u][at], ALU.add).then_inc(added.sem, PAIRS)

                def bend(g, u, turn, parts, tiles):
                    at = (slice(0, parts), slice(0, tiles))
                    dve.wait_ge(added.sem, added.at(g))
                    dve.scalar_tensor_tensor(g_in[u][at], res[u][at], 0.0, x[u][at], ALU.max, ALU.add).then_inc(bent.sem, 1)

                def join(g, u, turn, parts, tiles):
                    at = (slice(0, parts), slice(0, tiles))
                    dve.wait_ge(split.sem, split.at(g))
                    dve.wait_ge(bent.sem, bent.at(g))
                    dve.scalar_tensor_tensor(res[u][at], half[u % 2][at], neg_slope[0:parts, 0:1], g_in[u][at],
                                             ALU.mult, ALU.add).then_inc(ready.sem, 1)

                def statistics(g, u, turn, parts, tiles):
                    if hyper:
                        dve.wait_ge(ready.sem, ready.at(g))
                    else:
                        dve.wait_ge(added.sem, added.at(g, all_added(tiles)))
                    for j in range(tiles):
                        ins = dve.bn_stats(stats[0:parts, j, :], res[u][0:parts, j, :])
                    ins.then_inc(stat_ok.sem, 1)

                def reciprocals(g, u, turn, parts, tiles):
                    at = (slice(0, parts), slice(0, tiles))
                    dve.wait_ge(rooted.sem, rooted.at(g))
                    dve.reciprocal(rstd[u][at], std[u][at]).then_inc(inverted.sem, 1)

                def aggregate(g, u, turn, parts, tiles):
                    dve.wait_ge(stat_ok.sem, stat_ok.at(g))
                    dve.sem_inc(dve_beat, 1)
                    for j in range(tiles):
                        ins = dve.bn_aggr(mean_var[u][0:parts, j, :], stats[0:parts, j, :])
                    ins.then_inc(aggregated.sem, 1)

                def shifts(g, u, turn, parts, tiles):
                    at = (slice(0, parts), slice(0, tiles))
                    dve.wait_ge(inverted.sem, inverted.at(g, 1))
                    dve.scalar_tensor_tensor(shift[u][at], mean_var[u][0:parts, 0:tiles, 0], -1.0, rstd[u][at],
                                             ALU.mult, ALU.mult).then_inc(inverted.sem, 1)

                def add_up_rows(g, u, turn, parts, tiles):
                    at = (slice(0, parts), slice(0, tiles))
                    dve.wait_ge(added.sem, added.at(g, all_added(tiles)))
                    dve.wait_ge(totalled.sem, totalled.at(g - 2))
                    dve.tensor_reduce(part[u % 2][0:parts, 0, :], res[u][at].rearrange("p j f -> p f j"),
                                      mybir.AxisListType.X, ALU.add)

                def add_up_squares(g, u, turn, parts, tiles):
                    at = (slice(0, parts), slice(0, tiles))
                    dve.wait_ge(squared.sem, squared.at(g))
                    dve.tensor_reduce(part[u % 2][0:parts, 1, :], half[u % 2][at].rearrange("p j f -> p f j"),
                                      mybir.AxisListType.X, ALU.add).then_inc(reduced.sem, 2)

                if hyper:
                    pipeline(dve, SL, (1, add), (0, join), (1, bend), (0, statistics), (-1, reciprocals), (0, aggregate),
                             (-1, shifts))
                elif norm:
                    pipeline(dve, SL, (-1, reciprocals), (AHEAD, partial(fill, engine=dve)), (-1, shifts), (0, add),
                             (0, statistics), (0, aggregate))
                else:
                    pipeline(dve, SL, (AHEAD, partial(fill, engine=dve)), (-1, add_up_squares), (0, add), (0, add_up_rows))
                if not norm:
                    dve.wait_ge(total.sem, 1)
                    dve.tensor_copy(stat_rows[:], stat_ps[0:1, :].rearrange("p (s f) -> p s f", s=2))


def final_pass(nc, top, k, table, rooted_rows, stat_rows, gamma, beta, out):
    SL = 4
    name = "final"
    with ExitStack() as ctx:
        def sb1(n, shape, dt=F32):
            return ctx.enter_context(nc.sbuf_tensor(f"{name}_{n}", shape, dt))

        def sb(n, shape, dt=F32):
            return [sb1(f"{n}{u}", shape, dt) for u in range(SL)]

        x, y, res = sb("x", [P, G, C]), sb("y", [P, G, C]), sb("res", [P, G, C])
        stats, mean_var = sb1("stats", [P, G, 6]), sb("mean_var", [P, G, 2])
        std, rstd, shift = sb("std", [P, G]), sb("rstd", [P, G]), sb("shift", [P, G])
        gb = sb1("gamma_beta", [1, 2, C])
        mom = sb1("moments", [1, 2, C])
        sq, bn_var, bn_std, bn_inv, fac, mf = (sb1(n, [1, C]) for n in ("mean_sq", "bn_var", "bn_std", "bn_inv", "fac", "mf"))
        coef = sb1("coef", [1, 2, C])
        coefs = sb1("coefs", [P, 2, C])
        ones_row = sb1("ones_row", [1, P])
        ps = ctx.enter_context(nc.psum_tensor(f"{name}_ps", [P, 2, C], F32))
        T = lambda n, per=1, lead=0: Tally(nc, f"{name}_{n}", per, lead)
        s_in, s_prep, s_root, s_ps = (nc.alloc_semaphore(f"{name}_{n}") for n in ("in", "prep", "root", "ps"))
        s_co = nc.alloc_semaphore(f"{name}_co")
        dve_beat = nc.alloc_semaphore(f"{name}_dve_beat")
        loaded = [T(f"loaded{u}", 32) for u in range(SL)]
        scaled, shifted = T("scaled"), T("shifted")
        once, twice = T("once", lead=0), T("twice", lead=SL)
        stat_ok, aggregated, rooted = T("stat_ok"), T("aggregated"), T("rooted")
        inverted, kept = T("inverted", 2), T("kept")
        stored = [T(f"stored{u}", 16) for u in range(SL)]
        with nc.Block() as block:
            @block.sync
            def _(sp):
                sp.dma_start(gb[:, 0, :], gamma.rearrange("(o f) -> o f", o=1)).then_inc(s_in, 16)
                sp.dma_start(gb[:, 1, :], beta.rearrange("(o f) -> o f", o=1)).then_inc(s_in, 16)

                def group(g, u, turn, parts, tiles):
                    sp.wait_ge(twice.sem, twice.at(g - SL))
                    for t, to in ((table, x), (rooted_rows, y)):
                        sp.dma_start(to[u][0:parts, 0:tiles, :], node_rows(t, g, parts, tiles)).then_inc(loaded[u].sem, 16)
                groups(sp, SL, group)

            @block.tensor
            def _(pe):
                pe.wait_ge(s_prep, 8)
                pe.matmul(ps[:].rearrange("p s f -> p (s f)"), ones_row[:], coef[:].rearrange("p s f -> p (s f)"),
                          start=True, stop=True).then_inc(s_ps, 1)

            @block.gpsimd
            def _(pool):
                pool.wait_ge(s_co, 1)

                def scale(g, u, turn, parts, tiles):
                    at = (slice(0, parts), slice(0, tiles))
                    pool.wait_ge(loaded[u].sem, loaded[u].at(turn))
                    pool.tensor_tensor(y[u][at], y[u][at], coefs[0:parts, 0, :].unsqueeze(1).to_broadcast([parts, tiles, C]),
                                       ALU.mult).then_inc(scaled.sem, 1)

                def shift_rows(g, u, turn, parts, tiles):
                    at = (slice(0, parts), slice(0, tiles))
                    pool.wait_ge(scaled.sem, scaled.at(g))
                    pool.tensor_tensor(y[u][at], y[u][at], coefs[0:parts, 1, :].unsqueeze(1).to_broadcast([parts, tiles, C]),
                                       ALU.add).then_inc(shifted.sem, 1)
                pipeline(pool, SL, (1, scale), (0, shift_rows))

            @block.vector
            def _(dve):
                twice.open(dve)
                dve.memset(ones_row[:], 1.0)
                dve.tensor_scalar(mom[:], stat_rows[:], 1.0 / N, None, ALU.mult).then_inc(s_prep, 1)
                dve.wait_ge(s_prep, 1)
                dve.tensor_tensor(sq[:], mom[:, 0, :], mom[:, 0, :], ALU.mult).then_inc(s_prep, 1)
                dve.wait_ge(s_prep, 2)
                dve.tensor_tensor(bn_var[:], mom[:, 1, :], sq[:], ALU.subtract).then_inc(s_prep, 1)
                dve.wait_ge(s_root, 1)
                dve.reciprocal(bn_inv[:], bn_std[:]).then_inc(s_prep, 1)
                dve.wait_ge(s_prep, 4)
                dve.wait_ge(s_in, 32)
                dve.tensor_tensor(coef[:, 0, :], bn_inv[:], gb[:, 0, :], ALU.mult).then_inc(s_prep, 1)
                dve.wait_ge(s_prep, 5)
                dve.tensor_tensor(mf[:], mom[:, 0, :], coef[:, 0, :], ALU.mult).then_inc(s_prep, 1)
                dve.wait_ge(s_prep, 6)
                dve.tensor_tensor(coef[:, 1, :], gb[:, 1, :], mf[:], ALU.subtract).then_inc(s_prep, 2)
                dve.wait_ge(s_ps, 1)
                dve.tensor_copy(coefs[:], ps[:]).then_inc(s_co, 1)

                def relu_add(g, u, turn, parts, tiles):
                    at = (slice(0, parts), slice(0, tiles))
                    dve.wait_ge(shifted.sem, shifted.at(g))
                    if later(turn):
                        dve.wait_ge(stored[u].sem, stored[u].at(turn - 1))
                    dve.scalar_tensor_tensor(res[u][at], y[u][at], 0.0, x[u][at], ALU.max, ALU.add).then_inc(once.sem, 1)

                def relu_add_again(g, u, turn, parts, tiles):
                    at = (slice(0, parts), slice(0, tiles))
                    dve.wait_ge(once.sem, once.at(g))
                    dve.scalar_tensor_tensor(res[u][at], res[u][at], 0.0, x[u][at], ALU.max, ALU.add).then_inc(twice.sem, 1)

                def statistics(g, u, turn, parts, tiles):
                    dve.wait_ge(twice.sem, twice.at(g))
                    for j in range(tiles):
                        ins = dve.bn_stats(stats[0:parts, j, :], res[u][0:parts, j, :])
                    ins.then_inc(stat_ok.sem, 1)

                def reciprocals(g, u, turn, parts, tiles):
                    at = (slice(0, parts), slice(0, tiles))
                    dve.wait_ge(rooted.sem, rooted.at(g))
                    dve.reciprocal(rstd[u][at], std[u][at]).then_inc(inverted.sem, 1)

                def aggregate(g, u, turn, parts, tiles):
                    dve.wait_ge(stat_ok.sem, stat_ok.at(g))
                    dve.sem_inc(dve_beat, 1)
                    for j in range(tiles):
                        ins = dve.bn_aggr(mean_var[u][0:parts, j, :], stats[0:parts, j, :])
                    ins.then_inc(aggregated.sem, 1)

                def shifts(g, u, turn, parts, tiles):
                    at = (slice(0, parts), slice(0, tiles))
                    dve.wait_ge(inverted.sem, inverted.at(g, 1))
                    dve.scalar_tensor_tensor(shift[u][at], mean_var[u][0:parts, 0:tiles, 0], -1.0, rstd[u][at],
                                             ALU.mult, ALU.mult).then_inc(inverted.sem, 1)

                pipeline(dve, SL, (-1, reciprocals), (-1, shifts), (0, relu_add), (0, relu_add_again), (0, statistics),
                         (0, aggregate))

            @block.scalar
            def _(act):
                act.wait_ge(s_prep, 3)
                act.activation(bn_std[:], bn_var[:], ACT.Sqrt, bias=k.eps[0:1, :]).then_inc(s_root, 1)

                def root(g, u, turn, parts, tiles):
                    act.wait_ge(aggregated.sem, aggregated.at(g))
                    act.activation(std[u][0:parts, 0:tiles], mean_var[u][0:parts, 0:tiles, 1], ACT.Sqrt,
                                   bias=k.eps[0:parts, :]).then_inc(rooted.sem, 1)

                def norm(g, u, turn, parts, tiles):
                    act.wait_ge(inverted.sem, inverted.at(g))
                    for j in range(tiles):
                        ins = act.activation(res[u][0:parts, j, :], res[u][0:parts, j, :], ACT.Identity,
                                             bias=shift[u][0:parts, j:j + 1], scale=rstd[u][0:parts, j:j + 1])
                    ins.then_inc(kept.sem, 1)
                    act.wait_ge(kept.sem, kept.at(g))
                    act.dma_start(node_rows(out, g, parts, tiles), res[u][0:parts, 0:tiles, :]).then_inc(stored[u].sem, 16)
                pipeline(act, SL, (-1, norm), (0, root))
                for u in range(SL):
                    act.wait_ge(stored[u].sem, stored[u].at((NG - u) // SL))


def graph_layers(nc, x, src, dst, edge_weight, w, out):
    class Kept:
        pass

    k = Kept()
    nodes = [nc.dram_tensor(f"nodes{n}", (N, C), F32, kind="Internal").ap() for n in (1, 2, 3)]
    rooted = nc.dram_tensor("rooted", (N, C), F32, kind="Internal").ap()
    sums = [nc.dram_tensor(f"sums{n}", (EP, C), F32, kind="Internal").ap() for n in range(7)]
    with ExitStack() as top:
        with stage(nc):
            constants(nc, top, k)
        with ExitStack() as sorting:
            with stage(nc):
                key_columns(nc, top, sorting, k, src, dst, edge_weight)
            with stage(nc):
                sort_edges(nc, top, k)
        with stage(nc):
            position_columns(nc, top, k)
        with stage(nc):
            load_weights(nc, top, k, w)
        end = k.node_end
        with stage(nc):
            attention_pass(nc, top, k, "att0", 8, x, "other", x, sums[0], True, 32 ** -0.5, bias=k.row["bs"])
        with stage(nc):
            node_pass(nc, top, k, "node0", "attention", x, end["dst"], sums[0], k.row["bs"], nodes[0], matrix=k.w["Ws"])
        with stage(nc):
            sum_pass(nc, top, k, "hyp1", "dst", nodes[0], "other", sums[1], matrix=k.w["W1"], scaled=True)
        with stage(nc):
            sum_pass(nc, top, k, "hyp2", "src", sums[1], "other_end", sums[2], scaled=True, bias=k.row["b1"], prelu=True)
        with stage(nc):
            sum_pass(nc, top, k, "hyp3", "dst", sums[2], "other_end", sums[3], matrix=k.w["W2"], scaled=True)
        with stage(nc):
            sum_pass(nc, top, k, "hyp4", "src", sums[3], "other_end", sums[4], scaled=True, bias=k.row["b2"])
        with stage(nc):
            node_pass(nc, top, k, "node1", "hyper", nodes[0], end["src"], sums[4], k.row["b2"], nodes[1])
        with stage(nc):
            attention_pass(nc, top, k, "att2", 4, nodes[1], "other", nodes[1], sums[5], False, 1.0)
        with stage(nc):
            node_pass(nc, top, k, "node2", "plain", nodes[1], end["dst"], sums[5], k.row["zero"], nodes[2])
        with stage(nc):
            sum_pass(nc, top, k, "rel3", "dst", nodes[2], "other", sums[6], matrix=k.wT["W_rel"], weighted=True,
                     bias=k.row["b_rel"])
        with ExitStack() as last:
            stat_rows = last.enter_context(nc.sbuf_tensor("stat_rows", [1, 2, C], F32))
            with stage(nc):
                node_pass(nc, top, k, "node3", "root", nodes[2], end["dst"], sums[6], k.row["b_rel"], rooted,
                          matrix=k.wT["W_root"], stat_rows=stat_rows)
            with stage(nc):
                final_pass(nc, top, k, nodes[2], rooted, stat_rows, w["gamma"], w["beta"], out)


_INS = ["x", "src", "dst", "edge_weight", "L0_gnn_Wq", "L0_gnn_bq", "L0_gnn_Wk", "L0_gnn_bk", "L0_gnn_Wv", "L0_gnn_bv",
        "L0_gnn_Ws", "L0_gnn_bs", "L1_gnn_W1", "L1_gnn_b1", "L1_gnn_W2", "L1_gnn_b2", "L1_gnn_a", "L2_gnn_W",
        "L2_gnn_att", "L3_gnn_W_rel", "L3_gnn_b_rel", "L3_gnn_W_root", "L3_gnn_gamma", "L3_gnn_beta"]


def kernel(**inputs):
    import numpy as _np
    import concourse.bacc as _bacc
    from concourse import mybir as _mybir
    from concourse.bass_utils import run_bass_kernel_spmd as _run

    nc = _bacc.Bacc("TRN2", target_bir_lowering=False, num_devices=1)
    arrays, args = {}, {}
    for name in _INS:
        a = _np.ascontiguousarray(inputs[name])
        arrays[f"in_{name}_dram"] = a
        args[name] = nc.dram_tensor(f"in_{name}_dram", a.shape, _mybir.dt.from_np(a.dtype), kind="ExternalInput").ap()
    out = nc.dram_tensor("out_0_dram", (N, C), F32, kind="ExternalOutput").ap()
    weights = {n.split("_gnn_")[1]: a for n, a in args.items() if "_gnn_" in n}
    graph_layers(nc, args["x"], args["src"], args["dst"], args["edge_weight"], weights, out)
    r = _run(nc, [arrays], core_ids=[0])
    return r.results[0]["out_0_dram"]
```
